# Optimizing a Trainium2 kernel written in Bass

```python
import numpy as np
import jax
import jax.numpy as jnp

def _softmax(x, axis=-1):
    return jax.nn.softmax(x, axis=axis)

def _gelu(x):
    return jax.nn.gelu(x, approximate=True)

def _silu(x):
    return jax.nn.silu(x)

def _sigmoid(x):
    return jax.nn.sigmoid(x)

def _layernorm(x, axis=-1, eps=1e-05):
    m = jnp.mean(x, axis=axis, keepdims=True)
    v = jnp.var(x, axis=axis, keepdims=True)
    return (x - m) / jnp.sqrt(v + eps)

def _scatter_add(tgt, idx, src, axis=0):
    return tgt.at[idx].add(src)

def _segment_sum(src, seg, n):
    return jax.ops.segment_sum(src, seg, n)
kernel_name = 'mk_decoder_postln_d2_seqx_r4_288578'

def setup_inputs(seed: int=0):
    np.random.seed(seed)
    _w = jnp.asarray

    def _rec_inputs():
        import jax
        import jax.numpy as jnp
        _rk = jax.random.key(seed)
        x = -0.0002928 + 1 * jax.random.normal(jax.random.fold_in(_rk, 1), (16, 256, 256), jnp.float32)
        _lenS = 256 - jax.random.randint(jax.random.fold_in(_rk, 7), (16,), 0, max(1, 256 // 4) + 1, jnp.int32)
        _lenS2 = 256 - jax.random.randint(jax.random.fold_in(_rk, 8), (16,), 0, max(1, 256 // 4) + 1, jnp.int32)
        _ctx_1024P = jax.random.normal(jax.random.fold_in(_rk, 11), (16, 16, 256), jnp.float32)
        _ctx_1024c = jax.random.dirichlet(jax.random.fold_in(_rk, 511), 0.3 * jnp.ones((16,), jnp.float32), (16, 256))
        _ctx_1024t = jnp.einsum('bsk,bkd->bsd', _ctx_1024c, _ctx_1024P)
        _ctx_1024t = _ctx_1024t * jax.lax.rsqrt(jnp.mean(jnp.square(_ctx_1024t)) + 1e-12) * 0.953939
        ctx_1024 = -1.39393e-06 + 0.999914 * (_ctx_1024t + 0.3 * jax.random.normal(jax.random.fold_in(_rk, 611), (16, 256, 256), jnp.float32))
        _validS = jnp.arange(256)[None, :] < _lenS[:, None]
        _validS2 = jnp.arange(256)[None, :] < _lenS2[:, None]
        _causal = jnp.tril(jnp.ones((256, 256), dtype=bool))
        mask_Bx16xSxS2_ff0 = jnp.where(jnp.ones((16, 16, 256, 256), dtype=bool), 0.0, -1000000000.0).astype(jnp.float32)
        return (x, ctx_1024, mask_Bx16xSxS2_ff0)
    x, ctx_1024, mask_Bx16xSxS2_ff0 = _rec_inputs()

    def _L0_attn_setup():
        import jax, jax.numpy as jnp
        import numpy as np
        H = 16
        D_MODEL = 256
        D_HEAD = 64
        SLOT = 32
        K_DIM = SLOT // 2
        N_KEYS = 64
        TOP_K = 8
        NUM_SLOTS = 2 * H
        TOTAL = 3 * H
        SLEN, BSZ = (512, 4)
        EPS = 1e-05

        def _ln(x, g, b, eps=1e-05):
            m = x.mean(-1, keepdims=True)
            v = ((x - m) ** 2).mean(-1, keepdims=True)
            return (x - m) / jnp.sqrt(v + eps) * g + b
        key = jax.random.key(seed)
        ks = jax.random.split(key, 8)

        def u(k, shape, fan_in):
            b = 1.0 / np.sqrt(fan_in)
            return jax.random.uniform(k, shape, minval=-b, maxval=b, dtype=jnp.float32)
        return {'h': jax.random.normal(ks[0], (SLEN, BSZ, D_MODEL), jnp.float32), 'Wq': u(ks[1], (TOTAL * K_DIM, D_MODEL), D_MODEL), 'bq': jnp.zeros((TOTAL * K_DIM,), jnp.float32), 'gq': jnp.ones((K_DIM,), jnp.float32), 'bq_ln': jnp.zeros((K_DIM,), jnp.float32), 'keys': u(ks[2], (NUM_SLOTS, N_KEYS, K_DIM), K_DIM), 'values': jax.random.normal(ks[3], (NUM_SLOTS, N_KEYS, SLOT), jnp.float32) / np.sqrt(SLOT), 'Wres': u(ks[4], (SLOT, K_DIM), K_DIM), 'bres': jnp.zeros((SLOT,), jnp.float32), 'Wmem': u(ks[5], (D_HEAD, SLOT), SLOT), 'bmem': jnp.zeros((D_HEAD,), jnp.float32), 'Wo': u(ks[6], (D_MODEL, H * D_HEAD), H * D_HEAD), 'g_out': jnp.ones((D_MODEL,), jnp.float32), 'b_out': jnp.zeros((D_MODEL,), jnp.float32)}
    _L0_attn_all = _L0_attn_setup()
    _L0_attn_in = {k: v for k, v in _L0_attn_all.items() if k in ('Wq', 'bq', 'gq', 'bq_ln', 'keys', 'values', 'Wres', 'bres', 'Wmem', 'bmem', 'Wo', 'g_out', 'b_out')}
    del _L0_attn_all

    def _L0_xattn_setup():
        import jax, jax.numpy as jnp
        import numpy as np
        B, S, D, H = (2, 512, 256, 16)
        key = jax.random.key(seed)
        kq, kk, kv, kw = jax.random.split(key, 4)
        Q = jax.random.normal(kq, (B, S, D), dtype=jnp.float32)
        K = jax.random.normal(kk, (B, S, D), dtype=jnp.float32)
        V = jax.random.normal(kv, (B, S, D), dtype=jnp.float32)
        Wo = jax.random.normal(kw, (D, D), dtype=jnp.float32) * (1.0 / np.sqrt(D))
        return {'Q': Q, 'K': K, 'V': V, 'Wo': Wo, 'num_heads': H}
    _L0_xattn_all = _L0_xattn_setup()
    _L0_xattn_in = {k: v for k, v in _L0_xattn_all.items() if k in ('Wo',)}
    del _L0_xattn_all

    def _L0_ffn_setup():
        import jax, jax.numpy as jnp
        import numpy as np
        E = 8
        TOPK = 2
        SCALE = 2.0
        key = jax.random.key(seed)
        ks = jax.random.split(key, 12)
        B, S, D, F, R = (2, 128, 256, 1024, 16)
        w = lambda k, shp: jax.random.normal(k, shp, dtype=jnp.float32) * 0.02
        return {'hidden_states': jax.random.normal(ks[0], (B, S, D), dtype=jnp.float32), 'gate_w': w(ks[1], (E, D)), 'w_gate': w(ks[2], (F, D)), 'w_up': w(ks[3], (F, D)), 'w_down': w(ks[4], (D, F)), 'A1': w(ks[5], (E, R, D)), 'B1': w(ks[6], (E, F, R)), 'A3': w(ks[7], (E, R, D)), 'B3': w(ks[8], (E, F, R)), 'A2': w(ks[9], (E, R, F)), 'B2': w(ks[10], (E, D, R))}
    _L0_ffn_all = _L0_ffn_setup()
    _L0_ffn_in = {k: v for k, v in _L0_ffn_all.items() if k in ('gate_w', 'w_gate', 'w_up', 'w_down', 'A1', 'B1', 'A3', 'B3', 'A2', 'B2')}
    del _L0_ffn_all

    def _L1_attn_setup():
        import jax, jax.numpy as jnp
        import numpy as np
        NUM_BUCKETS = 63

        def _rp_bucket(N):
            rel = jnp.arange(N)[None, :] - jnp.arange(N)[:, None]
            half = NUM_BUCKETS // 2
            return (jnp.clip(rel, -half, half) + half).astype(jnp.int32)
        key = jax.random.key(seed)
        ks = jax.random.split(key, 7)
        B, N, C, H = (4, 256, 256, 16)
        hd = C // H
        g = lambda k, shp, sc: jax.random.normal(k, shp, jnp.float32) * sc
        return {'x': g(ks[0], (B, N, C), 1.0), 'w_qkv': g(ks[1], (3 * C, C), C ** (-0.5)), 'w_proj': g(ks[2], (C, C), C ** (-0.5)), 'b_proj': jnp.zeros((C,), jnp.float32), 'rpe_q_table': g(ks[3], (H, hd, NUM_BUCKETS), 0.02), 'rpe_k_table': g(ks[4], (H, hd, NUM_BUCKETS), 0.02), 'rpe_v_table': g(ks[5], (H, NUM_BUCKETS, hd), 0.02)}
    _L1_attn_all = _L1_attn_setup()
    _L1_attn_in = {k: v for k, v in _L1_attn_all.items() if k in ('w_qkv', 'w_proj', 'b_proj', 'rpe_q_table', 'rpe_k_table', 'rpe_v_table')}
    del _L1_attn_all

    def _L1_xattn_setup():
        import jax, jax.numpy as jnp
        import numpy as np
        B, S, D = (2, 512, 256)
        H = 16
        DH = D // H
        LAMBDA_INIT = 0.8
        EPS = 1e-05
        SCALE = 1.0 / np.sqrt(DH)
        key = jax.random.key(seed)
        ks = jax.random.split(key, 13)
        inp = {'query': jax.random.normal(ks[0], (B, S, D), jnp.float32), 'key': jax.random.normal(ks[1], (B, S, D), jnp.float32), 'value': jax.random.normal(ks[2], (B, S, D), jnp.float32), 'attn_mask': jnp.zeros((B, H, S, S), jnp.float32), 'W_q': jax.random.normal(ks[3], (D, 2 * DH * H), jnp.float32) * 0.02, 'W_k': jax.random.normal(ks[4], (D, 2 * DH * H), jnp.float32) * 0.02, 'W_v': jax.random.normal(ks[5], (D, DH * H), jnp.float32) * 0.02, 'W_o': jax.random.normal(ks[6], (DH * H, D), jnp.float32) * 0.02, 'lambda_q1': jax.random.normal(ks[7], (H, DH), jnp.float32) * 0.1, 'lambda_k1': jax.random.normal(ks[8], (H, DH), jnp.float32) * 0.1, 'lambda_q2': jax.random.normal(ks[9], (H, DH), jnp.float32) * 0.1, 'lambda_k2': jax.random.normal(ks[10], (H, DH), jnp.float32) * 0.1, 'rms_scale': jnp.ones((DH,), jnp.float32)}
        return inp
    _L1_xattn_all = _L1_xattn_setup()
    _L1_xattn_in = {k: v for k, v in _L1_xattn_all.items() if k in ('W_q', 'W_k', 'W_v', 'W_o', 'lambda_q1', 'lambda_k1', 'lambda_q2', 'lambda_k2', 'rms_scale')}
    del _L1_xattn_all

    def _L1_ffn_setup():
        import jax, jax.numpy as jnp
        import numpy as np
        import math
        D = 256
        H = 16
        E = 8
        TOPK = 2
        LAT = D // 2
        KPH = LAT // H
        HD = D // H

        def _forward(hs, q_w, q_b, k_w, k_b, v_w, v_b, o_w, o_b, router_w, router_b, w1, b1, w2, b2):
            B, S, _ = hs.shape
            Q = (hs @ q_w + q_b).reshape(B, S, H, HD).transpose(0, 2, 1, 3)
            K = (hs @ k_w + k_b).reshape(B, S, H, KPH).transpose(0, 2, 1, 3)
            V = (hs @ v_w + v_b).reshape(B, S, H, KPH).transpose(0, 2, 1, 3)
            scores = jnp.einsum('bhsk,bhtk->bhst', Q[..., :KPH], K) / math.sqrt(KPH)
            attn = jax.nn.softmax(scores, axis=-1)
            ao = jnp.einsum('bhst,bhtv->bhsv', attn, V)
            ao = ao.transpose(0, 2, 1, 3).reshape(B, S, H * KPH)
            ao = jnp.concatenate([ao, jnp.zeros((B, S, D - LAT), ao.dtype)], axis=-1)
            mla_out = ao @ o_w + o_b
            probs = jax.nn.softmax(mla_out @ router_w + router_b, axis=-1)
            topw, topi = jax.lax.top_k(probs, TOPK)
            topw = topw / (topw.sum(-1, keepdims=True) + 1e-08)
            combine = jnp.sum(jax.nn.one_hot(topi, E, dtype=probs.dtype) * topw[..., None], axis=-2)
            h1 = jnp.einsum('bsd,edf->ebsf', mla_out, w1) + b1[:, None, None, :]
            h1 = jax.nn.gelu(h1, approximate=False)
            h2 = jnp.einsum('ebsf,efd->ebsd', h1, w2) + b2[:, None, None, :]
            moe_out = jnp.einsum('bse,ebsd->bsd', combine, h2)
            return hs + 0.3 * moe_out
        key = jax.random.key(seed)
        ks = jax.random.split(key, 16)
        s = 0.02
        inp = {'hidden_states': jax.random.normal(ks[0], (2, 512, D), jnp.float32), 'q_w': jax.random.normal(ks[1], (D, D), jnp.float32) * s, 'q_b': jnp.zeros((D,), jnp.float32), 'k_w': jax.random.normal(ks[2], (D, LAT), jnp.float32) * s, 'k_b': jnp.zeros((LAT,), jnp.float32), 'v_w': jax.random.normal(ks[3], (D, LAT), jnp.float32) * s, 'v_b': jnp.zeros((LAT,), jnp.float32), 'o_w': jax.random.normal(ks[4], (D, D), jnp.float32) * s, 'o_b': jnp.zeros((D,), jnp.float32), 'router_w': jax.random.normal(ks[5], (D, E), jnp.float32) * s, 'router_b': jnp.zeros((E,), jnp.float32), 'w1': jax.random.normal(ks[6], (E, D, 2 * D), jnp.float32) * s, 'b1': jnp.zeros((E, 2 * D), jnp.float32), 'w2': jax.random.normal(ks[7], (E, 2 * D, D), jnp.float32) * s, 'b2': jnp.zeros((E, D), jnp.float32)}
        return inp
    _L1_ffn_all = _L1_ffn_setup()
    _L1_ffn_in = {k: v for k, v in _L1_ffn_all.items() if k in ('q_w', 'q_b', 'k_w', 'k_b', 'v_w', 'v_b', 'o_w', 'o_b', 'router_w', 'router_b', 'w1', 'b1', 'w2', 'b2')}
    del _L1_ffn_all
    return {'x': x, 'ctx_1024': ctx_1024, 'mask_Bx16xSxS2_ff0': mask_Bx16xSxS2_ff0, 'L0_attn_Wq': _L0_attn_in['Wq'], 'L0_attn_bq': _L0_attn_in['bq'], 'L0_attn_gq': _L0_attn_in['gq'], 'L0_attn_bq_ln': _L0_attn_in['bq_ln'], 'L0_attn_keys': _L0_attn_in['keys'], 'L0_attn_values': _L0_attn_in['values'], 'L0_attn_Wres': _L0_attn_in['Wres'], 'L0_attn_bres': _L0_attn_in['bres'], 'L0_attn_Wmem': _L0_attn_in['Wmem'], 'L0_attn_bmem': _L0_attn_in['bmem'], 'L0_attn_Wo': _L0_attn_in['Wo'], 'L0_attn_g_out': _L0_attn_in['g_out'], 'L0_attn_b_out': _L0_attn_in['b_out'], 'L0_xattn_Wo': _L0_xattn_in['Wo'], 'L0_ffn_gate_w': _L0_ffn_in['gate_w'], 'L0_ffn_w_gate': _L0_ffn_in['w_gate'], 'L0_ffn_w_up': _L0_ffn_in['w_up'], 'L0_ffn_w_down': _L0_ffn_in['w_down'], 'L0_ffn_A1': _L0_ffn_in['A1'], 'L0_ffn_B1': _L0_ffn_in['B1'], 'L0_ffn_A3': _L0_ffn_in['A3'], 'L0_ffn_B3': _L0_ffn_in['B3'], 'L0_ffn_A2': _L0_ffn_in['A2'], 'L0_ffn_B2': _L0_ffn_in['B2'], 'L1_attn_w_qkv': _L1_attn_in['w_qkv'], 'L1_attn_w_proj': _L1_attn_in['w_proj'], 'L1_attn_b_proj': _L1_attn_in['b_proj'], 'L1_attn_rpe_q_table': _L1_attn_in['rpe_q_table'], 'L1_attn_rpe_k_table': _L1_attn_in['rpe_k_table'], 'L1_attn_rpe_v_table': _L1_attn_in['rpe_v_table'], 'L1_xattn_W_q': _L1_xattn_in['W_q'], 'L1_xattn_W_k': _L1_xattn_in['W_k'], 'L1_xattn_W_v': _L1_xattn_in['W_v'], 'L1_xattn_W_o': _L1_xattn_in['W_o'], 'L1_xattn_lambda_q1': _L1_xattn_in['lambda_q1'], 'L1_xattn_lambda_k1': _L1_xattn_in['lambda_k1'], 'L1_xattn_lambda_q2': _L1_xattn_in['lambda_q2'], 'L1_xattn_lambda_k2': _L1_xattn_in['lambda_k2'], 'L1_xattn_rms_scale': _L1_xattn_in['rms_scale'], 'L1_ffn_q_w': _L1_ffn_in['q_w'], 'L1_ffn_q_b': _L1_ffn_in['q_b'], 'L1_ffn_k_w': _L1_ffn_in['k_w'], 'L1_ffn_k_b': _L1_ffn_in['k_b'], 'L1_ffn_v_w': _L1_ffn_in['v_w'], 'L1_ffn_v_b': _L1_ffn_in['v_b'], 'L1_ffn_o_w': _L1_ffn_in['o_w'], 'L1_ffn_o_b': _L1_ffn_in['o_b'], 'L1_ffn_router_w': _L1_ffn_in['router_w'], 'L1_ffn_router_b': _L1_ffn_in['router_b'], 'L1_ffn_w1': _L1_ffn_in['w1'], 'L1_ffn_b1': _L1_ffn_in['b1'], 'L1_ffn_w2': _L1_ffn_in['w2'], 'L1_ffn_b2': _L1_ffn_in['b2']}

def reference(x, ctx_1024, mask_Bx16xSxS2_ff0, L0_attn_Wq, L0_attn_bq, L0_attn_gq, L0_attn_bq_ln, L0_attn_keys, L0_attn_values, L0_attn_Wres, L0_attn_bres, L0_attn_Wmem, L0_attn_bmem, L0_attn_Wo, L0_attn_g_out, L0_attn_b_out, L0_xattn_Wo, L0_ffn_gate_w, L0_ffn_w_gate, L0_ffn_w_up, L0_ffn_w_down, L0_ffn_A1, L0_ffn_B1, L0_ffn_A3, L0_ffn_B3, L0_ffn_A2, L0_ffn_B2, L1_attn_w_qkv, L1_attn_w_proj, L1_attn_b_proj, L1_attn_rpe_q_table, L1_attn_rpe_k_table, L1_attn_rpe_v_table, L1_xattn_W_q, L1_xattn_W_k, L1_xattn_W_v, L1_xattn_W_o, L1_xattn_lambda_q1, L1_xattn_lambda_k1, L1_xattn_lambda_q2, L1_xattn_lambda_k2, L1_xattn_rms_scale, L1_ffn_q_w, L1_ffn_q_b, L1_ffn_k_w, L1_ffn_k_b, L1_ffn_v_w, L1_ffn_v_b, L1_ffn_o_w, L1_ffn_o_b, L1_ffn_router_w, L1_ffn_router_b, L1_ffn_w1, L1_ffn_b1, L1_ffn_w2, L1_ffn_b2):
    import jax
    import jax.numpy as jnp

    def _L0_attn_ref(h, Wq, bq, gq, bq_ln, keys, values, Wres, bres, Wmem, bmem, Wo, g_out, b_out):
        import jax, jax.numpy as jnp
        import numpy as np
        H = 16
        D_MODEL = 256
        D_HEAD = 64
        SLOT = 32
        K_DIM = SLOT // 2
        N_KEYS = 64
        TOP_K = 8
        NUM_SLOTS = 2 * H
        TOTAL = 3 * H
        SLEN, BSZ = (512, 4)
        EPS = 1e-05

        def _ln(x, g, b, eps=1e-05):
            m = x.mean(-1, keepdims=True)
            v = ((x - m) ** 2).mean(-1, keepdims=True)
            return (x - m) / jnp.sqrt(v + eps) * g + b
        slen, bsz, dm = h.shape
        x = h.reshape(-1, dm)
        q = (x @ Wq.T + bq).reshape(-1, TOTAL, K_DIM)
        q = _ln(q, gq, bq_ln)
        key = jnp.concatenate([keys, keys[:H]], axis=0)
        key = key / jnp.linalg.norm(key, axis=-1, keepdims=True)
        scores = jnp.einsum('bnd,nkd->bnk', q, key)
        B = scores.shape[0] * TOTAL
        flat = scores.reshape(B, N_KEYS)
        _, topi = jax.lax.top_k(flat, TOP_K)
        mask = jnp.ones_like(flat).at[jnp.arange(B)[:, None], topi].set(0.0)
        sc = jax.nn.softmax(flat + -1000000.0 * mask, axis=-1).reshape(scores.shape)
        value = jnp.concatenate([values, values[:H]], axis=0)
        out = jnp.einsum('bnk,nkd->bnd', sc, value)
        out = out + q @ Wres.T + bres
        out = out @ Wmem.T + bmem
        out = out.reshape(slen, bsz, TOTAL, D_HEAD)
        head_k, head_v, head_q = (out[:, :, :H], out[:, :, H:2 * H], out[:, :, 2 * H:])
        hq = jax.nn.elu(jnp.transpose(head_q, (1, 2, 0, 3))) + 1.0
        hk = jax.nn.elu(jnp.transpose(head_k, (1, 2, 0, 3))) + 1.0
        hv = jnp.transpose(head_v, (1, 2, 0, 3))
        denom_acc = jnp.cumsum(hk, axis=2)
        denom = jnp.sum(denom_acc * hq, axis=-1, keepdims=True)

        def step(W, qkv):
            qt, kt, vt = qkv
            W = W + jnp.einsum('bhd,bhe->bhde', kt, vt)
            return (W, jnp.einsum('bhd,bhde->bhe', qt, W))
        W0 = jnp.zeros((bsz, H, D_HEAD, D_HEAD), hq.dtype)
        _, outs = jax.lax.scan(step, W0, (jnp.transpose(hq, (2, 0, 1, 3)), jnp.transpose(hk, (2, 0, 1, 3)), jnp.transpose(hv, (2, 0, 1, 3))))
        lo = jnp.transpose(outs, (1, 2, 0, 3))
        scale = 1.0 / np.sqrt(D_HEAD)
        lo = scale * lo / (denom + EPS)
        lo = jnp.transpose(lo, (0, 2, 1, 3)).reshape(bsz, slen, H * D_HEAD)
        lo = jnp.transpose(lo, (1, 0, 2))
        attn = lo @ Wo.T
        return _ln(h + attn, g_out, b_out)

    def _L0_xattn_ref(Q, K, V, Wo, num_heads):
        import jax, jax.numpy as jnp
        import numpy as np
        B, S, D, H = (2, 512, 256, 16)
        b, s, d = Q.shape
        dk = d // num_heads
        q = Q.reshape(b, s, num_heads, dk).transpose(0, 2, 1, 3)
        k = K.reshape(b, s, num_heads, dk).transpose(0, 2, 1, 3)
        v = V.reshape(b, s, num_heads, dk).transpose(0, 2, 1, 3)
        scale = 1.0 / jnp.sqrt(jnp.asarray(dk, dtype=q.dtype))
        logits = jnp.einsum('bhqd,bhkd->bhqk', q, k) * scale
        probs = jax.nn.softmax(logits, axis=-1).astype(q.dtype)
        o = jnp.einsum('bhqk,bhkd->bhqd', probs, v)
        o = o.transpose(0, 2, 1, 3).reshape(b, s, d)
        return jnp.einsum('dk,bsk->bsd', Wo, o)

    def _L0_ffn_ref(hidden_states, gate_w, w_gate, w_up, w_down, A1, B1, A3, B3, A2, B2):
        import jax, jax.numpy as jnp
        import numpy as np
        E = 8
        TOPK = 2
        SCALE = 2.0
        B, S, D = hidden_states.shape
        x = hidden_states.reshape(-1, D)
        N = x.shape[0]
        probs = jax.nn.softmax(x @ gate_w.T, axis=-1)
        vals, idx = jax.lax.top_k(probs, TOPK)
        rw = vals / jnp.sum(vals, axis=-1, keepdims=True)
        weight = jnp.zeros((N, E), x.dtype).at[jnp.arange(N)[:, None], idx].add(rw)
        common_w1 = x @ w_gate.T
        common_w3 = x @ w_up.T
        d1 = jnp.einsum('enr,efr->enf', jnp.einsum('nd,erd->enr', x, A1), B1) * SCALE
        d3 = jnp.einsum('enr,efr->enf', jnp.einsum('nd,erd->enr', x, A3), B3) * SCALE
        act = jax.nn.silu(common_w1[None] + d1) * (common_w3[None] + d3)
        out = jnp.einsum('ne,enf->nf', weight, act) @ w_down.T
        z = jnp.einsum('enf,erf->enr', act, A2)
        out = out + jnp.einsum('ne,enr,edr->nd', weight, z, B2) * SCALE
        return out.reshape(B, S, D)

    def _L1_attn_ref(x, w_qkv, w_proj, b_proj, rpe_q_table, rpe_k_table, rpe_v_table):
        import jax, jax.numpy as jnp
        import numpy as np
        NUM_BUCKETS = 63

        def _rp_bucket(N):
            rel = jnp.arange(N)[None, :] - jnp.arange(N)[:, None]
            half = NUM_BUCKETS // 2
            return (jnp.clip(rel, -half, half) + half).astype(jnp.int32)
        B, N, C = x.shape
        H = rpe_k_table.shape[0]
        hd = C // H
        scale = hd ** (-0.5)
        qkv = (x @ w_qkv.T).reshape(B, N, 3, H, hd).transpose(2, 0, 3, 1, 4)
        q, k, v = (qkv[0] * scale, qkv[1], qkv[2])
        attn = jnp.einsum('bhid,bhjd->bhij', q, k)
        rp = _rp_bucket(N)
        idx = rp[None, None]
        qL = jnp.einsum('bhid,hdm->bhim', q, rpe_k_table)
        attn = attn + jnp.take_along_axis(qL, idx, axis=-1)
        kL = jnp.einsum('bhjd,hdm->bhjm', k * scale, rpe_q_table)
        attn = attn + jnp.swapaxes(jnp.take_along_axis(kL, idx, axis=-1), 2, 3)
        attn = jax.nn.softmax(attn, axis=-1)
        out = jnp.einsum('bhij,bhjd->bhid', attn, v)
        a_t = attn.transpose(2, 3, 0, 1)
        S = jax.vmap(lambda a, seg: jax.ops.segment_sum(a, seg, num_segments=NUM_BUCKETS))(a_t, rp)
        out = out + jnp.einsum('inbh,hnd->bhid', S, rpe_v_table)
        x_out = out.transpose(0, 2, 1, 3).reshape(B, N, C)
        return x_out @ w_proj.T + b_proj

    def _L1_xattn_ref(query, key, value, attn_mask, W_q, W_k, W_v, W_o, lambda_q1, lambda_k1, lambda_q2, lambda_k2, rms_scale):
        import jax, jax.numpy as jnp
        import numpy as np
        B, S, D = (2, 512, 256)
        H = 16
        DH = D // H
        LAMBDA_INIT = 0.8
        EPS = 1e-05
        SCALE = 1.0 / np.sqrt(DH)
        b, s, _ = value.shape
        q = (query @ W_q).reshape(b, s, H, 2 * DH).transpose(0, 2, 1, 3)
        k = (key @ W_k).reshape(b, s, H, 2 * DH).transpose(0, 2, 1, 3)
        v = (value @ W_v).reshape(b, s, H, DH).transpose(0, 2, 1, 3)
        q1, q2 = (q[..., :DH], q[..., DH:])
        k1, k2 = (k[..., :DH], k[..., DH:])
        lam = jnp.exp(jnp.sum(lambda_q1 * lambda_k1, -1)) - jnp.exp(jnp.sum(lambda_q2 * lambda_k2, -1)) + LAMBDA_INIT
        lam = lam[None, :, None, None]
        s1 = jnp.einsum('bhqd,bhkd->bhqk', q1, k1) * SCALE + attn_mask
        s2 = jnp.einsum('bhqd,bhkd->bhqk', q2, k2) * SCALE + attn_mask
        attn = jax.nn.softmax(s1, axis=-1) - lam * jax.nn.softmax(s2, axis=-1)
        out = jnp.einsum('bhqk,bhkd->bhqd', attn, v)
        rms = jnp.sqrt(jnp.mean(out * out, axis=-1, keepdims=True) + EPS)
        out = out / rms * rms_scale
        out = out * (1.0 - LAMBDA_INIT)
        out = out.transpose(0, 2, 1, 3).reshape(b, s, H * DH)
        return out @ W_o

    def _L1_ffn_ref(hidden_states, q_w, q_b, k_w, k_b, v_w, v_b, o_w, o_b, router_w, router_b, w1, b1, w2, b2):
        import jax, jax.numpy as jnp
        import numpy as np
        import math
        D = 256
        H = 16
        E = 8
        TOPK = 2
        LAT = D // 2
        KPH = LAT // H
        HD = D // H

        def _forward(hs, q_w, q_b, k_w, k_b, v_w, v_b, o_w, o_b, router_w, router_b, w1, b1, w2, b2):
            B, S, _ = hs.shape
            Q = (hs @ q_w + q_b).reshape(B, S, H, HD).transpose(0, 2, 1, 3)
            K = (hs @ k_w + k_b).reshape(B, S, H, KPH).transpose(0, 2, 1, 3)
            V = (hs @ v_w + v_b).reshape(B, S, H, KPH).transpose(0, 2, 1, 3)
            scores = jnp.einsum('bhsk,bhtk->bhst', Q[..., :KPH], K) / math.sqrt(KPH)
            attn = jax.nn.softmax(scores, axis=-1)
            ao = jnp.einsum('bhst,bhtv->bhsv', attn, V)
            ao = ao.transpose(0, 2, 1, 3).reshape(B, S, H * KPH)
            ao = jnp.concatenate([ao, jnp.zeros((B, S, D - LAT), ao.dtype)], axis=-1)
            mla_out = ao @ o_w + o_b
            probs = jax.nn.softmax(mla_out @ router_w + router_b, axis=-1)
            topw, topi = jax.lax.top_k(probs, TOPK)
            topw = topw / (topw.sum(-1, keepdims=True) + 1e-08)
            combine = jnp.sum(jax.nn.one_hot(topi, E, dtype=probs.dtype) * topw[..., None], axis=-2)
            h1 = jnp.einsum('bsd,edf->ebsf', mla_out, w1) + b1[:, None, None, :]
            h1 = jax.nn.gelu(h1, approximate=False)
            h2 = jnp.einsum('ebsf,efd->ebsd', h1, w2) + b2[:, None, None, :]
            moe_out = jnp.einsum('bse,ebsd->bsd', combine, h2)
            return hs + 0.3 * moe_out
        return _forward(hidden_states, q_w, q_b, k_w, k_b, v_w, v_b, o_w, o_b, router_w, router_b, w1, b1, w2, b2)
    x = _layernorm(x + _L0_attn_ref(x, L0_attn_Wq, L0_attn_bq, L0_attn_gq, L0_attn_bq_ln, L0_attn_keys, L0_attn_values, L0_attn_Wres, L0_attn_bres, L0_attn_Wmem, L0_attn_bmem, L0_attn_Wo, L0_attn_g_out, L0_attn_b_out), axis=-1)
    x = _layernorm(x + _L0_xattn_ref(x, ctx_1024, ctx_1024, L0_xattn_Wo, 16), axis=-1)
    x = _layernorm(x + _L0_ffn_ref(x, L0_ffn_gate_w, L0_ffn_w_gate, L0_ffn_w_up, L0_ffn_w_down, L0_ffn_A1, L0_ffn_B1, L0_ffn_A3, L0_ffn_B3, L0_ffn_A2, L0_ffn_B2), axis=-1)
    x = _layernorm(x + _L1_attn_ref(x, L1_attn_w_qkv, L1_attn_w_proj, L1_attn_b_proj, L1_attn_rpe_q_table, L1_attn_rpe_k_table, L1_attn_rpe_v_table), axis=-1)
    x = _layernorm(x + _L1_xattn_ref(x, ctx_1024, ctx_1024, mask_Bx16xSxS2_ff0, L1_xattn_W_q, L1_xattn_W_k, L1_xattn_W_v, L1_xattn_W_o, L1_xattn_lambda_q1, L1_xattn_lambda_k1, L1_xattn_lambda_q2, L1_xattn_lambda_k2, L1_xattn_rms_scale), axis=-1)
    x = _layernorm(x + _L1_ffn_ref(x, L1_ffn_q_w, L1_ffn_q_b, L1_ffn_k_w, L1_ffn_k_b, L1_ffn_v_w, L1_ffn_v_b, L1_ffn_o_w, L1_ffn_o_b, L1_ffn_router_w, L1_ffn_router_b, L1_ffn_w1, L1_ffn_b1, L1_ffn_w2, L1_ffn_b2), axis=-1)
    return x

_drawn_inputs = setup_inputs


def setup_inputs(seed=0):
    import zlib

    import numpy as np

    out = dict(_drawn_inputs(seed))
    spreads = {'L0_attn_bq': (0.0, 0.8),
     'L0_attn_gq': (1.0, 0.6),
     'L0_attn_bq_ln': (0.0, 0.8),
     'L0_attn_bres': (0.0, 0.8),
     'L0_attn_bmem': (0.0, 0.8),
     'L0_attn_g_out': (1.0, 0.2),
     'L0_attn_b_out': (0.0, 0.1),
     'L1_attn_b_proj': (0.0, 0.1),
     'L1_xattn_rms_scale': (1.0, 0.6),
     'L1_ffn_q_b': (0.0, 0.8),
     'L1_ffn_k_b': (0.0, 2.0),
     'L1_ffn_v_b': (0.0, 0.8),
     'L1_ffn_o_b': (0.0, 0.8),
     'L1_ffn_router_b': (0.0, 0.527),
     'L1_ffn_b1': (0.0, 0.8),
     'L1_ffn_b2': (0.0, 2.0)}
    factors = {'L0_attn_Wq': 8.0,
     'L0_attn_keys': 8.0,
     'L0_attn_values': 8.0,
     'L0_attn_Wres': 8.0,
     'L0_attn_Wmem': 8.0,
     'L0_attn_Wo': 7.729,
     'L0_ffn_gate_w': 8.0,
     'L0_ffn_A1': 8.0,
     'L0_ffn_B1': 8.0,
     'L0_ffn_A3': 8.0,
     'L0_ffn_B3': 8.0,
     'L0_ffn_A2': 8.0,
     'L0_ffn_B2': 8.0,
     'L1_attn_rpe_q_table': 8.0,
     'L1_attn_rpe_k_table': 8.0,
     'L1_attn_rpe_v_table': 4.583,
     'L1_xattn_W_q': 3.061,
     'L1_xattn_W_k': 3.019,
     'L1_xattn_lambda_q1': 8.0,
     'L1_xattn_lambda_k1': 8.0,
     'L1_xattn_lambda_q2': 8.0,
     'L1_xattn_lambda_k2': 8.0,
     'L1_ffn_q_w': 8.0,
     'L1_ffn_k_w': 8.0,
     'L1_ffn_v_w': 8.0,
     'L1_ffn_o_w': 8.0,
     'L1_ffn_router_w': 8.0,
     'L1_ffn_w1': 8.0,
     'L1_ffn_w2': 8.0}
    for name, (base, spread) in spreads.items():
        noise = np.random.default_rng([zlib.crc32(name.encode()), seed]).standard_normal(out[name].shape)
        drawn = base * np.exp(spread * noise) if base else spread * noise
        out[name] = jnp.asarray(drawn.astype(out[name].dtype))
    for name, factor in factors.items():
        out[name] = (out[name] * factor).astype(out[name].dtype)
    return out
```

```python
from contextlib import ExitStack, contextmanager

import numpy as np
import concourse.bass as bass
from concourse import mybir

F32 = mybir.dt.float32
U32 = mybir.dt.uint32
ALU = mybir.AluOpType
ACT = mybir.ActivationFunctionType
AX = mybir.AxisListType
P = 128
D = 256
DC = D // P
NB = 16
S = 256
NT = S // P
H = 16
EPS = 1e-5


class Scope:

    def __init__(self, nc, ctx, prefix):
        self.nc, self.ctx, self.prefix, self.sems = nc, ctx, prefix, []

    def sb(self, name, shape, dt=F32):
        return self.ctx.enter_context(self.nc.sbuf_tensor(f"{self.prefix}_{name}", list(shape), dt))

    def ps(self, name, shape=(P, 512)):
        return self.ctx.enter_context(self.nc.psum_tensor(f"{self.prefix}_{name}", list(shape), F32))

    def sem(self, name):
        s = self.nc.alloc_semaphore(name=f"{self.prefix}_{name}")
        self.sems.append(s)
        return s

    def clear(self):
        self.nc.all_engine_barrier()
        for s in self.sems:
            self.nc.gpsimd.sem_clear(s)
        self.nc.all_engine_barrier()

    def release(self):
        for s in self.sems:
            self.nc.release_semaphore(s)


@contextmanager
def stage(nc, prefix):
    with ExitStack() as ctx:
        scope = Scope(nc, ctx, prefix)
        yield scope
        scope.release()


class Chain:

    def __init__(self, eng, sem):
        self.eng, self.sem, self.n = eng, sem, 0

    def __call__(self, instruction):
        self.n += 1
        instruction.then_inc(self.sem, 1)
        self.eng.wait_ge(self.sem, self.n)


def make_identity(nc, sc, ident):
    filled, done = sc.sem("ident_filled"), sc.sem("ident_done")
    with nc.Block() as block:
        @block.gpsimd
        def _(pool):
            nc.gpsimd.memset(ident[:, :], 0.0).then_inc(filled, 1)
            pool.wait_ge(filled, 1)
            nc.gpsimd.affine_select(out=ident[:, :], in_=ident[:, :], compare_op=ALU.not_equal, fill=1.0,
                                    base=0, pattern=[[-1, P]], channel_multiplier=1).then_inc(done, 1)
            pool.wait_ge(done, 1)


def load_weights(nc, sc, ident, zeroed, loads, turned):
    s_zero, s_load = sc.sem("w_zeroed"), sc.sem("w_loaded")
    s_tr, s_ev = sc.sem("w_transposed"), sc.sem("w_evacuated")
    with ExitStack() as ctx:
        slots = [ctx.enter_context(nc.psum_tensor(f"{sc.prefix}_wt{i}", [P, P], F32)) for i in range(2)]
        with nc.Block() as block:
            @block.gpsimd
            def _(pool):
                for t in zeroed:
                    nc.gpsimd.memset(t, 0.0).then_inc(s_zero, 1)

            @block.sync
            def _(sp):
                if zeroed:
                    sp.wait_ge(s_zero, len(zeroed))
                for dst, src in loads:
                    sp.dma_start(dst, src).then_inc(s_load, 16)
                sp.wait_ge(s_load, 16 * len(loads))

            @block.tensor
            def _(pe):
                if turned:
                    pe.wait_ge(s_load, 16 * len(loads))
                for n, (src, dst) in enumerate(turned):
                    p, f = src.shape[0], int(np.prod(src.shape[1:]))
                    if n >= 2:
                        pe.wait_ge(s_ev, n - 1)
                    nc.tensor.transpose(slots[n % 2][0:f, 0:p], src, ident[0:p, 0:p]).then_inc(s_tr, 1)

            @block.vector
            def _(dve):
                for n, (src, dst) in enumerate(turned):
                    p, f = src.shape[0], int(np.prod(src.shape[1:]))
                    dve.wait_ge(s_tr, n + 1)
                    nc.vector.tensor_copy(dst, slots[n % 2][0:f, 0:p]).then_inc(s_ev, 1)
    sc.clear()


def rows(x, b):
    return x[b, :, :].rearrange("(t p) d -> p t d", p=P)


def memory_constants():
    p = np.arange(P)
    same, step = (p[:, None] % 8) == (p[None, :] % 8), (p[:, None] // 8) <= (p[None, :] // 8)
    return {"causal": (same & step).astype(np.float32)}


def self_attention_0(nc, x_in, x_out, W):
    TOTAL, KD, NK, SLOT, DH, SLOTS = 3 * H, 16, 64, 32, 64, 2 * H
    QC = TOTAL * KD // P
    PR, FO = TOTAL // 2, H * DH // P
    BIG = 3.0e38
    with stage(nc, "sa0") as sc:
        ident = sc.sb("ident", [P, P])
        make_identity(nc, sc, ident)
        wqT, bq = sc.sb("wqT", [P, DC, TOTAL * KD]), sc.sb("bq", [1, TOTAL * KD])
        woT = sc.sb("woT", [P, FO, D])
        kblk = sc.sb("keys", [P, SLOTS // 8, 8 * NK])
        vblk = sc.sb("values", [P, SLOTS // 2, P])
        wr, bm = sc.sb("wr", [P, 4, P]), sc.sb("bm", [1, P])
        gq, bl = sc.sb("gq", [P, KD]), sc.sb("bq_ln", [P, KD])
        g_out, b_out = sc.sb("g_out", [P, D]), sc.sb("b_out", [P, D])
        causal, ones = sc.sb("causal", [P, P]), sc.sb("ones", [1, S])
        row = lambda name: W["L0_attn_" + name].rearrange("(a n) -> a n", a=1)
        with ExitStack() as raw_ctx:
            raw = lambda name, shape: raw_ctx.enter_context(nc.sbuf_tensor(f"sa0_raw_{name}", shape, F32))
            wq_r, wo_r = raw("wq", [P, QC, D]), raw("wo", [P, DC, H * DH])
            k_r, k_pad = raw("keys", [P, SLOTS // 2, KD]), raw("keys_pad", [P, SLOTS // 2, P])
            k_sq, k_ss, k_rn = raw("keys_sq", [P, SLOTS // 2, KD]), raw("keys_ss", [P, SLOTS // 2]), raw("keys_rn", [P, SLOTS // 2])
            k_pw = raw("keys_pw", [P, SLOTS // 2])
            v_r, vT = raw("values", [P, SLOTS // 2, SLOT]), raw("valuesT", [SLOT, SLOTS // 2, P])
            wm_r, wmT = raw("wmem", [DH, SLOT]), raw("wmemT", [SLOT, DH])
            wres_r, bres, bmem = raw("wres", [SLOT, 2, P]), raw("bres", [SLOT, 1]), raw("bmem", [1, DH])
            loads = [(wq_r[:, :, :], W["L0_attn_Wq"].rearrange("(c p) d -> p c d", p=P)),
                     (wo_r[:, :, :], W["L0_attn_Wo"].rearrange("(c p) f -> p c f", p=P)),
                     (bq[:, :], row("bq")), (bres[:, :], W["L0_attn_bres"].rearrange("(n a) -> n a", a=1)), (bmem[:, :], row("bmem")),
                     (wm_r[:, :], W["L0_attn_Wmem"]), (causal[:, :], W["const_causal"])]
            for hp in range(2):
                for dst, name in ((k_r, "keys"), (v_r, "values")):
                    loads.append((dst[NK * hp:NK * (hp + 1), :, :],
                                  W["L0_attn_" + name].rearrange("(r hp) k d -> hp k r d", hp=2)[hp, :, :, :]))
                for a in range(4):
                    loads.append((wres_r[:, hp, 32 * a + 16 * hp:32 * a + 16 * (hp + 1)], W["L0_attn_Wres"]))
            for dst, name, n in ((gq, "gq", KD), (bl, "bq_ln", KD), (g_out, "g_out", D), (b_out, "b_out", D)):
                loads.append((dst[:, :], row(name).broadcast_to([P, n])))
            turned = [(wq_r[:, o, c * P:(c + 1) * P], wqT[:, c, o * P:(o + 1) * P]) for o in range(QC) for c in range(DC)]
            turned += [(wo_r[:, o, f * P:(f + 1) * P], woT[:, f, o * P:(o + 1) * P]) for o in range(DC) for f in range(FO)]
            turned += [(v_r[:, r, :], vT[:, r, :]) for r in range(SLOTS // 2)] + [(wm_r[:, :], wmT[:, :])]
            load_weights(nc, sc, ident, [k_pad[:, :, :], wres_r[:, :, :], vblk[:, :, :], wr[:, :, :]], loads, turned)
            s_pw, s_ss, s_rn, s_kp, s_tr, s_ev, s_ch = (sc.sem(n) for n in ("k_pw", "k_ss", "k_rn", "k_pad", "k_tr", "k_ev", "k_ch"))
            with ExitStack() as psum_ctx:
                tmp = [psum_ctx.enter_context(nc.psum_tensor(f"sa0_prep{i}", [P, P], F32)) for i in range(2)]
                N = SLOTS // 2
                with nc.Block() as block:
                    @block.gpsimd
                    def _(pool):
                        nc.gpsimd.memset(ones[:, :], 1.0).then_inc(s_pw, 1)
                        nc.gpsimd.memset(k_pw[:, :], -0.5).then_inc(s_pw, 1)
                        pool.wait_ge(s_pw, 2)
                        pool.wait_ge(s_ss, 1)
                        nc.gpsimd.tensor_tensor(k_rn[:, :], k_ss[:, :], k_pw[:, :], ALU.pow).then_inc(s_rn, 1)

                    @block.tensor
                    def _(pe):
                        pe.wait_ge(s_pw, 2)
                        pe.wait_ge(s_kp, 1)
                        for n in range(N):
                            if n >= 2:
                                pe.wait_ge(s_ev, n - 1)
                            nc.tensor.transpose(tmp[n % 2][:, :], k_pad[:, n, :], ident[:, :]).then_inc(s_tr, 1)
                        for n in range(N, 2 * N):
                            pe.wait_ge(s_ev, n - 1)
                            nc.tensor.matmul(tmp[n % 2][:, 0:DH], vT[:, n - N, :], wmT[:, :], start=True, stop=True).then_inc(s_tr, 1)
                        pe.wait_ge(s_ev, 2 * N)
                        for hp in range(2):
                            ins = nc.tensor.matmul(tmp[0][:, hp * DH:(hp + 1) * DH], wres_r[:, hp, :], wmT[:, :], start=True, stop=True)
                        nc.tensor.matmul(tmp[1][0:1, 0:DH], bres[:, :], wmT[:, :], start=True, stop=True).then_inc(s_tr, 1)

                    @block.vector
                    def _(dve):
                        link = Chain(dve, s_ch)
                        link(nc.vector.tensor_tensor(k_sq[:, :, :], k_r[:, :, :], k_r[:, :, :], ALU.mult))
                        nc.vector.tensor_reduce(k_ss[:, :], k_sq[:, :, :], AX.X, ALU.add).then_inc(s_ss, 1)
                        dve.wait_ge(s_rn, 1)
                        link(nc.vector.tensor_tensor(k_r[:, :, :], k_r[:, :, :], k_rn[:, :].unsqueeze(2).broadcast_to([P, N, KD]), ALU.mult))
                        for r in range(N):
                            for hp in range(2):
                                at = (2 * (r % 4) + hp) * KD
                                ins = nc.vector.tensor_copy(k_pad[NK * hp:NK * (hp + 1), r, at:at + KD], k_r[NK * hp:NK * (hp + 1), r, :])
                        ins.then_inc(s_kp, 1)
                        for n in range(N):
                            dve.wait_ge(s_tr, n + 1)
                            nc.vector.tensor_copy(kblk[:, n // 4, (n % 4) * P:(n % 4 + 1) * P], tmp[n % 2][:, :]).then_inc(s_ev, 1)
                        for n in range(N, 2 * N):
                            dve.wait_ge(s_tr, n + 1)
                            for hp in range(2):
                                ins = nc.vector.tensor_copy(vblk[NK * hp:NK * (hp + 1), n - N, DH * hp:DH * (hp + 1)],
                                                            tmp[n % 2][NK * hp:NK * (hp + 1), 0:DH])
                            ins.then_inc(s_ev, 1)
                        dve.wait_ge(s_tr, 2 * N + 1)
                        for a in range(4):
                            link(nc.vector.tensor_copy(wr[32 * a:32 * a + 32, a, :], tmp[0][32 * a:32 * a + 32, :]))
                        for hp in range(2):
                            link(nc.vector.tensor_tensor(bm[:, hp * DH:(hp + 1) * DH], tmp[1][0:1, 0:DH], bmem[:, :], ALU.add))
        x, y, xT = sc.sb("x", [P, NT, D]), sc.sb("y", [P, NT, D]), sc.sb("xT", [P, DC, S])
        q, sq = sc.sb("q", [P, NT, TOTAL * KD]), sc.sb("sq", [P, TOTAL * KD])
        mean, var, rstd, pw = (sc.sb(n, [P, NT, TOTAL]) for n in ("mean", "var", "rstd", "pw"))
        qT = sc.sb("qT", [P, QC, S])
        mx, d8, s8 = sc.sb("top8", [P, 2, 8, 8]), sc.sb("top8_shift", [P, 2, 8, 8]), sc.sb("sum8", [P, 2, 8])
        sh, rep, em = sc.sb("shift", [P, 2, 8 * NK]), sc.sb("replaced", [P, 2, 8 * NK]), sc.sb("em", [P, 2, 8 * NK])
        wT = sc.sb("wT", [P, PR, S])
        ex = sc.sb("ex", [P, 2, 2 * S])
        hk, hq = sc.sb("hk", [P, PR // 3, S]), sc.sb("hq", [P, PR // 3, S])
        v = sc.sb("v", [P, NT, H, DH + 1])
        at = sc.sb("at", [P, 2, 2, 2, P])
        den = sc.sb("den", [P, 2, 4])
        lo, loT = sc.sb("lo", [P, NT, H * DH]), sc.sb("loT", [P, FO, S])
        banks = [sc.ps(f"bank{i}") for i in range(8)]
        L = NormTiles(sc, 2 * NT)
        (s_x, s_xT, s_xTs, s_q, s_var, s_rstd, s_pw, s_qn, s_qT, s_qTs, s_sc, s_sh, s_e, s_em, s_en, s_tr, s_wT, s_kq, s_mn, s_ex, s_hh, s_v, s_vs,
         s_a, s_at, s_lo, s_los, s_loT, s_loTs, s_y, s_dve, s_ln, s_st) = (sc.sem(n) for n in (
             "x xT xTs q var rstd pw qn qT qTs sc sh e em en tr wT kq mn ex hh v vs a at lo los loT loTs y dve ln st").split())
        steps = [(c, t) for c in range(QC) for t in range(NT)]
        NS = len(steps)
        kq = [(dst, i, pair0) for dst, pair0 in ((hk, 0), (hq, PR * 2 // 3)) for i in range(4)]
        vsteps = [(t, half) for t in range(NT) for half in range(2)]
        groups = [(t, g) for t in range(NT) for g in range(4)]
        seqs = lambda ap, b, t: ap[:, bass.ds(b * 16 + 8 * t, 8), :]
        with nc.Fori(0, NB) as b:
            L.asked = 0
            with nc.Block() as block:
                @block.sync
                def _(sp):
                    for t in range(NT):
                        sp.dma_start(x[:, t, :], seqs(x_in, b, t)).then_inc(s_x, 16)
                    sp.wait_ge(s_ln, 1)
                    for t in range(NT):
                        sp.dma_start(seqs(x_out, b, t), y[:, t, :]).then_inc(s_st, 16)
                    sp.wait_ge(s_st, 16 * NT)

                @block.gpsimd
                def _(pool):
                    nc.gpsimd.memset(pw[:, :, :], -0.5).then_inc(s_pw, 1)
                    pool.wait_ge(s_pw, 1)
                    for t in range(NT):
                        pool.wait_ge(s_var, t + 1)
                        nc.gpsimd.tensor_tensor(rstd[:, t, :], var[:, t, :], pw[:, t, :], ALU.pow).then_inc(s_rstd, 1)
                    for n in range(NS):
                        pool.wait_ge(s_em, n + 1)
                        e = em[:, n % 2, :].rearrange("p (h k) -> p h k", h=8)
                        nc.gpsimd.tensor_tensor(e, e, s8[:, n % 2, :].unsqueeze(2).broadcast_to([P, 8, NK]), ALU.mult).then_inc(s_en, 1)
                    norm_powers(nc, pool, L, range(2 * NT))

                @block.tensor
                def _(pe):
                    pe.wait_ge(s_x, 16 * NT)
                    for c in range(DC):
                        for t in range(NT):
                            ins = nc.tensor.transpose(banks[0][:, c * S + t * P:c * S + (t + 1) * P],
                                                      x[:, t, c * P:(c + 1) * P], ident[:, :])
                    ins.then_inc(s_xT, 1)
                    pe.wait_ge(s_xTs, 1)
                    for t in range(NT):
                        for lo_, n in ((0, 512), (512, 256)):
                            o = banks[1 + 2 * t + lo_ // 512][:, 0:n]
                            for c in range(DC):
                                nc.tensor.matmul(o, xT[:, c, t * P:(t + 1) * P], wqT[:, c, lo_:lo_ + n], start=(c == 0), stop=False)
                            ins = nc.tensor.matmul(o, ones[0:1, 0:P], bq[0:1, lo_:lo_ + n], start=False, stop=True)
                        ins.then_inc(s_q, 1)
                    pe.wait_ge(s_qn, NT)
                    for j in range(QC // 2):
                        for k in range(2):
                            for t in range(NT):
                                c = 2 * j + k
                                ins = nc.tensor.transpose(banks[5 + j][:, k * S + t * P:k * S + (t + 1) * P],
                                                          q[:, t, c * P:(c + 1) * P], ident[:, :])
                        ins.then_inc(s_qT, 1)
                    pe.wait_ge(s_qTs, QC // 2)
                    for n in range(NS + 1):
                        if n < NS:
                            c, t = steps[n]
                            if n >= 2:
                                pe.wait_ge(s_sh, n - 1)
                            nc.tensor.matmul(banks[n % 2][:, :], qT[:, c, t * P:(t + 1) * P], kblk[:, c % 4, :],
                                             start=True, stop=True).then_inc(s_sc, 1)
                        if n >= 1:
                            m = n - 1
                            pe.wait_ge(s_en, m + 1)
                            if m >= 2:
                                pe.wait_ge(s_wT, m - 1)
                            for r in range(4):
                                ins = nc.tensor.transpose(banks[2 + m % 2][:, r * P:(r + 1) * P], em[:, m % 2, r * P:(r + 1) * P],
                                                          ident[:, :])
                            ins.then_inc(s_tr, 1)
                    pe.wait_ge(s_wT, NS)

                    def mixed(o, r, tok, tokens_stationary):
                        c, a = r // 4, r % 4
                        parts = ((wT[:, r, tok], vblk[:, r % 16, :]), (qT[:, c, tok], wr[:, a, :]),
                                 (ones[0:1, 0:tok.stop - tok.start], bm[0:1, :]))
                        for n, (tokens, w) in enumerate(parts):
                            l, rr = (tokens, w) if tokens_stationary else (w, tokens)
                            ins = nc.tensor.matmul(o, l, rr, start=(n == 0), stop=(n == 2))
                        return ins

                    for n, (dst, i, pair0) in enumerate(kq):
                        if n >= 2:
                            pe.wait_ge(s_hh, n - 1)
                        for k in range(2):
                            ins = mixed(banks[4 + n % 2][:, k * S:(k + 1) * S], pair0 + 2 * i + k, slice(0, S), False)
                        ins.then_inc(s_kq, 1)
                    for n, (t, half) in enumerate(vsteps):
                        if n >= 2:
                            pe.wait_ge(s_vs, n - 1)
                        for k in range(4):
                            ins = mixed(banks[6 + n % 2][:, k * P:(k + 1) * P], H // 2 + 4 * half + k, slice(t * P, (t + 1) * P), True)
                        ins.then_inc(s_v, 1)
                    pe.wait_ge(s_hh, len(kq))
                    pe.wait_ge(s_vs, len(vsteps))
                    NGR = len(groups)
                    for n in range(NGR + 1):
                        if n < NGR:
                            t, g = groups[n]
                            if n >= 2:
                                pe.wait_ge(s_at, n - 1)
                            for k in range(4):
                                h = 4 * g + k
                                r, p0 = h // 2, DH * (h % 2)
                                ins = nc.tensor.matmul(banks[4 * (k % 2) + n % 2][:, (k // 2) * P:(k // 2 + 1) * P], hk[p0:p0 + DH, r, t * P:(t + 1) * P],
                                                       hq[p0:p0 + DH, r, t * P:(t + 1) * P], start=True, stop=True)
                            ins.then_inc(s_a, 1)
                        if n >= 1:
                            m = n - 1
                            t, g = groups[m]
                            pe.wait_ge(s_at, m + 1)
                            if m >= 2:
                                pe.wait_ge(s_los, m - 1)
                            for k in range(4):
                                ins = nc.tensor.matmul(banks[2 + m % 2][:, k * (DH + 1):(k + 1) * (DH + 1)], at[:, m % 2, k % 2, k // 2, :],
                                                       v[:, t, 4 * g + k, :], start=True, stop=True)
                            ins.then_inc(s_lo, 1)
                    pe.wait_ge(s_los, NGR)
                    for n in range(FO // 2):
                        if n >= 2:
                            pe.wait_ge(s_loTs, n - 1)
                        for k in range(2):
                            for t in range(NT):
                                f = 2 * n + k
                                ins = nc.tensor.transpose(banks[4 + n % 2][:, k * S + t * P:k * S + (t + 1) * P],
                                                          lo[:, t, f * P:(f + 1) * P], ident[:, :])
                        ins.then_inc(s_loT, 1)
                    pe.wait_ge(s_loTs, FO // 2)
                    for t in range(NT):
                        for f in range(FO):
                            ins = nc.tensor.matmul(banks[6][:, t * D:(t + 1) * D], loT[:, f, t * P:(t + 1) * P], woT[:, f, :],
                                                   start=(f == 0), stop=(f == FO - 1))
                    ins.then_inc(s_y, 1)

                @block.scalar
                def _(act):
                    for n in range(NS + 1):
                        if n < NS:
                            act.wait_ge(s_sh, n + 1)
                            nc.scalar.activation(d8[:, n % 2, :, :], d8[:, n % 2, :, :], ACT.Exp)
                            nc.scalar.activation(sh[:, n % 2, :], sh[:, n % 2, :], ACT.Exp).then_inc(s_e, 1)
                        if n >= 1:
                            m = n - 1
                            c, t = steps[m]
                            act.wait_ge(s_tr, m + 1)
                            nc.scalar.copy(wT[:, 4 * c:4 * c + 4, t * P:(t + 1) * P],
                                           banks[2 + m % 2][:, :].rearrange("p (r s) -> p r s", r=4)).then_inc(s_wT, 1)
                    for n in range(len(kq)):
                        act.wait_ge(s_mn, n + 1)
                        nc.scalar.activation(ex[:, n % 2, :], ex[:, n % 2, :], ACT.Exp).then_inc(s_ex, 1)
                    for n, (t, half) in enumerate(vsteps):
                        act.wait_ge(s_v, n + 1)
                        nc.scalar.copy(v[:, t, 8 * half:8 * half + 8, 0:DH], banks[6 + n % 2][:, :].rearrange("p (h e) -> p h e", h=8))\
                            .then_inc(s_vs, 1)
                    for n in range(FO // 2):
                        act.wait_ge(s_loT, n + 1)
                        nc.scalar.copy(loT[:, 2 * n:2 * n + 2, :], banks[4 + n % 2][:, :].rearrange("p (f s) -> p f s", f=2))\
                            .then_inc(s_loTs, 1)

                @block.vector
                def _(dve):
                    link = Chain(dve, s_dve)
                    heads = lambda ap: ap.rearrange("p (h d) -> p h d", d=KD)
                    link(nc.vector.memset(v[:, :, :, DH:DH + 1], 1.0))
                    dve.wait_ge(s_xT, 1)
                    nc.vector.tensor_copy(xT[:, :, :], banks[0][:, :].rearrange("p (c s) -> p c s", c=DC)).then_inc(s_xTs, 1)
                    for t in range(NT):
                        dve.wait_ge(s_q, t + 1)
                        for lo_, n in ((0, 512), (512, 256)):
                            h0, nh = lo_ // KD, n // KD
                            ins = nc.vector.tensor_reduce(mean[:, t, h0:h0 + nh], heads(banks[1 + 2 * t + lo_ // 512][:, 0:n]), AX.X, ALU.add)
                        link(ins)
                        link(nc.vector.tensor_scalar(mean[:, t, :], mean[:, t, :], 1.0 / KD, None, ALU.mult))
                        for lo_, n in ((0, 512), (512, 256)):
                            h0, nh = lo_ // KD, n // KD
                            ins = nc.vector.tensor_tensor(heads(q[:, t, lo_:lo_ + n]), heads(banks[1 + 2 * t + lo_ // 512][:, 0:n]),
                                                          mean[:, t, h0:h0 + nh].unsqueeze(2).broadcast_to([P, nh, KD]), ALU.subtract)
                        link(ins)
                        link(nc.vector.tensor_tensor(sq[:, :], q[:, t, :], q[:, t, :], ALU.mult))
                        link(nc.vector.tensor_reduce(var[:, t, :], heads(sq[:, :]), AX.X, ALU.add))
                        nc.vector.tensor_scalar(var[:, t, :], var[:, t, :], 1.0 / KD, EPS, ALU.mult, ALU.add).then_inc(s_var, 1)
                    for t in range(NT):
                        dve.wait_ge(s_rstd, t + 1)
                        link(nc.vector.tensor_tensor(heads(q[:, t, :]), heads(q[:, t, :]),
                                                     rstd[:, t, :].unsqueeze(2).broadcast_to([P, TOTAL, KD]), ALU.mult))
                        link(nc.vector.tensor_tensor(heads(q[:, t, :]), heads(q[:, t, :]),
                                                     gq[:, :].unsqueeze(1).broadcast_to([P, TOTAL, KD]), ALU.mult))
                        nc.vector.tensor_tensor(heads(q[:, t, :]), heads(q[:, t, :]),
                                                bl[:, :].unsqueeze(1).broadcast_to([P, TOTAL, KD]), ALU.add).then_inc(s_qn, 1)
                    for j in range(QC // 2):
                        dve.wait_ge(s_qT, j + 1)
                        nc.vector.tensor_copy(qT[:, 2 * j:2 * j + 2, :], banks[5 + j][:, :].rearrange("p (c s) -> p c s", c=2)).then_inc(s_qTs, 1)

                    def keep(m):
                        dve.wait_ge(s_e, m + 1)
                        link(nc.vector.tensor_reduce(s8[:, m % 2, :], d8[:, m % 2, :, :], AX.X, ALU.add))
                        link(nc.vector.reciprocal(s8[:, m % 2, :], s8[:, m % 2, :]))
                        if m >= 2:
                            dve.wait_ge(s_tr, m - 1)
                        nc.vector.scalar_tensor_tensor(em[:, m % 2, :], rep[:, m % 2, :], BIG, sh[:, m % 2, :],
                                                       ALU.is_equal, ALU.mult).then_inc(s_em, 1)

                    for n in range(NS + 1):
                        if n < NS:
                            dve.wait_ge(s_sc, n + 1)
                            if n >= 2:
                                dve.wait_ge(s_en, n - 1)
                                dve.wait_ge(s_em, n - 1)
                            bank = banks[n % 2]
                            for k in range(8):
                                ins = nc.vector.max(mx[:, n % 2, k, :], bank[:, k * NK:(k + 1) * NK])
                            link(ins)
                            for k in range(8):
                                ins = nc.vector.match_replace(rep[:, n % 2, k * NK:(k + 1) * NK], mx[:, n % 2, k, :],
                                                              bank[:, k * NK:(k + 1) * NK], BIG)
                            nc.vector.tensor_tensor(d8[:, n % 2, :, :], mx[:, n % 2, :, :],
                                                    mx[:, n % 2, :, 0:1].broadcast_to([P, 8, 8]), ALU.subtract)
                            link(nc.vector.tensor_tensor(sh[:, n % 2, :].rearrange("p (h k) -> p h k", h=8), bank[:, :].rearrange("p (h k) -> p h k", h=8),
                                                    mx[:, n % 2, :, 0:1].broadcast_to([P, 8, NK]), ALU.subtract))
                            nc.vector.engine_nop().then_inc(s_sh, 1)
                        if n >= 1:
                            keep(n - 1)
                    for n in range(len(kq) + 1):
                        if n < len(kq):
                            dve.wait_ge(s_kq, n + 1)
                            nc.vector.tensor_scalar(ex[:, n % 2, :], banks[4 + n % 2][:, :], 0.0, None, ALU.min).then_inc(s_mn, 1)
                        if n >= 1:
                            m = n - 1
                            dst, i, _ = kq[m]
                            dve.wait_ge(s_ex, m + 1)
                            nc.vector.scalar_tensor_tensor(dst[:, 2 * i:2 * i + 2, :].rearrange("p r s -> p (r s)"), banks[4 + m % 2][:, :], 0.0,
                                                           ex[:, m % 2, :], ALU.max, ALU.add).then_inc(s_hh, 1)
                            dve.wait_ge(s_hh, m + 1)
                    for n in range(len(groups) + 1):
                        if n < len(groups):
                            dve.wait_ge(s_a, n + 1)
                            if n >= 2:
                                dve.wait_ge(s_lo, n - 1)
                            for k in range(2):
                                ins = nc.vector.tensor_tensor(at[:, n % 2, k, :, :], banks[4 * k + n % 2][:, 0:2 * P].rearrange("p (j s) -> p j s", j=2),
                                                              causal[:, :].unsqueeze(1).broadcast_to([P, 2, P]), ALU.mult)
                            ins.then_inc(s_at, 1)
                        if n >= 1:
                            m = n - 1
                            t, g = groups[m]
                            dve.wait_ge(s_lo, m + 1)
                            bank = banks[2 + m % 2][:, 0:4 * (DH + 1)].rearrange("p (k e) -> p k e", k=4)
                            dn = den[:, m % 2, :].unsqueeze(2)
                            link(nc.vector.tensor_scalar(dn, bank[:, :, DH:DH + 1], EPS, None, ALU.add))
                            link(nc.vector.reciprocal(den[:, m % 2, :], den[:, m % 2, :]))
                            link(nc.vector.tensor_scalar(den[:, m % 2, :], den[:, m % 2, :], DH ** -0.5, None, ALU.mult))
                            nc.vector.tensor_tensor(lo[:, t, 4 * g * DH:4 * (g + 1) * DH].rearrange("p (k e) -> p k e", k=4),
                                                    bank[:, :, 0:DH], dn.broadcast_to([P, 4, DH]), ALU.mult).then_inc(s_los, 1)
                    dve.wait_ge(s_y, 1)
                    for t in range(NT):
                        link(nc.vector.tensor_tensor(y[:, t, :], x[:, t, :], banks[6][:, t * D:(t + 1) * D], ALU.add))
                        layer_norm(nc, dve, link, y[:, t, :], y[:, t, :], L, t)
                        link(nc.vector.tensor_tensor(y[:, t, :], y[:, t, :], g_out[:, :], ALU.mult))
                        link(nc.vector.tensor_tensor(y[:, t, :], y[:, t, :], b_out[:, :], ALU.add))
                    for t in range(NT):
                        link(nc.vector.tensor_tensor(x[:, t, :], x[:, t, :], y[:, t, :], ALU.add))
                        layer_norm(nc, dve, link, x[:, t, :], y[:, t, :], L, NT + t)
                    nc.vector.engine_nop().then_inc(s_ln, 1)
            sc.clear()


def attend(nc, W, pe=None, dve=None, act=None):
    N = W.heads
    if pe is not None:
        for n in range(N + 2):
            if n < N:
                if n >= 2:
                    pe.wait_ge(W.s_exp, n - 1)
                a, blk = n % 4, n // 4
                for t in range(NT):
                    ins = nc.tensor.matmul(W.scores[n % 2][:, t * S:(t + 1) * S],
                                           W.qT[32 * a:32 * a + W.dk, blk, t * P:(t + 1) * P],
                                           W.kT[32 * a:32 * a + W.dk, blk, :], start=True, stop=True)
                ins.then_inc(W.s_scores, 1)
            if 1 <= n <= N:
                m = n - 1
                pe.wait_ge(W.s_exp, m + 1)
                if m >= 2:
                    pe.wait_ge(W.s_wT, m - 1)
                for jt in range(NT):
                    for t in range(NT):
                        ins = nc.tensor.transpose(W.turned[m % 2][:, jt * S + t * P:jt * S + (t + 1) * P],
                                                  W.E[:, m % 3, t, jt * P:(jt + 1) * P], W.ident[:, :])
                ins.then_inc(W.s_turned, 1)
            if n >= 2:
                m = n - 2
                pe.wait_ge(W.s_wT, m + 1)
                for t in range(NT):
                    for jt in range(NT):
                        ins = nc.tensor.matmul(W.out[:, t * (N * W.dv) + m * W.dv:t * (N * W.dv) + (m + 1) * W.dv],
                                               W.wT[:, m % 3, jt, t * P:(t + 1) * P],
                                               W.V(jt, m), start=(jt == 0), stop=(jt == NT - 1))
                ins.then_inc(W.s_av, 1)
    if dve is not None:
        for n in range(N + 1):
            if n < N:
                dve.wait_ge(W.s_scores, n + 1)
                nc.vector.tensor_reduce(W.negmax[:, n, :], W.scores[n % 2][:, :].rearrange("p (t k) -> p t k", t=NT),
                                        AX.X, ALU.max, negate=True).then_inc(W.s_max, 1)
            if n >= 1:
                m = n - 1
                dve.wait_ge(W.s_turned, m + 1)
                if m >= 3:
                    dve.wait_ge(W.s_av, m - 2)
                nc.vector.tensor_copy(W.wT[:, m % 3, :, :], W.turned[m % 2][:, :].rearrange("p (j k) -> p j k", j=NT))\
                    .then_inc(W.s_wT, 1)
    if act is not None:
        for n in range(N):
            act.wait_ge(W.s_max, n + 1)
            if n >= 3:
                act.wait_ge(W.s_turned, n - 2)
            for t in range(NT):
                ins = nc.scalar.activation(W.E[:, n % 3, t, :], W.scores[n % 2][:, t * S:(t + 1) * S], ACT.Exp,
                                           bias=W.negmax[:, n, t:t + 1], scale=1.0,
                                           accum_out=W.sums[:, n, t:t + 1])
            ins.then_inc(W.s_exp, 1)


class AttentionTiles:

    def __init__(self, sc, ident, heads, dk, dv, scores, turned, out):
        self.heads, self.dk, self.dv, self.ident = heads, dk, dv, ident
        self.scores, self.turned, self.out = scores, turned, out
        self.qT = sc.sb("qT", [P, heads // 4, S])
        self.kT = sc.sb("kT", [P, heads // 4, S])
        self.E = sc.sb("E", [P, 3, NT, S])
        self.wT = sc.sb("wT", [P, 3, NT, S])
        self.negmax = sc.sb("negmax", [P, heads, NT])
        self.sums = sc.sb("sums", [P, heads, NT])
        self.s_scores, self.s_max, self.s_exp = sc.sem("scores"), sc.sem("max"), sc.sem("exp")
        self.s_turned, self.s_wT, self.s_av = sc.sem("turned"), sc.sem("wT"), sc.sem("av")


def layer_norm(nc, dve, link, z, out, L, t):
    link(nc.vector.bn_stats(L.stats[:, t, :], z))
    link(nc.vector.bn_aggr(L.mv[:, t, :], L.stats[:, t, :]))
    nc.vector.tensor_scalar(L.ve[:, t:t + 1], L.mv[:, t, 1:2], EPS, None, ALU.add).then_inc(L.s_ve, 1)
    L.asked += 1
    dve.wait_ge(L.s_rstd, L.asked)
    link(nc.vector.tensor_scalar(out, z, L.mv[:, t, 0:1], L.rstd[:, t:t + 1], ALU.subtract, ALU.mult))


class NormTiles:
    def __init__(self, sc, n=NT):
        self.stats, self.mv = sc.sb("ln_stats", [P, n, 6]), sc.sb("ln_mv", [P, n, 2])
        self.ve, self.rstd = sc.sb("ln_ve", [P, n]), sc.sb("ln_rstd", [P, n])
        self.power = sc.sb("ln_power", [P, 1])
        self.s_ve, self.s_rstd, self.s_power = sc.sem("ln_ve"), sc.sem("ln_rstd"), sc.sem("ln_power")
        self.asked = 0


def norm_powers(nc, pool, L, order):
    nc.gpsimd.memset(L.power[:, :], -0.5).then_inc(L.s_power, 1)
    pool.wait_ge(L.s_power, 1)
    for n, t in enumerate(order):
        pool.wait_ge(L.s_ve, n + 1)
        nc.gpsimd.tensor_tensor(L.rstd[:, t:t + 1], L.ve[:, t:t + 1], L.power[:, :], ALU.pow).then_inc(L.s_rstd, 1)


def cross_attention(nc, x_in, x_out, ctx_in, Wo):
    dk = D // H
    with stage(nc, "xa0") as sc:
        ident = sc.sb("ident", [P, P])
        make_identity(nc, sc, ident)
        wo_raw, woT = sc.sb("wo_raw", [P, DC, D]), sc.sb("woT", [P, DC, D])
        xp = sc.sb("x_padded", [P, NT, H, 32])
        cp = sc.sb("ctx_padded", [P, NT, H, 32])
        load_weights(nc, sc, ident, [xp[:, :, :, :], cp[:, :, :, :]],
                     [(wo_raw[:, :, :], Wo.rearrange("(c p) k -> p c k", p=P))],
                     [(wo_raw[:, o, c * P:(c + 1) * P], woT[:, c, o * P:(o + 1) * P]) for o in range(DC) for c in range(DC)])
        x = sc.sb("x", [P, NT, D])
        cx = sc.sb("ctx", [P, NT, D])
        y = sc.sb("y", [P, NT, D])
        o_sb, oT = sc.sb("o", [P, NT, D]), sc.sb("oT", [P, DC, S])
        rs = sc.sb("rsums", [P, H, NT])
        banks = [sc.ps(f"bank{i}") for i in range(8)]
        A = AttentionTiles(sc, ident, H, dk, dk, banks[0:2], banks[2:4], banks[4])
        A.V = lambda jt, h: cx[:, jt, h * dk:(h + 1) * dk]
        L = NormTiles(sc)
        s_x, s_pad, s_qk, s_qkT = sc.sem("x"), sc.sem("pad"), sc.sem("qk"), sc.sem("qkT")
        s_o, s_oT, s_oTs, s_y, s_dve, s_ln, s_st = (sc.sem(n) for n in ("o", "oT", "oTs", "y", "dve", "ln", "stored"))
        with nc.Fori(0, NB) as b:
            L.asked = 0
            with nc.Block() as block:
                @block.sync
                def _(sp):
                    sp.dma_start(x[:, :, :], rows(x_in, b)).then_inc(s_x, 16)
                    sp.dma_start(cx[:, :, :], rows(ctx_in, b)).then_inc(s_x, 16)
                    sp.wait_ge(s_ln, 1)
                    sp.dma_start(rows(x_out, b), y[:, :, :]).then_inc(s_st, 16)
                    sp.wait_ge(s_st, 16)

                @block.gpsimd
                def _(pool):
                    norm_powers(nc, pool, L, range(NT))

                @block.tensor
                def _(pe):
                    pe.wait_ge(s_pad, 2)
                    n = 0
                    for src in (xp, cp):
                        for half in range(2):
                            if n >= 2:
                                pe.wait_ge(s_qkT, n - 1)
                            for k in range(2):
                                for t in range(NT):
                                    blk = 2 * half + k
                                    ins = nc.tensor.transpose(banks[5 + n % 2][:, k * S + t * P:k * S + (t + 1) * P],
                                                              src[:, t, 4 * blk:4 * blk + 4, :].rearrange("p h d -> p (h d)"),
                                                              ident[:, :])
                            ins.then_inc(s_qk, 1)
                            n += 1
                    pe.wait_ge(s_qkT, 4)
                    attend(nc, A, pe=pe)
                    pe.wait_ge(s_o, 1)
                    for c in range(DC):
                        for t in range(NT):
                            ins = nc.tensor.transpose(banks[5][:, c * S + t * P:c * S + (t + 1) * P],
                                                      o_sb[:, t, c * P:(c + 1) * P], ident[:, :])
                    ins.then_inc(s_oT, 1)
                    pe.wait_ge(s_oTs, 1)
                    for t in range(NT):
                        for c in range(DC):
                            ins = nc.tensor.matmul(banks[6][:, t * D:(t + 1) * D], oT[:, c, t * P:(t + 1) * P],
                                                   woT[:, c, :], start=(c == 0), stop=(c == DC - 1))
                    ins.then_inc(s_y, 1)

                @block.scalar
                def _(act):
                    attend(nc, A, act=act)

                @block.vector
                def _(dve):
                    link = Chain(dve, s_dve)
                    dve.wait_ge(s_x, 32)
                    for dst, src in ((xp, x), (cp, cx)):
                        for t in range(NT):
                            ins = nc.vector.tensor_copy(dst[:, t, :, 0:dk], src[:, t, :].rearrange("p (h d) -> p h d", h=H))
                        ins.then_inc(s_pad, 1)
                    for n in range(4):
                        dve.wait_ge(s_qk, n + 1)
                        dst = (A.qT, A.kT)[n // 2][:, 2 * (n % 2):2 * (n % 2) + 2, :]
                        src = banks[5 + n % 2][:, :].rearrange("p (k s) -> p k s", k=2)
                        if n < 2:
                            nc.vector.tensor_scalar(dst, src, dk ** -0.5, None, ALU.mult).then_inc(s_qkT, 1)
                        else:
                            nc.vector.tensor_copy(dst, src).then_inc(s_qkT, 1)
                    attend(nc, A, dve=dve)
                    dve.wait_ge(A.s_exp, H)
                    link(nc.vector.reciprocal(rs[:, :, :], A.sums[:, :, :]))
                    dve.wait_ge(A.s_av, H)
                    for t in range(NT):
                        ins = nc.vector.tensor_tensor(o_sb[:, t, :].rearrange("p (h d) -> p h d", h=H),
                                                      banks[4][:, t * D:(t + 1) * D].rearrange("p (h d) -> p h d", h=H),
                                                      rs[:, :, t:t + 1].broadcast_to([P, H, dk]), ALU.mult)
                    ins.then_inc(s_o, 1)
                    dve.wait_ge(s_oT, 1)
                    nc.vector.tensor_copy(oT[:, :, :], banks[5][:, :].rearrange("p (c s) -> p c s", c=DC)).then_inc(s_oTs, 1)
                    dve.wait_ge(s_y, 1)
                    for t in range(NT):
                        link(nc.vector.tensor_tensor(x[:, t, :], x[:, t, :], banks[6][:, t * D:(t + 1) * D], ALU.add))
                        layer_norm(nc, dve, link, x[:, t, :], y[:, t, :], L, t)
                    nc.vector.engine_nop().then_inc(s_ln, 1)
            sc.clear()


def top2(nc, dve, link, lg, mx, ix, ixf, iota, onehot, t, times):
    link(nc.vector.max(mx[:, t, :], lg[:, t, :]))
    link(nc.vector.max_index(ix[:, t, :], mx[:, t, :], lg[:, t, :]))
    link(nc.vector.tensor_copy(ixf[:, t, :], ix[:, t, 0:2]))
    for k in range(2):
        ins = nc.vector.tensor_scalar(onehot[:, t, k, :], iota[:, :], ixf[:, t, k:k + 1], times, ALU.is_equal, ALU.mult)
    link(ins)


def ffn_0(nc, x_in, x_out, W):
    E, R, F = 8, 16, 1024
    FC, ER, SCALE = F // P, E * R, 2.0
    WD = D + ER
    with stage(nc, "ff0") as sc:
        ident = sc.sb("ident", [P, P])
        make_identity(nc, sc, ident)
        wgT, wuT = sc.sb("wgT", [P, DC, F]), sc.sb("wuT", [P, DC, F])
        wdT = sc.sb("wdT_A2T", [P, FC, WD])
        a13T = sc.sb("A13T", [P, DC, 2 * ER])
        b1T, b3T, b2T = sc.sb("B1T", [P, F]), sc.sb("B3T", [P, F]), sc.sb("B2T", [P, D])
        gateT = sc.sb("gateT", [P, DC, E])
        with ExitStack() as raw_ctx:
            raw = lambda name, shape: raw_ctx.enter_context(nc.sbuf_tensor(f"ff0_raw_{name}", shape, F32))
            wg_r, wu_r = raw("wg", [P, FC, D]), raw("wu", [P, FC, D])
            wd_r, a2_r = raw("wd", [P, DC, F]), raw("A2", [P, F])
            a1_r, a3_r = raw("A1", [P, D]), raw("A3", [P, D])
            b1_r, b3_r, b2_r = raw("B1", [P, FC, ER]), raw("B3", [P, FC, ER]), raw("B2", [P, DC, ER])
            g_r = raw("gate", [E, D])
            loads = [(wg_r[:, :, :], W["L0_ffn_w_gate"].rearrange("(c p) d -> p c d", p=P)),
                     (wu_r[:, :, :], W["L0_ffn_w_up"].rearrange("(c p) d -> p c d", p=P)),
                     (wd_r[:, :, :], W["L0_ffn_w_down"].rearrange("(c p) f -> p c f", p=P)),
                     (a2_r[:, :], W["L0_ffn_A2"].rearrange("e r f -> (e r) f")),
                     (a1_r[:, :], W["L0_ffn_A1"].rearrange("e r d -> (e r) d")),
                     (a3_r[:, :], W["L0_ffn_A3"].rearrange("e r d -> (e r) d")),
                     (g_r[:, :], W["L0_ffn_gate_w"])]
            for dst, src, n in ((b1_r, "L0_ffn_B1", FC), (b3_r, "L0_ffn_B3", FC), (b2_r, "L0_ffn_B2", DC)):
                for c in range(n):
                    loads.append((dst[:, c, :].rearrange("p (e r) -> p e r", e=E),
                                  W[src][:, c * P:(c + 1) * P, :].rearrange("e p r -> p e r")))
            turned = []
            for f in range(FC):
                for c in range(DC):
                    turned += [(wg_r[:, f, c * P:(c + 1) * P], wgT[:, c, f * P:(f + 1) * P]),
                               (wu_r[:, f, c * P:(c + 1) * P], wuT[:, c, f * P:(f + 1) * P]),
                               (wd_r[:, c, f * P:(f + 1) * P], wdT[:, f, c * P:(c + 1) * P])]
                turned += [(a2_r[:, f * P:(f + 1) * P], wdT[:, f, D:WD]),
                           (b1_r[:, f, :], b1T[:, f * P:(f + 1) * P]), (b3_r[:, f, :], b3T[:, f * P:(f + 1) * P])]
            for c in range(DC):
                turned += [(a1_r[:, c * P:(c + 1) * P], a13T[:, c, 0:ER]), (a3_r[:, c * P:(c + 1) * P], a13T[:, c, ER:2 * ER]),
                           (b2_r[:, c, :], b2T[:, c * P:(c + 1) * P]), (g_r[:, c * P:(c + 1) * P], gateT[:, c, :])]
            load_weights(nc, sc, ident, [], loads, turned)
        iota = sc.sb("iota", [P, E])
        s_iota = sc.sem("iota")
        with nc.Block() as block:
            @block.gpsimd
            def _(pool):
                for e in range(E):
                    nc.gpsimd.memset(iota[:, e:e + 1], float(e)).then_inc(s_iota, 1)
                pool.wait_ge(s_iota, E)
        x, y, xT = sc.sb("x", [P, NT, D]), sc.sb("y", [P, NT, D]), sc.sb("xT", [P, DC, S])
        lg, mx = sc.sb("logits", [P, NT, E]), sc.sb("top", [P, NT, 8])
        ix, ixf = sc.sb("index", [P, NT, 8], U32), sc.sb("indexf", [P, NT, 2])
        oh = sc.sb("onehot", [P, NT, 2, E])
        diff, wt = sc.sb("diff", [P, NT, 2]), sc.sb("weight", [P, NT, 2])
        coef = sc.sb("coef", [P, NT, 2, E])
        hm, hT = sc.sb("h", [P, 2, 2, NT, ER]), sc.sb("hT", [P, 2, 2, S])
        sg, a = sc.sb("silu", [P, 3, S]), sc.sb("act", [P, FC, 2, S])
        z, zz, zT = sc.sb("z", [P, NT, ER]), sc.sb("zz", [P, NT, ER]), sc.sb("zT", [P, S])
        banks = [sc.ps(f"bank{i}") for i in range(8)]
        L = NormTiles(sc)
        (s_x, s_xT, s_xTs, s_proj, s_hm, s_hT, s_hTs, s_gu, s_silu, s_act, s_down, s_z, s_zT, s_zTs, s_lo, s_dve, s_diff, s_wt,
         s_ln, s_st) = (sc.sem(n) for n in ("x xT xTs proj hm hT hTs gu silu act down z zT zTs lo dve diff wt ln st").split())
        with nc.Fori(0, NB) as b:
            L.asked = 0
            with nc.Block() as block:
                @block.sync
                def _(sp):
                    sp.dma_start(x[:, :, :], rows(x_in, b)).then_inc(s_x, 16)
                    sp.wait_ge(s_ln, 1)
                    sp.dma_start(rows(x_out, b), y[:, :, :]).then_inc(s_st, 16)
                    sp.wait_ge(s_st, 16)

                @block.gpsimd
                def _(pool):
                    norm_powers(nc, pool, L, range(NT))

                @block.tensor
                def _(pe):
                    pe.wait_ge(s_x, 16)
                    for c in range(DC):
                        for t in range(NT):
                            ins = nc.tensor.transpose(banks[0][:, c * S + t * P:c * S + (t + 1) * P],
                                                      x[:, t, c * P:(c + 1) * P], ident[:, :])
                    ins.then_inc(s_xT, 1)
                    pe.wait_ge(s_xTs, 1)
                    for t in range(NT):
                        for bank, w, n in ((banks[1], gateT, E), (banks[2], a13T, 2 * ER)):
                            for c in range(DC):
                                ins = nc.tensor.matmul(bank[:, t * n:(t + 1) * n], xT[:, c, t * P:(t + 1) * P], w[:, c, :],
                                                       start=(c == 0), stop=(c == DC - 1))
                    ins.then_inc(s_proj, 1)
                    pe.wait_ge(s_hm, 1)
                    for k in range(2):
                        for m in range(2):
                            for t in range(NT):
                                ins = nc.tensor.transpose(banks[3 + k][:, m * S + t * P:m * S + (t + 1) * P],
                                                          hm[:, k, m, t, :], ident[:, :])
                        ins.then_inc(s_hT, 1)
                    pe.wait_ge(s_hTs, 2)
                    for n in range(2 * FC):
                        f, k = n // 2, n % 2
                        if n >= 2:
                            pe.wait_ge(s_act, n - 1)
                        for m, (w, bT) in enumerate(((wgT, b1T), (wuT, b3T))):
                            o = banks[5 + n % 2][:, m * S:(m + 1) * S]
                            for c in range(DC):
                                nc.tensor.matmul(o, w[:, c, f * P:(f + 1) * P], xT[:, c, :], start=(c == 0), stop=False)
                            ins = nc.tensor.matmul(o, bT[:, f * P:(f + 1) * P], hT[:, k, m, :], start=False, stop=True)
                        ins.then_inc(s_gu, 1)
                    pe.wait_ge(s_act, 2 * FC)
                    for k in range(2):
                        for t in range(NT):
                            for f in range(FC):
                                ins = nc.tensor.matmul(banks[2 * k + t][:, 0:WD], a[:, f, k, t * P:(t + 1) * P], wdT[:, f, :],
                                                       start=(f == 0), stop=(f == FC - 1))
                            ins.then_inc(s_down, 1)
                    pe.wait_ge(s_z, 1)
                    for t in range(NT):
                        ins = nc.tensor.transpose(banks[4][:, t * P:(t + 1) * P], z[:, t, :], ident[:, :])
                    ins.then_inc(s_zT, 1)
                    pe.wait_ge(s_zTs, 1)
                    for t in range(NT):
                        ins = nc.tensor.matmul(banks[7][:, t * D:(t + 1) * D], zT[:, t * P:(t + 1) * P], b2T[:, :],
                                               start=True, stop=True)
                    ins.then_inc(s_lo, 1)

                @block.scalar
                def _(act):
                    act.wait_ge(s_diff, 1)
                    nc.scalar.activation(wt[:, :, :], diff[:, :, :], ACT.Sigmoid).then_inc(s_wt, 1)
                    for n in range(2 * FC):
                        act.wait_ge(s_gu, n + 1)
                        if n >= 3:
                            act.wait_ge(s_act, n - 2)
                        nc.scalar.activation(sg[:, n % 3, :], banks[5 + n % 2][:, 0:S], ACT.Silu).then_inc(s_silu, 1)

                @block.vector
                def _(dve):
                    link = Chain(dve, s_dve)
                    dve.wait_ge(s_xT, 1)
                    nc.vector.tensor_copy(xT[:, :, :], banks[0][:, :].rearrange("p (c s) -> p c s", c=DC)).then_inc(s_xTs, 1)
                    dve.wait_ge(s_proj, 1)
                    link(nc.vector.tensor_copy(lg[:, :, :], banks[1][:, 0:NT * E].rearrange("p (t e) -> p t e", t=NT)))
                    for t in range(NT):
                        top2(nc, dve, link, lg, mx, ix, ixf, iota, oh, t, SCALE)
                    nc.vector.tensor_tensor(diff[:, :, 0:1], mx[:, :, 0:1], mx[:, :, 1:2], ALU.subtract)
                    nc.vector.tensor_tensor(diff[:, :, 1:2], mx[:, :, 1:2], mx[:, :, 0:1], ALU.subtract).then_inc(s_diff, 1)
                    for t in range(NT):
                        for k in range(2):
                            for m in range(2):
                                ins = nc.vector.tensor_tensor(
                                    hm[:, k, m, t, :].rearrange("p (e r) -> p e r", e=E),
                                    banks[2][:, t * 2 * ER + m * ER:t * 2 * ER + (m + 1) * ER].rearrange("p (e r) -> p e r", e=E),
                                    oh[:, t, k, :].unsqueeze(2).broadcast_to([P, E, R]), ALU.mult)
                    ins.then_inc(s_hm, 1)
                    dve.wait_ge(s_wt, 1)
                    for t in range(NT):
                        for k in range(2):
                            ins = nc.vector.tensor_scalar(coef[:, t, k, :], oh[:, t, k, :], wt[:, t, k:k + 1], None, ALU.mult)
                    link(ins)
                    for k in range(2):
                        dve.wait_ge(s_hT, k + 1)
                        nc.vector.tensor_copy(hT[:, k, :, :], banks[3 + k][:, :].rearrange("p (m s) -> p m s", m=2)).then_inc(s_hTs, 1)
                    for n in range(2 * FC):
                        dve.wait_ge(s_silu, n + 1)
                        nc.vector.tensor_tensor(a[:, n // 2, n % 2, :], sg[:, n % 3, :], banks[5 + n % 2][:, S:2 * S],
                                                ALU.mult).then_inc(s_act, 1)
                    dve.wait_ge(s_down, 4)
                    for t in range(NT):
                        for k in range(2):
                            link(nc.vector.tensor_tensor(
                                (z, zz)[k][:, t, :].rearrange("p (e r) -> p e r", e=E),
                                banks[2 * k + t][:, D:WD].rearrange("p (e r) -> p e r", e=E),
                                coef[:, t, k, :].unsqueeze(2).broadcast_to([P, E, R]), ALU.mult))
                    nc.vector.tensor_tensor(z[:, :, :], z[:, :, :], zz[:, :, :], ALU.add).then_inc(s_z, 1)
                    dve.wait_ge(s_zT, 1)
                    nc.vector.tensor_copy(zT[:, :], banks[4][:, 0:S]).then_inc(s_zTs, 1)
                    for k in range(2):
                        for t in range(NT):
                            link(nc.vector.scalar_tensor_tensor(x[:, t, :], banks[2 * k + t][:, 0:D], wt[:, t, k:k + 1],
                                                                x[:, t, :], ALU.mult, ALU.add))
                    dve.wait_ge(s_lo, 1)
                    for t in range(NT):
                        link(nc.vector.tensor_tensor(x[:, t, :], x[:, t, :], banks[7][:, t * D:(t + 1) * D], ALU.add))
                        layer_norm(nc, dve, link, x[:, t, :], y[:, t, :], L, t)
                    nc.vector.engine_nop().then_inc(s_ln, 1)
            sc.clear()


RPE = 63
HALF = RPE // 2
GR = 32
NG = S // GR
BW = 128
WIN = GR + 2 * HALF


def window(g):
    lo, hi = GR * g - HALF, GR * g - HALF + WIN
    return max(lo, 0), min(hi, S), max(lo, 0) - lo


def edge_rows(t):
    rows = []
    for side in range(2):
        for edge in range(2):
            same = {}
            for g in (range(4 * t, 4 * t + 4) if side == 0 else range(NG)):
                lo, hi = GR * g - HALF, GR * g - HALF + WIN
                r = (0, max(lo, 0)) if edge == 0 else (min(hi, S), S)
                if side == 1:
                    r = (max(r[0], t * P), min(r[1], (t + 1) * P))
                if r[0] < r[1]:
                    same.setdefault(r if side else (g, r), []).append(g)
            for key, gs in same.items():
                rows.append((side, edge, gs, key if side else key[1]))
    assert len(rows) <= 16
    return rows


def shape_constants():
    qmask, qadd = np.zeros((P, NT, P), np.float32), np.zeros((P, NT, P), np.float32)
    kmask, kadd = np.zeros((P, NT, S), np.float32), np.zeros((P, NT, S), np.float32)
    for a in range(4):
        for t in range(NT):
            qmask[32 * a:32 * a + 16, t] = kmask[32 * a:32 * a + 16, t] = 1.0
            for n, (side, edge, gs, (lo, hi)) in enumerate(edge_rows(t)):
                r = 32 * a + 16 + n
                for g in gs:
                    if side == 0:
                        qmask[r, t, GR * g - t * P:GR * (g + 1) - t * P] = 1.0
                        kadd[r, t, lo:hi] = 1.0
                    else:
                        kmask[r, t, GR * g:GR * (g + 1)] = 1.0
                        qadd[r, t, lo - t * P:hi - t * P] = 1.0
    slots = np.zeros((P, P), np.float32)
    edges = np.zeros((P, NT, 16), np.float32)
    own = np.zeros((P, NT, 16), np.float32)
    for p in range(P):
        slots[p, p] = p % 32 < 16
        for t in range(NT):
            i = t * P + p
            own[p, t, i // GR] = own[p, t, 8 + i // GR] = 1.0
            for g in range(NG):
                edges[p, t, g] = i < GR * g - HALF
                edges[p, t, 8 + g] = i >= GR * g - HALF + WIN
    return {"qmask": qmask, "qadd": qadd, "kmask": kmask, "kadd": kadd, "slots": slots, "edges": edges, "own": own}


def skewed(scratch, g, h0, nh, transposed_t=None):
    lo, hi, cut = window(g)
    base = scratch[h0:h0 + nh, GR * g:GR * (g + 1), 0:hi - lo].rearrange("h p n -> p h n")
    return bass.AP(tensor=base.tensor, offset=base.offset + HALF + cut,
                   ap=[[BW - 1, GR], [S * BW, nh], [1, hi - lo]])


def self_attention_1(nc, x_in, x_out, W):
    DK = D // H
    BLK = H // 4
    with stage(nc, "sa1") as sc:
        ident = sc.sb("ident", [P, P])
        make_identity(nc, sc, ident)
        eq = nc.dram_tensor("rpe_q_rows", (H, S, BW), F32, kind="Internal").ap()
        ek = nc.dram_tensor("rpe_k_rows", (H, S, BW), F32, kind="Internal").ap()
        es = nc.dram_tensor("rpe_sums", (H, S, BW), F32, kind="Internal").ap()
        qwT, kwT = sc.sb("qwT", [P, DC, H * 32]), sc.sb("kwT", [P, DC, H * 32])
        vwT, pwT, pb = sc.sb("vwT", [P, DC, D]), sc.sb("pwT", [P, DC, D]), sc.sb("pb", [1, D])
        qmask, qadd = sc.sb("qmask", [P, NT, P]), sc.sb("qadd", [P, NT, P])
        kmask, kadd = sc.sb("kmask", [P, NT, S]), sc.sb("kadd", [P, NT, S])
        own, slots, edges = sc.sb("own", [P, NT, 16]), sc.sb("slots", [P, P]), sc.sb("edges", [P, NT, 16])
        tq, tk = sc.sb("tq", [P, BLK, RPE]), sc.sb("tk", [P, BLK, RPE])
        tqx, tkx = sc.sb("tqx", [P, BLK, BW]), sc.sb("tkx", [P, BLK, BW])
        extq, extk = sc.sb("extq", [P, NT, BLK, P]), sc.sb("extk", [P, NT, BLK, P])
        rvx, rve = sc.sb("rvx", [P, H, DK]), sc.sb("rve", [P, 2, H, DK])
        zero = sc.sb("zero", [P, 2 * BW])
        bq, bk = sc.sb("bq", [P, NT, 8, S]), sc.sb("bk", [P, NT, 8, S])
        with ExitStack() as raw_ctx:
            raw = lambda name, shape: raw_ctx.enter_context(nc.sbuf_tensor(f"sa1_raw_{name}", shape, F32))
            qw_r, kw_r = raw("qw", [P, BLK, D]), raw("kw", [P, BLK, D])
            vw_r, pw_r = raw("vw", [P, DC, D]), raw("pw", [P, DC, D])
            loads = []
            for blk in range(BLK):
                for a in range(4):
                    h = 4 * blk + a
                    for part, r in enumerate((qw_r, kw_r)):
                        loads.append((r[32 * a:32 * a + DK, blk, :], W["L1_attn_w_qkv"][part * D + h * DK:part * D + (h + 1) * DK, :]))
                    loads += [(tq[32 * a:32 * a + DK, blk, :], W["L1_attn_rpe_k_table"][h, :, :]),
                              (tk[32 * a:32 * a + DK, blk, :], W["L1_attn_rpe_q_table"][h, :, :])]
            loads += [(vw_r[:, :, :], W["L1_attn_w_qkv"][2 * D:3 * D, :].rearrange("(c p) d -> p c d", p=P)),
                      (pw_r[:, :, :], W["L1_attn_w_proj"].rearrange("(c p) d -> p c d", p=P)),
                      (pb[:, :], W["L1_attn_b_proj"].rearrange("(a n) -> a n", a=1))]
            for n, dst in (("qmask", qmask), ("qadd", qadd), ("kmask", kmask), ("kadd", kadd), ("own", own), ("edges", edges)):
                loads.append((dst[:, :, :], W["const_" + n]))
            loads.append((slots[:, :], W["const_slots"]))
            rv = W["L1_attn_rpe_v_table"].rearrange("h m d -> m h d")
            loads += [(rvx[0:GR, :, :], rv[0:1, :, :].broadcast_to([GR, H, DK])),
                      (rvx[GR:GR + RPE - 2, :, :], rv[1:RPE - 1, :, :]),
                      (rvx[GR + RPE - 2:P, :, :], rv[RPE - 1:RPE, :, :].broadcast_to([P - GR - RPE + 2, H, DK])),
                      (rve[:, 0, :, :], rv[0:1, :, :].broadcast_to([P, H, DK])),
                      (rve[:, 1, :, :], rv[RPE - 1:RPE, :, :].broadcast_to([P, H, DK]))]
            for h in range(H):
                loads.append((es[h, :, :].rearrange("(p r) n -> p (r n)", p=P), zero[:, :]))
            turned = []
            for c in range(DC):
                for blk in range(BLK):
                    turned += [(qw_r[:, blk, c * P:(c + 1) * P], qwT[:, c, blk * P:(blk + 1) * P]),
                               (kw_r[:, blk, c * P:(c + 1) * P], kwT[:, c, blk * P:(blk + 1) * P])]
                for o in range(DC):
                    turned += [(vw_r[:, o, c * P:(c + 1) * P], vwT[:, c, o * P:(o + 1) * P]),
                               (pw_r[:, o, c * P:(c + 1) * P], pwT[:, c, o * P:(o + 1) * P])]
            load_weights(nc, sc, ident, [qw_r[:, :, :], kw_r[:, :, :], tq[:, :, :], tk[:, :, :], zero[:, :],
                                         bq[:, :, :, :], bk[:, :, :, :], extq[:, :, :, :], extk[:, :, :, :]], loads, turned)
        ones, vx = sc.sb("ones", [1, P]), sc.sb("vx", [P, NT, H, 32])
        s_t, s_o1 = sc.sem("tables"), sc.sem("ones")
        with nc.Block() as block:
            @block.gpsimd
            def _(pool):
                nc.gpsimd.memset(ones[:, :], 1.0).then_inc(s_o1, 1)
                pool.wait_ge(s_o1, 1)

            @block.vector
            def _(dve):
                link = Chain(dve, s_t)
                link(nc.vector.tensor_scalar(tk[:, :, :], tk[:, :, :], DK ** -0.5, None, ALU.mult))
                for t, x in ((tq, tqx), (tk, tkx)):
                    link(nc.vector.tensor_copy(x[:, :, 0:GR], t[:, :, 0:1].broadcast_to([P, BLK, GR])))
                    link(nc.vector.tensor_copy(x[:, :, GR:GR + RPE - 2], t[:, :, 1:RPE - 1]))
                    link(nc.vector.tensor_copy(x[:, :, GR + RPE - 2:BW], t[:, :, RPE - 1:RPE].broadcast_to([P, BLK, BW - GR - RPE + 2])))
                for t in range(NT):
                    for blk in range(BLK):
                        link(nc.vector.tensor_copy(extq[:, t, blk, :], slots[:, :]))
                        link(nc.vector.tensor_copy(extk[:, t, blk, :], slots[:, :]))
                        for n, (side, edge, _, _) in enumerate(edge_rows(t)):
                            src, dst = ((tq, extq), (tk, extk))[side]
                            m = edge * (RPE - 1)
                            for a in range(4):
                                link(nc.vector.tensor_copy(dst[32 * a:32 * a + DK, t, blk, 32 * a + 16 + n:32 * a + 17 + n],
                                                           src[32 * a:32 * a + DK, blk, m:m + 1]))
                for t in range(NT):
                    link(nc.vector.tensor_copy(vx[:, t, :, 16:32], edges[:, t, :].unsqueeze(1).broadcast_to([P, H, 16])))
        x, y, xT = sc.sb("x", [P, NT, D]), sc.sb("y", [P, NT, D]), sc.sb("xT", [P, DC, S])
        qT, kT = sc.sb("qT", [P, BLK, S]), sc.sb("kT", [P, BLK, S])
        qE, kE = sc.sb("qE", [P, BLK, NT, P]), sc.sb("kE", [P, BLK, NT, S])
        tmp = sc.sb("tmp", [P, 2, 2 * S])
        er = sc.sb("er", [P, 4, NT, BW])
        E = sc.sb("E", [P, 3, NT, S])
        wT = sc.sb("wT", [P, 2, NT, S])
        top, sums, rs = sc.sb("max", [P, H, NT]), sc.sb("sums", [P, H, NT]), sc.sb("rs", [P, H, NT])
        sr, srT = sc.sb("sum_rows", [P, 2, NT, BW]), sc.sb("sum_rowsT", [P, 2, S])
        o_sb, oT = sc.sb("o", [P, NT, D]), sc.sb("oT", [P, DC, S])
        outside, pair = sc.sb("outside", [P, NT, H, 16]), sc.sb("pair", [P, NT, H, 2])
        banks = [sc.ps(f"bank{i}") for i in range(8)]
        L = NormTiles(sc)
        (s_x, s_xT, s_xTs, s_pr, s_prs, s_ext, s_tmp, s_exts, s_row, s_rows, s_win, s_sc, s_max, s_exp, s_tr, s_wT, s_av, s_sw,
         s_sr0, s_sr1, s_st1, s_srT, s_xo, s_o, s_oT, s_oTs, s_y, s_dve, s_ln, s_st) = (sc.sem(n) for n in (
             "x xT xTs pr prs ext tmp exts row rows win sc max exp tr wT av sw sr0 sr1 st1 srT xo o oT oTs y dve ln st").split())
        s_sr = (s_sr0, s_sr1)
        s_win2 = sc.sem("win2")
        s_bw = [sc.sem(f"bw{i}") for i in range(4)]
        proj = [(dst, w, i) for dst, w in ((qT, qwT), (kT, kwT)) for i in range(BLK // 2)]
        exts = [("q", 0, 0), ("q", 0, 1)] + [("k", t, i) for t in range(NT) for i in range(BLK // 2)]
        with nc.Fori(0, NB) as b:
            L.asked = 0
            with nc.Block() as block:
                @block.sync
                def _(sp):
                    sp.dma_start(x[:, :, :], rows(x_in, b)).then_inc(s_x, 16)
                    for n in range(2 * H):
                        h, dst = n // 2, (eq, ek)[n % 2]
                        sp.wait_ge(s_rows, n + 1)
                        sp.dma_start(dst[h, :, :].rearrange("(t p) n -> p t n", p=P), er[:, n % 4, :, :]).then_inc(s_bw[n % 4], 16)
                    for slot in range(4):
                        sp.wait_ge(s_bw[slot], 16 * H * 2 // 4)

                    def load_windows(half):
                        for src, dst in ((eq, bq), (ek, bk)):
                            for g in range(NG):
                                lo, hi, _ = window(g)
                                p0 = GR * (g % 4)
                                sp.dma_start(dst[p0:p0 + GR, g // 4, :, lo:hi], skewed(src, g, 8 * half, 8))\
                                  .then_inc((s_win, s_win2)[half], 16)

                    load_windows(0)
                    for h in range(H):
                        if h == 7:
                            sp.wait_ge(s_max, 8)
                            load_windows(1)
                        sp.wait_ge(s_exp, h + 1)
                        for g in range(NG):
                            lo, hi, _ = window(g)
                            p0 = GR * (g % 4)
                            sp.dma_start(skewed(es, g, h, 1), E[p0:p0 + GR, h % 3, g // 4:g // 4 + 1, lo:hi]).then_inc(s_sw, 16)
                        sp.wait_ge(s_sw, 16 * NG * (h + 1))
                        if h >= 2:
                            sp.wait_ge(s_st1, h - 1)
                        sp.dma_start(sr[:, h % 2, :, :], es[h, :, :].rearrange("(t p) n -> p t n", p=P)).then_inc(s_sr[h % 2], 16)
                    sp.wait_ge(s_ln, 1)
                    sp.dma_start(rows(x_out, b), y[:, :, :]).then_inc(s_st, 16)
                    sp.wait_ge(s_st, 16)

                @block.gpsimd
                def _(pool):
                    norm_powers(nc, pool, L, range(NT))

                @block.tensor
                def _(pe):
                    pe.wait_ge(s_x, 16)
                    for c in range(DC):
                        for t in range(NT):
                            ins = nc.tensor.transpose(banks[0][:, c * S + t * P:c * S + (t + 1) * P],
                                                      x[:, t, c * P:(c + 1) * P], ident[:, :])
                    ins.then_inc(s_xT, 1)
                    pe.wait_ge(s_xTs, 1)
                    for t in range(NT):
                        for c in range(DC):
                            ins = nc.tensor.matmul(banks[2][:, t * D:(t + 1) * D], xT[:, c, t * P:(t + 1) * P], vwT[:, c, :],
                                                   start=(c == 0), stop=(c == DC - 1))
                    ins.then_inc(s_pr, 1)
                    for n, (dst, w, i) in enumerate(proj):
                        if n >= 2:
                            pe.wait_ge(s_prs, n)
                        for k in range(2):
                            blk = 2 * i + k
                            for c in range(DC):
                                ins = nc.tensor.matmul(banks[3 + n % 2][:, k * S:(k + 1) * S], w[:, c, blk * P:(blk + 1) * P],
                                                       xT[:, c, :], start=(c == 0), stop=(c == DC - 1))
                        ins.then_inc(s_pr, 1)
                    pe.wait_ge(s_prs, 1 + len(proj))
                    for n in range(2 * H):
                        h, src, table = n // 2, (qT, kT)[n % 2], (tqx, tkx)[n % 2]
                        a, blk = h % 4, h // 4
                        if n >= 2:
                            pe.wait_ge(s_rows, n - 1)
                        for t in range(NT):
                            ins = nc.tensor.matmul(banks[5 + n % 2][:, t * BW:(t + 1) * BW], src[32 * a:32 * a + DK, blk, t * P:(t + 1) * P],
                                                   table[32 * a:32 * a + DK, blk, :], start=True, stop=True)
                        ins.then_inc(s_row, 1)
                    for n, (side, t, i) in enumerate(exts):
                        if n >= 2:
                            pe.wait_ge(s_tmp, n - 1)
                        for k in range(2):
                            blk = 2 * i + k
                            if side == "q":
                                for tt in range(NT):
                                    ins = nc.tensor.matmul(banks[n % 2][:, k * S + tt * P:k * S + (tt + 1) * P], extq[:, tt, blk, :],
                                                           qT[:, blk, tt * P:(tt + 1) * P], start=True, stop=True)
                            else:
                                ins = nc.tensor.matmul(banks[n % 2][:, k * S:(k + 1) * S], extk[:, t, blk, :], kT[:, blk, :],
                                                       start=True, stop=True)
                        ins.then_inc(s_ext, 1)
                    pe.wait_ge(s_exts, len(exts))
                    pe.wait_ge(s_rows, 2 * H)
                    for n in range(H + 3):
                        if n < H:
                            pe.wait_ge((s_win, s_win2)[n // 8], 16 * 2 * NG)
                            if n >= 2:
                                pe.wait_ge(s_max, n - 1)
                            a, blk = n % 4, n // 4
                            for t in range(NT):
                                o = banks[n % 2][:, t * S:(t + 1) * S]
                                nc.tensor.matmul(o, qE[32 * a:32 * a + 32, blk, t, :], kE[32 * a:32 * a + 32, blk, t, :],
                                                 start=True, stop=False)
                                for jt in range(NT):
                                    ins = nc.tensor.matmul(o[:, jt * P:(jt + 1) * P], bk[:, jt, n % 8, t * P:(t + 1) * P], ident[:, :],
                                                           start=False, stop=(jt == NT - 1))
                            ins.then_inc(s_sc, 1)
                        if 1 <= n <= H:
                            m = n - 1
                            pe.wait_ge(s_exp, m + 1)
                            if m >= 2:
                                pe.wait_ge(s_wT, m - 1)
                            for jt in range(NT):
                                for t in range(NT):
                                    ins = nc.tensor.transpose(banks[2 + m % 2][:, jt * S + t * P:jt * S + (t + 1) * P],
                                                              E[:, m % 3, t, jt * P:(jt + 1) * P], ident[:, :])
                            ins.then_inc(s_tr, 1)
                        if 2 <= n <= H + 1:
                            m = n - 2
                            pe.wait_ge(s_wT, m + 1)
                            for t in range(NT):
                                for jt in range(NT):
                                    ins = nc.tensor.matmul(banks[4 + t][:, m * 32:(m + 1) * 32], wT[:, m % 2, jt, t * P:(t + 1) * P],
                                                           vx[:, jt, m, :], start=(jt == 0), stop=(jt == NT - 1))
                            ins.then_inc(s_av, 1)
                        if n >= 3:
                            m = n - 3
                            pe.wait_ge(s_sr[m % 2], 16 * (m // 2 + 1))
                            if m >= 1:
                                pe.wait_ge(s_srT, m)
                            for t in range(NT):
                                ins = nc.tensor.transpose(banks[6][:, t * P:(t + 1) * P], sr[:, m % 2, t, :], ident[:, :])
                            ins.then_inc(s_st1, 1)
                            pe.wait_ge(s_srT, m + 1)
                            for t in range(NT):
                                ins = nc.tensor.matmul(banks[7][:, t * D + m * DK:t * D + (m + 1) * DK], srT[:, m % 2, t * P:(t + 1) * P],
                                                       rvx[:, m, :], start=True, stop=True)
                            ins.then_inc(s_xo, 1)
                    pe.wait_ge(s_o, 1)
                    for c in range(DC):
                        for t in range(NT):
                            ins = nc.tensor.transpose(banks[0][:, c * S + t * P:c * S + (t + 1) * P],
                                                      o_sb[:, t, c * P:(c + 1) * P], ident[:, :])
                    ins.then_inc(s_oT, 1)
                    pe.wait_ge(s_oTs, 1)
                    for t in range(NT):
                        o = banks[1][:, t * D:(t + 1) * D]
                        for c in range(DC):
                            nc.tensor.matmul(o, oT[:, c, t * P:(t + 1) * P], pwT[:, c, :], start=(c == 0), stop=False)
                        ins = nc.tensor.matmul(o, ones[0:1, :], pb[0:1, :], start=False, stop=True)
                    ins.then_inc(s_y, 1)

                @block.scalar
                def _(act):
                    for n in range(2 * H):
                        act.wait_ge(s_row, n + 1)
                        if n >= 4:
                            act.wait_ge(s_bw[n % 4], 16 * (n // 4))
                        nc.scalar.copy(er[:, n % 4, :, :], banks[5 + n % 2][:, 0:NT * BW].rearrange("p (t n) -> p t n", t=NT))\
                            .then_inc(s_rows, 1)
                    for n in range(H):
                        act.wait_ge(s_max, n + 1)
                        for t in range(NT):
                            ins = nc.scalar.activation(E[:, n % 3, t, :], E[:, n % 3, t, :], ACT.Exp, bias=top[:, n, t:t + 1],
                                                       scale=1.0, accum_out=sums[:, n, t:t + 1])
                        ins.then_inc(s_exp, 1)

                @block.vector
                def _(dve):
                    link = Chain(dve, s_dve)
                    dve.wait_ge(s_xT, 1)
                    nc.vector.tensor_copy(xT[:, :, :], banks[0][:, :].rearrange("p (c s) -> p c s", c=DC)).then_inc(s_xTs, 1)
                    dve.wait_ge(s_pr, 1)
                    for t in range(NT):
                        ins = nc.vector.tensor_copy(vx[:, t, :, 0:DK], banks[2][:, t * D:(t + 1) * D].rearrange("p (h d) -> p h d", h=H))
                    ins.then_inc(s_prs, 1)
                    for n, (dst, w, i) in enumerate(proj):
                        dve.wait_ge(s_pr, n + 2)
                        out, bank = dst[:, 2 * i:2 * i + 2, :], banks[3 + n % 2][:, :].rearrange("p (k s) -> p k s", k=2)
                        if dst is qT:
                            nc.vector.tensor_scalar(out, bank, DK ** -0.5, None, ALU.mult).then_inc(s_prs, 1)
                        else:
                            nc.vector.tensor_copy(out, bank).then_inc(s_prs, 1)
                    for n, (side, t, i) in enumerate(exts):
                        dve.wait_ge(s_ext, n + 1)
                        half = tmp[:, n % 2, :].rearrange("p (k s) -> p k s", k=2)
                        if side == "q":
                            mask, add = (m[:, :, :].rearrange("p t s -> p (t s)") for m in (qmask, qadd))
                            dst = qE[:, 2 * i:2 * i + 2, :, :].rearrange("p k t s -> p k (t s)")
                        else:
                            mask, add = kmask[:, t, :], kadd[:, t, :]
                            dst = kE[:, 2 * i:2 * i + 2, t, :]
                        nc.vector.tensor_tensor(half, banks[n % 2][:, :].rearrange("p (k s) -> p k s", k=2),
                                                mask.unsqueeze(1).broadcast_to([P, 2, S]), ALU.mult).then_inc(s_tmp, 1)
                        dve.wait_ge(s_tmp, n + 1)
                        nc.vector.tensor_tensor(dst, half, add.unsqueeze(1).broadcast_to([P, 2, S]), ALU.add).then_inc(s_exts, 1)

                    def sum_rows(m):
                        dve.wait_ge(s_st1, m + 1)
                        if m >= 2:
                            dve.wait_ge(s_xo, m - 1)
                        nc.vector.tensor_copy(srT[:, m % 2, :], banks[6][:, 0:S]).then_inc(s_srT, 1)

                    for n in range(H + 3):
                        if n < H:
                            dve.wait_ge(s_sc, n + 1)
                            dve.wait_ge((s_win, s_win2)[n // 8], 16 * 2 * NG)
                            if n >= 3:
                                dve.wait_ge(s_tr, n - 2)
                                dve.wait_ge(s_sw, 16 * NG * (n - 2))
                            for t in range(NT):
                                ins = nc.vector.tensor_tensor_reduce(
                                    out=E[:, n % 3, t, :], in0=banks[n % 2][:, t * S:(t + 1) * S], in1=bq[:, t, n % 8, :],
                                    scale=1.0, scalar=-3.0e38, op0=ALU.add, op1=ALU.max, accum_out=top[:, n, t:t + 1])
                            link(ins)
                            nc.vector.tensor_scalar(top[:, n, :], top[:, n, :], -1.0, None, ALU.mult).then_inc(s_max, 1)
                        if 1 <= n <= H:
                            m = n - 1
                            dve.wait_ge(s_tr, m + 1)
                            if m >= 2:
                                dve.wait_ge(s_av, m - 1)
                            nc.vector.tensor_copy(wT[:, m % 2, :, :], banks[2 + m % 2][:, :].rearrange("p (j k) -> p j k", j=NT))\
                                .then_inc(s_wT, 1)
                        if n >= 3:
                            sum_rows(n - 3)
                    dve.wait_ge(s_exp, H)
                    link(nc.vector.reciprocal(rs[:, :, :], sums[:, :, :]))
                    dve.wait_ge(s_av, H)
                    dve.wait_ge(s_xo, H)
                    v3 = lambda ap: ap.rearrange("p (h d) -> p h d", h=H)
                    for t in range(NT):
                        heads = banks[4 + t][:, :].rearrange("p (h k) -> p h k", h=H)
                        link(nc.vector.tensor_tensor(outside[:, t, :, :], heads[:, :, 16:32],
                                                     own[:, t, :].unsqueeze(1).broadcast_to([P, H, 16]), ALU.mult))
                        link(nc.vector.tensor_reduce(pair[:, t, :, :], outside[:, t, :, :].rearrange("p h (e g) -> p h e g", e=2),
                                                     AX.X, ALU.add))
                        link(nc.vector.tensor_copy(v3(o_sb[:, t, :]), heads[:, :, 0:DK]))
                        link(nc.vector.tensor_tensor(o_sb[:, t, :], o_sb[:, t, :], banks[7][:, t * D:(t + 1) * D], ALU.add))
                        for e in range(2):
                            link(nc.vector.tensor_tensor(outside[:, t, :, :], rve[:, e, :, :],
                                                         pair[:, t, :, e:e + 1].broadcast_to([P, H, DK]), ALU.mult))
                            link(nc.vector.tensor_tensor(v3(o_sb[:, t, :]), v3(o_sb[:, t, :]), outside[:, t, :, :], ALU.add))
                        ins = nc.vector.tensor_tensor(v3(o_sb[:, t, :]), v3(o_sb[:, t, :]),
                                                      rs[:, :, t:t + 1].broadcast_to([P, H, DK]), ALU.mult)
                    ins.then_inc(s_o, 1)
                    dve.wait_ge(s_oT, 1)
                    nc.vector.tensor_copy(oT[:, :, :], banks[0][:, :].rearrange("p (c s) -> p c s", c=DC)).then_inc(s_oTs, 1)
                    dve.wait_ge(s_y, 1)
                    for t in range(NT):
                        link(nc.vector.tensor_tensor(x[:, t, :], x[:, t, :], banks[1][:, t * D:(t + 1) * D], ALU.add))
                        layer_norm(nc, dve, link, x[:, t, :], y[:, t, :], L, t)
                    nc.vector.engine_nop().then_inc(s_ln, 1)
            sc.clear()


def cross_attention_1(nc, x_in, x_out, W):
    DH, LAMBDA_INIT = D // H, 0.8
    HQ = 2 * DH
    BLK = H // 4
    with stage(nc, "xa1") as sc:
        ident = sc.sb("ident", [P, P])
        make_identity(nc, sc, ident)
        qw, kw = sc.sb("qw", [P, DC, 2 * H * 32]), sc.sb("kw", [P, DC, 2 * H * 32])
        vw, ow = sc.sb("vw", [P, DC, D]), sc.sb("ow", [P, DC, D])
        lam_in = sc.sb("lambda_in", [P, 4, H, DH])
        rms_w = sc.sb("rms_scale", [P, DH])
        loads = []
        for dst, src in ((qw, W["L1_xattn_W_q"]), (kw, W["L1_xattn_W_k"])):
            for part in range(2):
                loads += padded_heads(dst[:, :, part * H * 32:(part + 1) * H * 32], src, H, HQ, part * DH, DH, 32)
        loads += [(vw[:, :, :], W["L1_xattn_W_v"].rearrange("(c p) n -> p c n", p=P)),
                  (ow[:, :, :], W["L1_xattn_W_o"].rearrange("(c p) n -> p c n", p=P)),
                  (rms_w[:, :], W["L1_xattn_rms_scale"].rearrange("(a d) -> a d", a=1).broadcast_to([P, DH]))]
        for i, name in enumerate(("lambda_q1", "lambda_k1", "lambda_q2", "lambda_k2")):
            loads.append((lam_in[:, i, :, :].rearrange("p h d -> p (h d)"),
                          W["L1_xattn_" + name].rearrange("(a h) d -> a (h d)", a=1).broadcast_to([P, H * DH])))
        load_weights(nc, sc, ident, [qw[:, :, :], kw[:, :, :]], loads, [])
        prod, dots = sc.sb("lambda_prod", [P, 2, H, DH]), sc.sb("lambda_dot", [P, 2, H])
        neglam = sc.sb("neg_lambda", [P, H])
        s_dots, s_elam, s_lam = sc.sem("dots"), sc.sem("elam"), sc.sem("lam")
        with nc.Block() as block:
            @block.scalar
            def _(act):
                act.wait_ge(s_dots, 1)
                nc.scalar.activation(dots[:, :, :], dots[:, :, :], ACT.Exp).then_inc(s_elam, 1)

            @block.vector
            def _(dve):
                link = Chain(dve, s_lam)
                for i in range(2):
                    ins = nc.vector.tensor_tensor(prod[:, i, :, :], lam_in[:, 2 * i, :, :], lam_in[:, 2 * i + 1, :, :], ALU.mult)
                link(ins)
                nc.vector.tensor_reduce(dots[:, :, :], prod[:, :, :, :], AX.X, ALU.add).then_inc(s_dots, 1)
                dve.wait_ge(s_elam, 1)
                link(nc.vector.tensor_tensor(neglam[:, :], dots[:, 1, :], dots[:, 0, :], ALU.subtract))
                link(nc.vector.tensor_scalar(neglam[:, :], neglam[:, :], -LAMBDA_INIT, None, ALU.add))
                link(nc.vector.tensor_scalar(rms_w[:, :], rms_w[:, :], 1.0 - LAMBDA_INIT, None, ALU.mult))
        x, cx, y = sc.sb("x", [P, NT, D]), sc.sb("ctx", [P, NT, D]), sc.sb("y", [P, NT, D])
        xT, cT, v = sc.sb("xT", [P, DC, S]), sc.sb("ctxT", [P, DC, S]), sc.sb("v", [P, NT, D])
        qT, kT = sc.sb("qT", [P, 2 * BLK, S]), sc.sb("kT", [P, 2 * BLK, S])
        MR = 3
        mask = sc.sb("mask", [P, MR, NT, S])
        E = sc.sb("E", [P, 3, 2, NT, S])
        wd, wT = sc.sb("w", [P, 2, NT, S]), sc.sb("wT", [P, 2, NT, S])
        top, sums = sc.sb("max", [P, H, 2, NT]), sc.sb("sums", [P, H, 2, NT])
        ratio = sc.sb("ratio", [P, H, NT])
        r1 = sc.sb("r1", [P, H, NT])
        o_sb, sq, oT = sc.sb("o", [P, NT, D]), sc.sb("sq", [P, NT, D]), sc.sb("oT", [P, DC, S])
        ms, rr, pw = sc.sb("ms", [P, NT, H]), sc.sb("rr", [P, NT, H]), sc.sb("pw", [P, NT, H])
        banks = [sc.ps(f"bank{i}") for i in range(8)]
        L = NormTiles(sc)
        (s_x, s_mask0, s_mask1, s_mask2, s_xT, s_xTs, s_pr, s_prs, s_sc, s_max, s_exp, s_w, s_tr, s_wT, s_av, s_ms, s_rr, s_pw, s_o, s_oT, s_oTs,
         s_y, s_dve, s_ln, s_st) = (sc.sem(n) for n in (
             "x mask0 mask1 mask2 xT xTs pr prs sc max exp w tr wT av ms rr pw o oT oTs y dve ln st").split())
        s_mask = (s_mask0, s_mask1, s_mask2)
        steps = [(dst, w, src, i) for dst, w, src in ((qT, qw, xT), (kT, kw, cT)) for i in range(BLK)]
        with nc.Fori(0, NB) as b:
            L.asked = 0
            with nc.Block() as block:
                @block.sync
                def _(sp):
                    sp.dma_start(x[:, :, :], rows(x_in, b)).then_inc(s_x, 16)
                    sp.dma_start(cx[:, :, :], rows(W["ctx_1024"], b)).then_inc(s_x, 16)
                    for h in range(H):
                        if h >= MR:
                            sp.wait_ge(s_max, h - MR + 1)
                        sp.dma_start(mask[:, h % MR, :, :],
                                     W["mask_Bx16xSxS2_ff0"][b, h, :, :].rearrange("(t p) k -> p t k", p=P))\
                          .then_inc(s_mask[h % MR], 16)
                    sp.wait_ge(s_ln, 1)
                    sp.dma_start(rows(x_out, b), y[:, :, :]).then_inc(s_st, 16)
                    sp.wait_ge(s_st, 16)

                @block.gpsimd
                def _(pool):
                    nc.gpsimd.memset(pw[:, :, :], -0.5).then_inc(s_pw, 1)
                    pool.wait_ge(s_pw, 1)
                    pool.wait_ge(s_ms, 1)
                    nc.gpsimd.tensor_tensor(rr[:, :, :], ms[:, :, :], pw[:, :, :], ALU.pow).then_inc(s_rr, 1)
                    norm_powers(nc, pool, L, range(NT))

                @block.tensor
                def _(pe):
                    pe.wait_ge(s_x, 32)
                    for n, src in enumerate((x, cx)):
                        for c in range(DC):
                            for t in range(NT):
                                ins = nc.tensor.transpose(banks[n][:, c * S + t * P:c * S + (t + 1) * P],
                                                          src[:, t, c * P:(c + 1) * P], ident[:, :])
                        ins.then_inc(s_xT, 1)
                    pe.wait_ge(s_xTs, 2)
                    for t in range(NT):
                        for c in range(DC):
                            ins = nc.tensor.matmul(banks[2][:, t * D:(t + 1) * D], cT[:, c, t * P:(t + 1) * P], vw[:, c, :],
                                                   start=(c == 0), stop=(c == DC - 1))
                    ins.then_inc(s_pr, 1)
                    for n, (dst, w, src, i) in enumerate(steps):
                        if n >= 2:
                            pe.wait_ge(s_prs, n)
                        for k in range(2):
                            blk = 2 * i + k
                            for c in range(DC):
                                ins = nc.tensor.matmul(banks[3 + n % 2][:, k * S:(k + 1) * S], w[:, c, blk * P:(blk + 1) * P],
                                                       src[:, c, :], start=(c == 0), stop=(c == DC - 1))
                        ins.then_inc(s_pr, 1)
                    pe.wait_ge(s_prs, 1 + len(steps))
                    for n in range(H + 2):
                        if n < H:
                            if n >= 2:
                                pe.wait_ge(s_max, n - 1)
                            a = n % 4
                            for j in range(2):
                                blk = j * BLK + n // 4
                                for t in range(NT):
                                    ins = nc.tensor.matmul(banks[2 * (n % 2) + j][:, t * S:(t + 1) * S],
                                                           qT[32 * a:32 * a + DH, blk, t * P:(t + 1) * P],
                                                           kT[32 * a:32 * a + DH, blk, :], start=True, stop=True)
                            ins.then_inc(s_sc, 1)
                        if 1 <= n <= H:
                            m = n - 1
                            pe.wait_ge(s_w, m + 1)
                            if m >= 2:
                                pe.wait_ge(s_wT, m - 1)
                            for jt in range(NT):
                                for t in range(NT):
                                    ins = nc.tensor.transpose(banks[4 + m % 2][:, jt * S + t * P:jt * S + (t + 1) * P],
                                                              wd[:, m % 2, t, jt * P:(jt + 1) * P], ident[:, :])
                            ins.then_inc(s_tr, 1)
                        if n >= 2:
                            m = n - 2
                            pe.wait_ge(s_wT, m + 1)
                            for t in range(NT):
                                for jt in range(NT):
                                    ins = nc.tensor.matmul(banks[6][:, t * D + m * DH:t * D + (m + 1) * DH],
                                                           wT[:, m % 2, jt, t * P:(t + 1) * P], v[:, jt, m * DH:(m + 1) * DH],
                                                           start=(jt == 0), stop=(jt == NT - 1))
                            ins.then_inc(s_av, 1)
                    pe.wait_ge(s_o, 1)
                    for c in range(DC):
                        for t in range(NT):
                            ins = nc.tensor.transpose(banks[0][:, c * S + t * P:c * S + (t + 1) * P],
                                                      o_sb[:, t, c * P:(c + 1) * P], ident[:, :])
                    ins.then_inc(s_oT, 1)
                    pe.wait_ge(s_oTs, 1)
                    for t in range(NT):
                        for c in range(DC):
                            ins = nc.tensor.matmul(banks[7][:, t * D:(t + 1) * D], oT[:, c, t * P:(t + 1) * P],
                                                   ow[:, c, :], start=(c == 0), stop=(c == DC - 1))
                    ins.then_inc(s_y, 1)

                @block.scalar
                def _(act):
                    for n in range(H + 1):
                        if n < H:
                            act.wait_ge(s_max, n + 1)
                            for j in range(2):
                                for t in range(NT):
                                    ins = nc.scalar.activation(E[:, n % 3, j, t, :], E[:, n % 3, j, t, :], ACT.Exp,
                                                               bias=top[:, n, j, t:t + 1], scale=1.0,
                                                               accum_out=sums[:, n, j, t:t + 1])
                            ins.then_inc(s_exp, 1)
                        if n >= 1:
                            m = n - 1
                            act.wait_ge(s_tr, m + 1)
                            if m >= 2:
                                act.wait_ge(s_av, m - 1)
                            nc.scalar.copy(wT[:, m % 2, :, :], banks[4 + m % 2][:, :].rearrange("p (j k) -> p j k", j=NT))\
                                .then_inc(s_wT, 1)

                @block.vector
                def _(dve):
                    link = Chain(dve, s_dve)
                    for n, dst in enumerate((xT, cT)):
                        dve.wait_ge(s_xT, n + 1)
                        nc.vector.tensor_copy(dst[:, :, :], banks[n][:, :].rearrange("p (c s) -> p c s", c=DC)).then_inc(s_xTs, 1)
                    dve.wait_ge(s_pr, 1)
                    nc.vector.tensor_copy(v[:, :, :], banks[2][:, :].rearrange("p (t n) -> p t n", t=NT)).then_inc(s_prs, 1)
                    for n, (dst, w, src, i) in enumerate(steps):
                        dve.wait_ge(s_pr, n + 2)
                        out, bank = dst[:, 2 * i:2 * i + 2, :], banks[3 + n % 2][:, :].rearrange("p (k s) -> p k s", k=2)
                        if dst is qT:
                            nc.vector.tensor_scalar(out, bank, DH ** -0.5, None, ALU.mult).then_inc(s_prs, 1)
                        else:
                            nc.vector.tensor_copy(out, bank).then_inc(s_prs, 1)

                    def combine(m):
                        dve.wait_ge(s_exp, m + 1)
                        link(nc.vector.reciprocal(ratio[:, m, :], sums[:, m, 1, :]))
                        link(nc.vector.scalar_tensor_tensor(ratio[:, m, :], ratio[:, m, :], neglam[:, m:m + 1],
                                                            sums[:, m, 0, :], ALU.mult, ALU.mult))
                        if m >= 2:
                            dve.wait_ge(s_tr, m - 1)
                        for t in range(NT):
                            ins = nc.vector.scalar_tensor_tensor(wd[:, m % 2, t, :], E[:, m % 3, 1, t, :], ratio[:, m, t:t + 1],
                                                                 E[:, m % 3, 0, t, :], ALU.mult, ALU.add)
                        ins.then_inc(s_w, 1)

                    for n in range(H + 1):
                        if n < H:
                            dve.wait_ge(s_sc, n + 1)
                            dve.wait_ge(s_mask[n % MR], 16 * (n // MR + 1))
                            if n >= 3:
                                dve.wait_ge(s_w, n - 2)
                            for j in range(2):
                                for t in range(NT):
                                    ins = nc.vector.tensor_tensor_reduce(
                                        out=E[:, n % 3, j, t, :], in0=banks[2 * (n % 2) + j][:, t * S:(t + 1) * S],
                                        in1=mask[:, n % MR, t, :], scale=1.0, scalar=-3.0e38, op0=ALU.add, op1=ALU.max,
                                        accum_out=top[:, n, j, t:t + 1])
                            link(ins)
                            nc.vector.tensor_scalar(top[:, n, :, :], top[:, n, :, :], -1.0, None, ALU.mult).then_inc(s_max, 1)
                        if n >= 1:
                            combine(n - 1)
                    link(nc.vector.reciprocal(r1[:, :, :], sums[:, :, 0, :]))
                    dve.wait_ge(s_av, H)
                    v4 = lambda ap: ap.rearrange("p (h d) -> p h d", h=H)
                    for t in range(NT):
                        link(nc.vector.tensor_tensor(v4(o_sb[:, t, :]), v4(banks[6][:, t * D:(t + 1) * D]),
                                                     r1[:, :, t:t + 1].broadcast_to([P, H, DH]), ALU.mult))
                    link(nc.vector.tensor_tensor(sq[:, :, :], o_sb[:, :, :], o_sb[:, :, :], ALU.mult))
                    for t in range(NT):
                        ins = nc.vector.tensor_reduce(ms[:, t, :], v4(sq[:, t, :]), AX.X, ALU.add)
                    link(ins)
                    nc.vector.tensor_scalar(ms[:, :, :], ms[:, :, :], 1.0 / DH, EPS, ALU.mult, ALU.add).then_inc(s_ms, 1)
                    for t in range(NT):
                        ins = nc.vector.tensor_tensor(v4(o_sb[:, t, :]), v4(o_sb[:, t, :]),
                                                      rms_w[:, :].unsqueeze(1).broadcast_to([P, H, DH]), ALU.mult)
                    link(ins)
                    dve.wait_ge(s_rr, 1)
                    for t in range(NT):
                        ins = nc.vector.tensor_tensor(v4(o_sb[:, t, :]), v4(o_sb[:, t, :]),
                                                      rr[:, t, :].unsqueeze(2).broadcast_to([P, H, DH]), ALU.mult)
                    ins.then_inc(s_o, 1)
                    dve.wait_ge(s_oT, 1)
                    nc.vector.tensor_copy(oT[:, :, :], banks[0][:, :].rearrange("p (c s) -> p c s", c=DC)).then_inc(s_oTs, 1)
                    dve.wait_ge(s_y, 1)
                    for t in range(NT):
                        link(nc.vector.tensor_tensor(x[:, t, :], x[:, t, :], banks[7][:, t * D:(t + 1) * D], ALU.add))
                        layer_norm(nc, dve, link, x[:, t, :], y[:, t, :], L, t)
                    nc.vector.engine_nop().then_inc(s_ln, 1)
            sc.clear()


def padded_heads(dst, src, heads, width, at, keep, stride):
    return [(dst[:, c, :].rearrange("p (h k) -> p h k", k=stride)[:, 0:heads, 0:keep],
             src[c * P:(c + 1) * P, :].rearrange("p (h w) -> p h w", w=width)[:, 0:heads, at:at + keep]) for c in range(DC)]


def ffn_1(nc, x_in, x_out, W):
    E, LAT, F = 8, D // 2, 2 * D
    KPH, HD, FC = LAT // H, D // H, F // P
    with stage(nc, "ff1") as sc:
        ident = sc.sb("ident", [P, P])
        make_identity(nc, sc, ident)
        qw, kw = sc.sb("qw", [P, DC, H * 32]), sc.sb("kw", [P, DC, H * 32])
        qb, kb = sc.sb("qb", [1, H * 32]), sc.sb("kb", [1, H * 32])
        vw, vb = sc.sb("vw", [P, DC, LAT]), sc.sb("vb", [1, LAT])
        ow, ob = sc.sb("ow", [P, D]), sc.sb("ob", [1, D])
        rw, rb = sc.sb("rw", [P, DC, E]), sc.sb("rb", [1, E])
        w1, w2 = sc.sb("w1", [P, E, DC, F]), sc.sb("w2", [P, E, FC, D])
        b1r, b1T, b2 = sc.sb("b1r", [E * FC, P]), sc.sb("b1T", [P, E * FC]), sc.sb("b2", [E, D])
        loads = padded_heads(qw, W["L1_ffn_q_w"], H, HD, 0, KPH, 32) + padded_heads(kw, W["L1_ffn_k_w"], H, KPH, 0, KPH, 32)
        loads += [(qb[:, :].rearrange("p (h k) -> p h k", k=32)[:, :, 0:KPH], W["L1_ffn_q_b"].rearrange("(a h w) -> a h w", a=1, w=HD)[:, :, 0:KPH]),
                  (kb[:, :].rearrange("p (h k) -> p h k", k=32)[:, :, 0:KPH], W["L1_ffn_k_b"].rearrange("(a h w) -> a h w", a=1, w=KPH)),
                  (vw[:, :, :], W["L1_ffn_v_w"].rearrange("(c p) n -> p c n", p=P)),
                  (vb[:, :], W["L1_ffn_v_b"].rearrange("(a n) -> a n", a=1)),
                  (ow[:, :], W["L1_ffn_o_w"][0:LAT, :]), (ob[:, :], W["L1_ffn_o_b"].rearrange("(a n) -> a n", a=1)),
                  (rw[:, :, :], W["L1_ffn_router_w"].rearrange("(c p) n -> p c n", p=P)),
                  (rb[:, :], W["L1_ffn_router_b"].rearrange("(a n) -> a n", a=1)),
                  (b1r[:, :], W["L1_ffn_b1"].rearrange("e (c p) -> (e c) p", p=P)), (b2[:, :], W["L1_ffn_b2"])]
        for e in range(E):
            loads += [(w1[:, e, :, :], W["L1_ffn_w1"][e, :, :].rearrange("(c p) f -> p c f", p=P)),
                      (w2[:, e, :, :], W["L1_ffn_w2"][e, :, :].rearrange("(c p) d -> p c d", p=P))]
        load_weights(nc, sc, ident, [qw[:, :, :], kw[:, :, :], qb[:, :], kb[:, :]], loads, [(b1r[:, :], b1T[:, :])])
        iota, ones = sc.sb("iota", [P, E]), sc.sb("ones", [1, S])
        s_iota = sc.sem("iota")
        with nc.Block() as block:
            @block.gpsimd
            def _(pool):
                for e in range(E):
                    nc.gpsimd.memset(iota[:, e:e + 1], float(e)).then_inc(s_iota, 1)
                nc.gpsimd.memset(ones[:, :], 1.0).then_inc(s_iota, 1)
                pool.wait_ge(s_iota, E + 1)
        x, y, xT = sc.sb("x", [P, NT, D]), sc.sb("y", [P, NT, D]), sc.sb("xT", [P, DC, S])
        v = sc.sb("v", [P, NT, LAT])
        o_sb, oT, rs = sc.sb("o", [P, NT, LAT]), sc.sb("oT", [P, S]), sc.sb("rsums", [P, H, NT])
        mT = sc.sb("mlaT", [P, DC, S])
        pr, mx = sc.sb("probs", [P, NT, E]), sc.sb("top", [P, NT, 8])
        negl, suml = sc.sb("neg_logit", [P, NT]), sc.sb("sum_logit", [P, NT])
        ix, ixf = sc.sb("index", [P, NT, 8], U32), sc.sb("indexf", [P, NT, 2])
        oh, den = sc.sb("onehot", [P, NT, 2, E]), sc.sb("den", [P, NT])
        comb, cT = sc.sb("combine", [P, NT, E]), sc.sb("combineT", [E, S])
        h1, acc = sc.sb("h1", [P, 2, FC, S]), sc.sb("acc", [P, NT, D])
        banks = [sc.ps(f"bank{i}") for i in range(8)]
        A = AttentionTiles(sc, ident, H, KPH, KPH, banks[0:2], banks[2:4], banks[4])
        A.V = lambda jt, h: v[:, jt, h * KPH:(h + 1) * KPH]
        L = NormTiles(sc)
        (s_x, s_xT, s_xTs, s_qk, s_qkT, s_v, s_vs, s_o, s_oT, s_oTs, s_m, s_mT, s_lg, s_neg, s_pexp, s_comb, s_cT, s_cTs, s_b2,
         s_h1, s_g, s_h2, s_acc, s_dve, s_ln, s_st) = (sc.sem(n) for n in (
             "x xT xTs qk qkT v vs o oT oTs m mT lg neg pexp comb cT cTs b2 h1 g h2 acc dve ln st").split())
        with nc.Fori(0, NB) as b:
            L.asked = 0
            with nc.Block() as block:
                @block.sync
                def _(sp):
                    sp.dma_start(x[:, :, :], rows(x_in, b)).then_inc(s_x, 16)
                    sp.wait_ge(s_ln, 1)
                    sp.dma_start(rows(x_out, b), y[:, :, :]).then_inc(s_st, 16)
                    sp.wait_ge(s_st, 16)

                @block.gpsimd
                def _(pool):
                    norm_powers(nc, pool, L, range(NT))

                @block.tensor
                def _(pe):
                    pe.wait_ge(s_x, 16)
                    for c in range(DC):
                        for t in range(NT):
                            ins = nc.tensor.transpose(banks[5][:, c * S + t * P:c * S + (t + 1) * P],
                                                      x[:, t, c * P:(c + 1) * P], ident[:, :])
                    ins.then_inc(s_xT, 1)
                    pe.wait_ge(s_xTs, 1)
                    for t in range(NT):
                        o = banks[7][:, t * LAT:(t + 1) * LAT]
                        for c in range(DC):
                            nc.tensor.matmul(o, xT[:, c, t * P:(t + 1) * P], vw[:, c, :], start=(c == 0), stop=False)
                        ins = nc.tensor.matmul(o, ones[0:1, 0:P], vb[0:1, :], start=False, stop=True)
                    ins.then_inc(s_v, 1)
                    n = 0
                    for w, bias in ((qw, qb), (kw, kb)):
                        for half in range(2):
                            if n >= 2:
                                pe.wait_ge(s_qkT, n - 1)
                            for k in range(2):
                                blk = 2 * half + k
                                o = banks[5 + n % 2][:, k * S:(k + 1) * S]
                                for c in range(DC):
                                    nc.tensor.matmul(o, w[:, c, blk * P:(blk + 1) * P], xT[:, c, :], start=(c == 0), stop=False)
                                ins = nc.tensor.matmul(o, bias[0:1, blk * P:(blk + 1) * P], ones[0:1, :], start=False, stop=True)
                            ins.then_inc(s_qk, 1)
                            n += 1
                    pe.wait_ge(s_qkT, 4)
                    pe.wait_ge(s_vs, 1)
                    attend(nc, A, pe=pe)
                    pe.wait_ge(s_o, 1)
                    for t in range(NT):
                        ins = nc.tensor.transpose(banks[5][:, t * P:(t + 1) * P], o_sb[:, t, :], ident[:, :])
                    ins.then_inc(s_oT, 1)
                    pe.wait_ge(s_oTs, 1)
                    for c in range(DC):
                        o = banks[6][:, c * S:(c + 1) * S]
                        nc.tensor.matmul(o, ow[:, c * P:(c + 1) * P], oT[:, :], start=True, stop=False)
                        ins = nc.tensor.matmul(o, ob[0:1, c * P:(c + 1) * P], ones[0:1, :], start=False, stop=True)
                    ins.then_inc(s_m, 1)
                    pe.wait_ge(s_mT, 1)
                    for t in range(NT):
                        o = banks[7][:, t * E:(t + 1) * E]
                        for c in range(DC):
                            nc.tensor.matmul(o, mT[:, c, t * P:(t + 1) * P], rw[:, c, :], start=(c == 0), stop=False)
                        ins = nc.tensor.matmul(o, ones[0:1, 0:P], rb[0:1, :], start=False, stop=True)
                    ins.then_inc(s_lg, 1)
                    for e in range(E + 1):
                        if e < E:
                            for half in range(2):
                                n = 2 * e + half
                                if n >= 4:
                                    pe.wait_ge(s_g, 2 * (n - 3))
                                for k in range(2):
                                    f = 2 * half + k
                                    for c in range(DC):
                                        ins = nc.tensor.matmul(banks[n % 4][:, k * S:(k + 1) * S], w1[:, e, c, f * P:(f + 1) * P],
                                                               mT[:, c, :], start=(c == 0), stop=(c == DC - 1))
                                ins.then_inc(s_h1, 1)
                        if e == 2:
                            pe.wait_ge(s_comb, 1)
                            for t in range(NT):
                                ins = nc.tensor.transpose(banks[4][0:E, t * P:(t + 1) * P], comb[:, t, :], ident[:, :])
                            ins.then_inc(s_cT, 1)
                            pe.wait_ge(s_cTs, 1)
                            for t in range(NT):
                                ins = nc.tensor.matmul(banks[7][:, t * D:(t + 1) * D], cT[:, t * P:(t + 1) * P], b2[:, :],
                                                       start=True, stop=True)
                            ins.then_inc(s_b2, 1)
                        if e >= 1:
                            m = e - 1
                            pe.wait_ge(s_g, 4 * (m + 1))
                            if m >= 2:
                                pe.wait_ge(s_acc, m - 1)
                            for t in range(NT):
                                for f in range(FC):
                                    ins = nc.tensor.matmul(banks[5 + m % 2][:, t * D:(t + 1) * D], h1[:, m % 2, f, t * P:(t + 1) * P],
                                                           w2[:, m, f, :], start=(f == 0), stop=(f == FC - 1))
                            ins.then_inc(s_h2, 1)

                @block.scalar
                def _(act):
                    attend(nc, A, act=act)
                    act.wait_ge(s_neg, 1)
                    for t in range(NT):
                        ins = nc.scalar.activation(pr[:, t, :], banks[7][:, t * E:(t + 1) * E], ACT.Exp, bias=negl[:, t:t + 1],
                                                   scale=1.0, accum_out=suml[:, t:t + 1])
                    ins.then_inc(s_pexp, 1)
                    for e in range(E):
                        if e >= 2:
                            act.wait_ge(s_h2, e - 1)
                        for f in range(FC):
                            act.wait_ge(s_h1, 2 * e + f // 2 + 1)
                            nc.scalar.activation(h1[:, e % 2, f, :], banks[(2 * e + f // 2) % 4][:, (f % 2) * S:(f % 2 + 1) * S],
                                                 ACT.Gelu, bias=b1T[:, e * FC + f:e * FC + f + 1], scale=1.0).then_inc(s_g, 1)

                @block.vector
                def _(dve):
                    link = Chain(dve, s_dve)
                    dve.wait_ge(s_xT, 1)
                    nc.vector.tensor_copy(xT[:, :, :], banks[5][:, :].rearrange("p (c s) -> p c s", c=DC)).then_inc(s_xTs, 1)
                    dve.wait_ge(s_v, 1)
                    nc.vector.tensor_copy(v[:, :, :], banks[7][:, 0:NT * LAT].rearrange("p (t n) -> p t n", t=NT)).then_inc(s_vs, 1)
                    for n in range(4):
                        dve.wait_ge(s_qk, n + 1)
                        dst = (A.qT, A.kT)[n // 2][:, 2 * (n % 2):2 * (n % 2) + 2, :]
                        src = banks[5 + n % 2][:, :].rearrange("p (k s) -> p k s", k=2)
                        if n < 2:
                            nc.vector.tensor_scalar(dst, src, KPH ** -0.5, None, ALU.mult).then_inc(s_qkT, 1)
                        else:
                            nc.vector.tensor_copy(dst, src).then_inc(s_qkT, 1)
                    attend(nc, A, dve=dve)
                    dve.wait_ge(A.s_exp, H)
                    link(nc.vector.reciprocal(rs[:, :, :], A.sums[:, :, :]))
                    dve.wait_ge(A.s_av, H)
                    for t in range(NT):
                        ins = nc.vector.tensor_tensor(o_sb[:, t, :].rearrange("p (h d) -> p h d", h=H),
                                                      banks[4][:, t * LAT:(t + 1) * LAT].rearrange("p (h d) -> p h d", h=H),
                                                      rs[:, :, t:t + 1].broadcast_to([P, H, KPH]), ALU.mult)
                    ins.then_inc(s_o, 1)
                    dve.wait_ge(s_oT, 1)
                    nc.vector.tensor_copy(oT[:, :], banks[5][:, 0:S]).then_inc(s_oTs, 1)
                    dve.wait_ge(s_m, 1)
                    nc.vector.tensor_copy(mT[:, :, :], banks[6][:, :].rearrange("p (c s) -> p c s", c=DC)).then_inc(s_mT, 1)
                    dve.wait_ge(s_lg, 1)
                    nc.vector.tensor_reduce(negl[:, :], banks[7][:, 0:NT * E].rearrange("p (t e) -> p t e", t=NT),
                                            AX.X, ALU.max, negate=True).then_inc(s_neg, 1)
                    dve.wait_ge(s_pexp, 1)
                    link(nc.vector.reciprocal(suml[:, :], suml[:, :]))
                    for t in range(NT):
                        link(nc.vector.tensor_scalar(pr[:, t, :], pr[:, t, :], suml[:, t:t + 1], None, ALU.mult))
                        top2(nc, dve, link, pr, mx, ix, ixf, iota, oh, t, 1.0)
                        link(nc.vector.tensor_scalar(den[:, t:t + 1], mx[:, t, 0:1], mx[:, t, 1:2], 1e-8, ALU.add, ALU.add))
                        link(nc.vector.reciprocal(den[:, t:t + 1], den[:, t:t + 1]))
                        for k in range(2):
                            ins = nc.vector.tensor_scalar(oh[:, t, k, :], oh[:, t, k, :], mx[:, t, k:k + 1], den[:, t:t + 1],
                                                          ALU.mult, ALU.mult)
                        link(ins)
                    nc.vector.tensor_tensor(comb[:, :, :], oh[:, :, 0, :], oh[:, :, 1, :], ALU.add).then_inc(s_comb, 1)
                    dve.wait_ge(s_comb, 1)
                    dve.wait_ge(s_cT, 1)
                    nc.vector.tensor_copy(cT[:, :], banks[4][0:E, 0:S]).then_inc(s_cTs, 1)
                    dve.wait_ge(s_b2, 1)
                    link(nc.vector.tensor_copy(acc[:, :, :], banks[7][:, :].rearrange("p (t d) -> p t d", t=NT)))
                    for e in range(E):
                        dve.wait_ge(s_h2, e + 1)
                        for t in range(NT):
                            ins = nc.vector.scalar_tensor_tensor(acc[:, t, :], banks[5 + e % 2][:, t * D:(t + 1) * D],
                                                                 comb[:, t, e:e + 1], acc[:, t, :], ALU.mult, ALU.add)
                        ins.then_inc(s_acc, 1)
                        dve.wait_ge(s_acc, e + 1)
                    for t in range(NT):
                        link(nc.vector.tensor_tensor(x[:, t, :], x[:, t, :], x[:, t, :], ALU.add))
                        link(nc.vector.scalar_tensor_tensor(x[:, t, :], acc[:, t, :], 0.3, x[:, t, :], ALU.mult, ALU.add))
                        layer_norm(nc, dve, link, x[:, t, :], y[:, t, :], L, t)
                    nc.vector.engine_nop().then_inc(s_ln, 1)
            sc.clear()


def decoder(nc, args, out):
    x1 = nc.dram_tensor("act1", (NB, S, D), F32, kind="Internal").ap()
    self_attention_0(nc, args["x"], x1, args)
    x2 = nc.dram_tensor("act2", (NB, S, D), F32, kind="Internal").ap()
    cross_attention(nc, x1, x2, args["ctx_1024"], args["L0_xattn_Wo"])
    x3 = nc.dram_tensor("act3", (NB, S, D), F32, kind="Internal").ap()
    ffn_0(nc, x2, x3, args)
    x4 = nc.dram_tensor("act4", (NB, S, D), F32, kind="Internal").ap()
    self_attention_1(nc, x3, x4, args)
    x5 = nc.dram_tensor("act5", (NB, S, D), F32, kind="Internal").ap()
    cross_attention_1(nc, x4, x5, args)
    ffn_1(nc, x5, out, args)


def constants():
    return {**memory_constants(), **shape_constants()}


_INS = ['x',
        'ctx_1024',
        'mask_Bx16xSxS2_ff0',
        'L0_attn_Wq',
        'L0_attn_bq',
        'L0_attn_gq',
        'L0_attn_bq_ln',
        'L0_attn_keys',
        'L0_attn_values',
        'L0_attn_Wres',
        'L0_attn_bres',
        'L0_attn_Wmem',
        'L0_attn_bmem',
        'L0_attn_Wo',
        'L0_attn_g_out',
        'L0_attn_b_out',
        'L0_xattn_Wo',
        'L0_ffn_gate_w',
        'L0_ffn_w_gate',
        'L0_ffn_w_up',
        'L0_ffn_w_down',
        'L0_ffn_A1',
        'L0_ffn_B1',
        'L0_ffn_A3',
        'L0_ffn_B3',
        'L0_ffn_A2',
        'L0_ffn_B2',
        'L1_attn_w_qkv',
        'L1_attn_w_proj',
        'L1_attn_b_proj',
        'L1_attn_rpe_q_table',
        'L1_attn_rpe_k_table',
        'L1_attn_rpe_v_table',
        'L1_xattn_W_q',
        'L1_xattn_W_k',
        'L1_xattn_W_v',
        'L1_xattn_W_o',
        'L1_xattn_lambda_q1',
        'L1_xattn_lambda_k1',
        'L1_xattn_lambda_q2',
        'L1_xattn_lambda_k2',
        'L1_xattn_rms_scale',
        'L1_ffn_q_w',
        'L1_ffn_q_b',
        'L1_ffn_k_w',
        'L1_ffn_k_b',
        'L1_ffn_v_w',
        'L1_ffn_v_b',
        'L1_ffn_o_w',
        'L1_ffn_o_b',
        'L1_ffn_router_w',
        'L1_ffn_router_b',
        'L1_ffn_w1',
        'L1_ffn_b1',
        'L1_ffn_w2',
        'L1_ffn_b2']


def kernel(**inputs):
    import numpy as _np
    import concourse.bacc as _bacc
    from concourse import mybir as _mybir
    from concourse.bass_utils import run_bass_kernel_spmd as _run

    nc = _bacc.Bacc("TRN2", target_bir_lowering=False, num_devices=1)
    arrays, args = {}, {}
    for name in _INS:
        a = _np.ascontiguousarray(inputs[name])
        arrays[f"in_{name}_dram"] = a
        args[name] = nc.dram_tensor(f"in_{name}_dram", a.shape, _mybir.dt.from_np(a.dtype), kind="ExternalInput").ap()
    for name, a in constants().items():
        arrays[f"const_{name}_dram"] = a
        args[f"const_{name}"] = nc.dram_tensor(f"const_{name}_dram", a.shape, _mybir.dt.float32, kind="ExternalInput").ap()
    out = nc.dram_tensor("out_dram", (16, 256, 256), _mybir.dt.float32, kind="ExternalOutput").ap()
    decoder(nc, args, out)
    r = _run(nc, [arrays], core_ids=[0])
    return r.results[0]["out_dram"]
```

```python
from contextlib import ExitStack, contextmanager
from itertools import zip_longest

import numpy as np
import concourse.bass as bass
from concourse import mybir

F32 = mybir.dt.float32
U32 = mybir.dt.uint32
ALU = mybir.AluOpType
ACT = mybir.ActivationFunctionType
AX = mybir.AxisListType
P = 128
D = 256
DC = D // P
NB = 16
S = 256
NT = S // P
H = 16
EPS = 1e-5
STREAMS = 2


class Scope:

    def __init__(self, nc, ctx, prefix):
        self.nc, self.ctx, self.prefix, self.sems = nc, ctx, prefix, []
        self.banks = None

    def part(self, u):
        if self.banks is None:
            self.banks = [self.ps(f"bank{i}") for i in range(8)]
            self.whole = self.prefix
        self.prefix = f"{self.whole}_{u}"
        n = 8 // STREAMS
        return self.banks[u * n:(u + 1) * n]

    def sb(self, name, shape, dt=F32):
        return self.ctx.enter_context(self.nc.sbuf_tensor(f"{self.prefix}_{name}", list(shape), dt))

    def ps(self, name, shape=(P, 512)):
        return self.ctx.enter_context(self.nc.psum_tensor(f"{self.prefix}_{name}", list(shape), F32))

    def sem(self, name):
        s = self.nc.alloc_semaphore(name=f"{self.prefix}_{name}")
        self.sems.append(s)
        return s

    def clear(self):
        self.nc.all_engine_barrier()
        for s in self.sems:
            self.nc.gpsimd.sem_clear(s)
        self.nc.all_engine_barrier()

    def release(self):
        for s in self.sems:
            self.nc.release_semaphore(s)


@contextmanager
def stage(nc, prefix):
    with ExitStack() as ctx:
        scope = Scope(nc, ctx, prefix)
        yield scope
        scope.release()


class Chain:

    def __init__(self, eng, sem):
        self.eng, self.sem, self.n = eng, sem, 0

    def __call__(self, instruction):
        self.n += 1
        instruction.then_inc(self.sem, 1)
        yield
        self.eng.wait_ge(self.sem, self.n)


def drain(steps):
    for _ in steps:
        pass


def run_streams(nc, sc, streams):
    with nc.Fori(0, NB // STREAMS) as i:
        with nc.Block() as block:
            def program(name, engine):
                live = [s[name](engine, i * STREAMS + u) for u, s in enumerate(streams)]
                for _ in zip_longest(*live):
                    pass

            @block.sync
            def _(sp):
                program("sync", sp)

            @block.gpsimd
            def _(pool):
                program("gpsimd", pool)

            @block.tensor
            def _(pe):
                program("tensor", pe)

            @block.scalar
            def _(act):
                program("scalar", act)

            @block.vector
            def _(dve):
                program("vector", dve)
        sc.clear()


def make_identity(nc, sc, ident):
    filled, done = sc.sem("ident_filled"), sc.sem("ident_done")
    with nc.Block() as block:
        @block.gpsimd
        def _(pool):
            nc.gpsimd.memset(ident[:, :], 0.0).then_inc(filled, 1)
            pool.wait_ge(filled, 1)
            nc.gpsimd.affine_select(out=ident[:, :], in_=ident[:, :], compare_op=ALU.not_equal, fill=1.0,
                                    base=0, pattern=[[-1, P]], channel_multiplier=1).then_inc(done, 1)
            pool.wait_ge(done, 1)


def load_weights(nc, sc, ident, zeroed, loads, turned):
    s_zero, s_load = sc.sem("w_zeroed"), sc.sem("w_loaded")
    s_tr, s_ev = sc.sem("w_transposed"), sc.sem("w_evacuated")
    with ExitStack() as ctx:
        slots = [ctx.enter_context(nc.psum_tensor(f"{sc.prefix}_wt{i}", [P, P], F32)) for i in range(2)]
        with nc.Block() as block:
            @block.gpsimd
            def _(pool):
                for t in zeroed:
                    nc.gpsimd.memset(t, 0.0).then_inc(s_zero, 1)

            @block.sync
            def _(sp):
                if zeroed:
                    sp.wait_ge(s_zero, len(zeroed))
                for dst, src in loads:
                    sp.dma_start(dst, src).then_inc(s_load, 16)
                sp.wait_ge(s_load, 16 * len(loads))

            @block.tensor
            def _(pe):
                if turned:
                    pe.wait_ge(s_load, 16 * len(loads))
                for n, (src, dst) in enumerate(turned):
                    p, f = src.shape[0], int(np.prod(src.shape[1:]))
                    if n >= 2:
                        pe.wait_ge(s_ev, n - 1)
                    nc.tensor.transpose(slots[n % 2][0:f, 0:p], src, ident[0:p, 0:p]).then_inc(s_tr, 1)

            @block.vector
            def _(dve):
                for n, (src, dst) in enumerate(turned):
                    p, f = src.shape[0], int(np.prod(src.shape[1:]))
                    dve.wait_ge(s_tr, n + 1)
                    nc.vector.tensor_copy(dst, slots[n % 2][0:f, 0:p]).then_inc(s_ev, 1)
    sc.clear()


def rows(x, b):
    return x[b, :, :].rearrange("(t p) d -> p t d", p=P)


def padded_heads(dst, src, heads, width, at, keep, stride):
    return [(dst[:, c, :].rearrange("p (h k) -> p h k", k=stride)[:, 0:heads, 0:keep],
             src[c * P:(c + 1) * P, :].rearrange("p (h w) -> p h w", w=width)[:, 0:heads, at:at + keep]) for c in range(DC)]


def memory_constants():
    p = np.arange(P)
    same, step = (p[:, None] % 8) == (p[None, :] % 8), (p[:, None] // 8) <= (p[None, :] // 8)
    return {"causal": (same & step).astype(np.float32)}


def self_attention_0(nc, x_in, x_out, W):
    TOTAL, KD, NK, SLOT, DH, SLOTS = 3 * H, 16, 64, 32, 64, 2 * H
    QC = TOTAL * KD // P
    PR, FO = TOTAL // 2, H * DH // P
    BIG = 3.0e38
    with stage(nc, "sa0") as sc:
        ident = sc.sb("ident", [P, P])
        make_identity(nc, sc, ident)
        wqT, bq = sc.sb("wqT", [P, DC, TOTAL * KD]), sc.sb("bq", [1, TOTAL * KD])
        woT = sc.sb("woT", [P, FO, D])
        kblk = sc.sb("keys", [P, SLOTS // 8, 8 * NK])
        vblk = sc.sb("values", [P, SLOTS // 2, P])
        wr, bm = sc.sb("wr", [P, 4, P]), sc.sb("bm", [1, DH])
        gq, bl = sc.sb("gq", [P, KD]), sc.sb("bq_ln", [P, KD])
        g_out, b_out = sc.sb("g_out", [P, D]), sc.sb("b_out", [P, D])
        causal, ones = sc.sb("causal", [P, P]), sc.sb("ones", [1, S])
        row = lambda name: W["L0_attn_" + name].rearrange("(a n) -> a n", a=1)
        with ExitStack() as raw_ctx:
            raw = lambda name, shape: raw_ctx.enter_context(nc.sbuf_tensor(f"sa0_raw_{name}", shape, F32))
            wq_r, wo_r = raw("wq", [P, QC, D]), raw("wo", [P, DC, H * DH])
            k_r, k_pad = raw("keys", [P, SLOTS // 2, KD]), raw("keys_pad", [P, SLOTS // 2, P])
            k_sq, k_ss, k_rn = raw("keys_sq", [P, SLOTS // 2, KD]), raw("keys_ss", [P, SLOTS // 2]), raw("keys_rn", [P, SLOTS // 2])
            k_pw = raw("keys_pw", [P, SLOTS // 2])
            v_r, vT = raw("values", [P, SLOTS // 2, SLOT]), raw("valuesT", [SLOT, SLOTS // 2, P])
            wm_r, wmT = raw("wmem", [DH, SLOT]), raw("wmemT", [SLOT, DH])
            wres_r, bres, bmem = raw("wres", [SLOT, 2, P]), raw("bres", [SLOT, 1]), raw("bmem", [1, DH])
            loads = [(wq_r[:, :, :], W["L0_attn_Wq"].rearrange("(c p) d -> p c d", p=P)),
                     (wo_r[:, :, :], W["L0_attn_Wo"].rearrange("(c p) f -> p c f", p=P)),
                     (bq[:, :], row("bq")), (bres[:, :], W["L0_attn_bres"].rearrange("(n a) -> n a", a=1)), (bmem[:, :], row("bmem")),
                     (wm_r[:, :], W["L0_attn_Wmem"]), (causal[:, :], W["const_causal"])]
            for hp in range(2):
                for dst, name in ((k_r, "keys"), (v_r, "values")):
                    loads.append((dst[NK * hp:NK * (hp + 1), :, :],
                                  W["L0_attn_" + name].rearrange("(r hp) k d -> hp k r d", hp=2)[hp, :, :, :]))
                for a in range(4):
                    loads.append((wres_r[:, hp, 32 * a + 16 * hp:32 * a + 16 * (hp + 1)], W["L0_attn_Wres"]))
            for dst, name, n in ((gq, "gq", KD), (bl, "bq_ln", KD), (g_out, "g_out", D), (b_out, "b_out", D)):
                loads.append((dst[:, :], row(name).broadcast_to([P, n])))
            turned = [(wq_r[:, o, c * P:(c + 1) * P], wqT[:, c, o * P:(o + 1) * P]) for o in range(QC) for c in range(DC)]
            turned += [(wo_r[:, o, f * P:(f + 1) * P], woT[:, f, o * P:(o + 1) * P]) for o in range(DC) for f in range(FO)]
            turned += [(v_r[:, r, :], vT[:, r, :]) for r in range(SLOTS // 2)] + [(wm_r[:, :], wmT[:, :])]
            load_weights(nc, sc, ident, [k_pad[:, :, :], wres_r[:, :, :], vblk[:, :, :], wr[:, :, :]], loads, turned)
            s_pw, s_ss, s_rn, s_kp, s_tr, s_ev, s_ch, s_b1, s_b2 = (sc.sem(n) for n in ("k_pw", "k_ss", "k_rn", "k_pad", "k_tr", "k_ev", "k_ch", "b_1", "b_2"))
            with ExitStack() as psum_ctx:
                tmp = [psum_ctx.enter_context(nc.psum_tensor(f"sa0_prep{i}", [P, P], F32)) for i in range(2)]
                N = SLOTS // 2
                with nc.Block() as block:
                    @block.gpsimd
                    def _(pool):
                        nc.gpsimd.memset(ones[:, :], 1.0).then_inc(s_pw, 1)
                        nc.gpsimd.memset(k_pw[:, :], -0.5).then_inc(s_pw, 1)
                        pool.wait_ge(s_pw, 2)
                        pool.wait_ge(s_ss, 1)
                        nc.gpsimd.tensor_tensor(k_rn[:, :], k_ss[:, :], k_pw[:, :], ALU.pow).then_inc(s_rn, 1)

                    @block.tensor
                    def _(pe):
                        pe.wait_ge(s_pw, 2)
                        pe.wait_ge(s_kp, 1)
                        for n in range(N):
                            if n >= 2:
                                pe.wait_ge(s_ev, n - 1)
                            nc.tensor.transpose(tmp[n % 2][:, :], k_pad[:, n, :], ident[:, :]).then_inc(s_tr, 1)
                        pe.wait_ge(s_ev, N)
                        nc.tensor.matmul(tmp[0][0:1, 0:DH], bres[:, :], wmT[:, :], start=True, stop=True).then_inc(s_b1, 1)
                        pe.wait_ge(s_b2, 1)
                        for n in range(N, 2 * N):
                            pe.wait_ge(s_ev, n - 1)
                            nc.tensor.matmul(tmp[n % 2][:, 0:DH], vT[:, n - N, :], wmT[:, :], start=True, stop=False)
                            nc.tensor.matmul(tmp[n % 2][:, 0:DH], ones[0:1, 0:P], bm[:, :], start=False, stop=True).then_inc(s_tr, 1)
                        pe.wait_ge(s_ev, 2 * N)
                        for hp in range(2):
                            ins = nc.tensor.matmul(tmp[0][:, hp * DH:(hp + 1) * DH], wres_r[:, hp, :], wmT[:, :], start=True, stop=True)
                        ins.then_inc(s_tr, 1)

                    @block.vector
                    def _(dve):
                        link = Chain(dve, s_ch)
                        drain(link(nc.vector.tensor_tensor(k_sq[:, :, :], k_r[:, :, :], k_r[:, :, :], ALU.mult)))
                        nc.vector.tensor_reduce(k_ss[:, :], k_sq[:, :, :], AX.X, ALU.add).then_inc(s_ss, 1)
                        dve.wait_ge(s_rn, 1)
                        drain(link(nc.vector.tensor_tensor(k_r[:, :, :], k_r[:, :, :], k_rn[:, :].unsqueeze(2).broadcast_to([P, N, KD]), ALU.mult)))
                        for r in range(N):
                            for hp in range(2):
                                at = (2 * (r % 4) + hp) * KD
                                ins = nc.vector.tensor_copy(k_pad[NK * hp:NK * (hp + 1), r, at:at + KD], k_r[NK * hp:NK * (hp + 1), r, :])
                        ins.then_inc(s_kp, 1)
                        for n in range(N):
                            dve.wait_ge(s_tr, n + 1)
                            nc.vector.tensor_copy(kblk[:, n // 4, (n % 4) * P:(n % 4 + 1) * P], tmp[n % 2][:, :]).then_inc(s_ev, 1)
                        dve.wait_ge(s_b1, 1)
                        nc.vector.tensor_tensor(bm[:, :], tmp[0][0:1, 0:DH], bmem[:, :], ALU.add).then_inc(s_b2, 1)
                        for n in range(N, 2 * N):
                            dve.wait_ge(s_tr, n + 1)
                            for hp in range(2):
                                ins = nc.vector.tensor_copy(vblk[NK * hp:NK * (hp + 1), n - N, DH * hp:DH * (hp + 1)],
                                                            tmp[n % 2][NK * hp:NK * (hp + 1), 0:DH])
                            ins.then_inc(s_ev, 1)
                        dve.wait_ge(s_tr, 2 * N + 1)
                        for a in range(4):
                            drain(link(nc.vector.tensor_copy(wr[32 * a:32 * a + 32, a, :], tmp[0][32 * a:32 * a + 32, :])))
        def stream(u):
            sc.part(u)
            x, y, xT = sc.sb("x", [P, NT, D]), sc.sb("y", [P, NT, D]), sc.sb("xT", [P, DC, S])
            q = sc.sb("q", [P, NT, TOTAL * KD])
            mean, var, rstd, pw = (sc.sb(n, [P, NT, TOTAL]) for n in ("mean", "var", "rstd", "pw"))
            qT = sc.sb("qT", [P, QC, S])
            mx, d8, s8 = sc.sb("top8", [P, 2, 8, 8]), sc.sb("top8_shift", [P, 2, 8, 8]), sc.sb("sum8", [P, 2, 8])
            sh, rep, em = sc.sb("shift", [P, 2, 8 * NK]), sc.sb("replaced", [P, 2, 8 * NK]), sc.sb("em", [P, 2, 8 * NK])
            wT = sc.sb("wT", [P, PR, S])
            sq = sh[:, :, :].rearrange("p a n -> p (a n)")[:, 0:TOTAL * KD]
            ex, at = rep, sh[:, :, :].rearrange("p a (k j s) -> p a k j s", k=2, j=2)
            lo, loT = wT[:, 8:16, :].rearrange("p (t f) s -> p t (f s)", t=NT), wT[:, 0:FO, :]
            hk, hq = sc.sb("hk", [P, PR // 3, S]), sc.sb("hq", [P, PR // 3, S])
            v = sc.sb("v", [P, NT, H, DH + 1])
            den = sc.sb("den", [P, 2, 4])
            banks = sc.part(u)
            L = NormTiles(sc, 2 * NT)
            (s_x, s_xT, s_xTs, s_q, s_var, s_rstd, s_pw, s_qn, s_qT, s_qTs, s_sc, s_sh, s_e, s_em, s_en, s_tr, s_wT, s_kq, s_mn, s_ex, s_hh, s_v, s_vs,
             s_a, s_at, s_lo, s_los, s_loT, s_loTs, s_y, s_dve, s_ln, s_st) = (sc.sem(n) for n in (
                 "x xT xTs q var rstd pw qn qT qTs sc sh e em en tr wT kq mn ex hh v vs a at lo los loT loTs y dve ln st").split())
            steps = [(c, t) for c in range(QC) for t in range(NT)]
            NS = len(steps)
            kq = [(dst, i, pair0) for dst, pair0 in ((hk, 0), (hq, PR * 2 // 3)) for i in range(4)]
            vsteps = [(t, half) for t in range(NT) for half in range(2)]
            groups = [(t, g) for t in range(NT) for g in range(4)]
            seqs = lambda ap, b, t: ap[:, bass.ds(b * 16 + 8 * t, 8), :]

            def sync(sp, b):
                for t in range(NT):
                    sp.dma_start(x[:, t, :], seqs(x_in, b, t)).then_inc(s_x, 16)
                    yield
                sp.wait_ge(s_ln, 1)
                for t in range(NT):
                    sp.dma_start(seqs(x_out, b, t), y[:, t, :]).then_inc(s_st, 16)
                    yield
                sp.wait_ge(s_st, 16 * NT)

            def gpsimd(pool, b):
                nc.gpsimd.memset(pw[:, :, :], -0.5).then_inc(s_pw, 1)
                yield
                pool.wait_ge(s_pw, 1)
                for t in range(NT):
                    pool.wait_ge(s_var, t + 1)
                    nc.gpsimd.tensor_tensor(rstd[:, t, :], var[:, t, :], pw[:, t, :], ALU.pow).then_inc(s_rstd, 1)
                    yield
                for n in range(NS):
                    pool.wait_ge(s_em, n + 1)
                    e = em[:, n % 2, :].rearrange("p (h k) -> p h k", h=8)
                    nc.gpsimd.tensor_tensor(e, e, s8[:, n % 2, :].unsqueeze(2).broadcast_to([P, 8, NK]), ALU.mult).then_inc(s_en, 1)
                    yield
                yield from norm_powers(nc, pool, L, range(2 * NT))

            def tensor(pe, b):
                pe.wait_ge(s_x, 16 * NT)
                for c in range(DC):
                    for t in range(NT):
                        ins = nc.tensor.transpose(banks[0][:, c * S + t * P:c * S + (t + 1) * P],
                                                  x[:, t, c * P:(c + 1) * P], ident[:, :])
                ins.then_inc(s_xT, 1)
                yield
                pe.wait_ge(s_xTs, 1)
                for t in range(NT):
                    for lo_, n in ((0, 512), (512, 256)):
                        o = banks[(1 + 2 * t + lo_ // 512) % 4][:, 0:n]
                        for c in range(DC):
                            nc.tensor.matmul(o, xT[:, c, t * P:(t + 1) * P], wqT[:, c, lo_:lo_ + n], start=(c == 0), stop=False)
                        ins = nc.tensor.matmul(o, ones[0:1, 0:P], bq[0:1, lo_:lo_ + n], start=False, stop=True)
                    ins.then_inc(s_q, 1)
                    yield
                pe.wait_ge(s_qn, NT)
                for j in range(QC // 2):
                    for k in range(2):
                        for t in range(NT):
                            c = 2 * j + k
                            ins = nc.tensor.transpose(banks[1 + j][:, k * S + t * P:k * S + (t + 1) * P],
                                                      q[:, t, c * P:(c + 1) * P], ident[:, :])
                    ins.then_inc(s_qT, 1)
                    yield
                pe.wait_ge(s_qTs, QC // 2)
                for n in range(NS + 1):
                    if n < NS:
                        c, t = steps[n]
                        if n >= 2:
                            pe.wait_ge(s_sh, n - 1)
                        nc.tensor.matmul(banks[n % 2][:, :], qT[:, c, t * P:(t + 1) * P], kblk[:, c % 4, :],
                                         start=True, stop=True).then_inc(s_sc, 1)
                        yield
                    if n >= 1:
                        m = n - 1
                        pe.wait_ge(s_en, m + 1)
                        if m >= 2:
                            pe.wait_ge(s_wT, m - 1)
                        for r in range(4):
                            ins = nc.tensor.transpose(banks[2 + m % 2][:, r * P:(r + 1) * P], em[:, m % 2, r * P:(r + 1) * P],
                                                      ident[:, :])
                        ins.then_inc(s_tr, 1)
                        yield
                pe.wait_ge(s_wT, NS)

                def mixed(o, r, tok, tokens_stationary):
                    c, a = r // 4, r % 4
                    parts = ((wT[:, r, tok], vblk[:, r % 16, :]), (qT[:, c, tok], wr[:, a, :]))
                    for n, (tokens, w) in enumerate(parts):
                        l, rr = (tokens, w) if tokens_stationary else (w, tokens)
                        ins = nc.tensor.matmul(o, l, rr, start=(n == 0), stop=(n == 1))
                    return ins

                for n, (dst, i, pair0) in enumerate(kq):
                    if n >= 2:
                        pe.wait_ge(s_hh, n - 1)
                    for k in range(2):
                        ins = mixed(banks[n % 2][:, k * S:(k + 1) * S], pair0 + 2 * i + k, slice(0, S), False)
                    ins.then_inc(s_kq, 1)
                    yield
                for n, (t, half) in enumerate(vsteps):
                    if n >= 2:
                        pe.wait_ge(s_vs, n - 1)
                    for k in range(4):
                        ins = mixed(banks[2 + n % 2][:, k * P:(k + 1) * P], H // 2 + 4 * half + k, slice(t * P, (t + 1) * P), True)
                    ins.then_inc(s_v, 1)
                    yield
                pe.wait_ge(s_hh, len(kq))
                pe.wait_ge(s_vs, len(vsteps))
                NGR = len(groups)
                for n in range(NGR + 1):
                    if n < NGR:
                        t, g = groups[n]
                        if n >= 1:
                            pe.wait_ge(s_at, n)
                        for k in range(4):
                            h = 4 * g + k
                            r, p0 = h // 2, DH * (h % 2)
                            ins = nc.tensor.matmul(banks[k % 2][:, (k // 2) * P:(k // 2 + 1) * P], hk[p0:p0 + DH, r, t * P:(t + 1) * P],
                                                   hq[p0:p0 + DH, r, t * P:(t + 1) * P], start=True, stop=True)
                        ins.then_inc(s_a, 1)
                        yield
                    if n >= 1:
                        m = n - 1
                        t, g = groups[m]
                        pe.wait_ge(s_at, m + 1)
                        if m >= 2:
                            pe.wait_ge(s_los, m - 1)
                        for k in range(4):
                            ins = nc.tensor.matmul(banks[2 + m % 2][:, k * (DH + 1):(k + 1) * (DH + 1)], at[:, m % 2, k % 2, k // 2, :],
                                                   v[:, t, 4 * g + k, :], start=True, stop=True)
                        ins.then_inc(s_lo, 1)
                        yield
                pe.wait_ge(s_los, NGR)
                for n in range(FO // 2):
                    if n >= 2:
                        pe.wait_ge(s_loTs, n - 1)
                    for k in range(2):
                        for t in range(NT):
                            f = 2 * n + k
                            ins = nc.tensor.transpose(banks[n % 2][:, k * S + t * P:k * S + (t + 1) * P],
                                                      lo[:, t, f * P:(f + 1) * P], ident[:, :])
                    ins.then_inc(s_loT, 1)
                    yield
                pe.wait_ge(s_loTs, FO // 2)
                for t in range(NT):
                    for f in range(FO):
                        ins = nc.tensor.matmul(banks[2][:, t * D:(t + 1) * D], loT[:, f, t * P:(t + 1) * P], woT[:, f, :],
                                               start=(f == 0), stop=(f == FO - 1))
                ins.then_inc(s_y, 1)
                yield

            def scalar(act, b):
                for n in range(NS + 1):
                    if n < NS:
                        act.wait_ge(s_sh, n + 1)
                        nc.scalar.activation(d8[:, n % 2, :, :], d8[:, n % 2, :, :], ACT.Exp)
                        nc.scalar.activation(sh[:, n % 2, :], sh[:, n % 2, :], ACT.Exp).then_inc(s_e, 1)
                        yield
                    if n >= 1:
                        m = n - 1
                        c, t = steps[m]
                        act.wait_ge(s_tr, m + 1)
                        nc.scalar.copy(wT[:, 4 * c:4 * c + 4, t * P:(t + 1) * P],
                                       banks[2 + m % 2][:, :].rearrange("p (r s) -> p r s", r=4)).then_inc(s_wT, 1)
                        yield
                for n in range(len(kq)):
                    act.wait_ge(s_mn, n + 1)
                    nc.scalar.activation(ex[:, n % 2, :], ex[:, n % 2, :], ACT.Exp).then_inc(s_ex, 1)
                    yield
                for n, (t, half) in enumerate(vsteps):
                    act.wait_ge(s_v, n + 1)
                    nc.scalar.copy(v[:, t, 8 * half:8 * half + 8, 0:DH], banks[2 + n % 2][:, :].rearrange("p (h e) -> p h e", h=8))\
                        .then_inc(s_vs, 1)
                    yield
                for n in range(FO // 2):
                    act.wait_ge(s_loT, n + 1)
                    nc.scalar.copy(loT[:, 2 * n:2 * n + 2, :], banks[n % 2][:, :].rearrange("p (f s) -> p f s", f=2))\
                        .then_inc(s_loTs, 1)
                    yield

            def vector(dve, b):
                link = Chain(dve, s_dve)
                L.asked = 0
                heads = lambda ap: ap.rearrange("p (h d) -> p h d", d=KD)
                yield from link(nc.vector.memset(v[:, :, :, DH:DH + 1], 1.0))
                dve.wait_ge(s_xT, 1)
                nc.vector.tensor_copy(xT[:, :, :], banks[0][:, :].rearrange("p (c s) -> p c s", c=DC)).then_inc(s_xTs, 1)
                yield
                for t in range(NT):
                    dve.wait_ge(s_q, t + 1)
                    for lo_, n in ((0, 512), (512, 256)):
                        h0, nh = lo_ // KD, n // KD
                        ins = nc.vector.tensor_reduce(mean[:, t, h0:h0 + nh], heads(banks[(1 + 2 * t + lo_ // 512) % 4][:, 0:n]), AX.X, ALU.add)
                    yield from link(ins)
                    yield from link(nc.vector.tensor_scalar(mean[:, t, :], mean[:, t, :], 1.0 / KD, None, ALU.mult))
                    for lo_, n in ((0, 512), (512, 256)):
                        h0, nh = lo_ // KD, n // KD
                        ins = nc.vector.tensor_tensor(heads(q[:, t, lo_:lo_ + n]), heads(banks[(1 + 2 * t + lo_ // 512) % 4][:, 0:n]),
                                                      mean[:, t, h0:h0 + nh].unsqueeze(2).broadcast_to([P, nh, KD]), ALU.subtract)
                    yield from link(ins)
                    yield from link(nc.vector.tensor_tensor(sq, q[:, t, :], q[:, t, :], ALU.mult))
                    yield from link(nc.vector.tensor_reduce(var[:, t, :], heads(sq), AX.X, ALU.add))
                    nc.vector.tensor_scalar(var[:, t, :], var[:, t, :], 1.0 / KD, EPS, ALU.mult, ALU.add).then_inc(s_var, 1)
                    yield
                for t in range(NT):
                    dve.wait_ge(s_rstd, t + 1)
                    yield from link(nc.vector.tensor_tensor(heads(q[:, t, :]), heads(q[:, t, :]),
                                                 rstd[:, t, :].unsqueeze(2).broadcast_to([P, TOTAL, KD]), ALU.mult))
                    yield from link(nc.vector.tensor_tensor(heads(q[:, t, :]), heads(q[:, t, :]),
                                                 gq[:, :].unsqueeze(1).broadcast_to([P, TOTAL, KD]), ALU.mult))
                    nc.vector.tensor_tensor(heads(q[:, t, :]), heads(q[:, t, :]),
                                            bl[:, :].unsqueeze(1).broadcast_to([P, TOTAL, KD]), ALU.add).then_inc(s_qn, 1)
                    yield
                for j in range(QC // 2):
                    dve.wait_ge(s_qT, j + 1)
                    nc.vector.tensor_copy(qT[:, 2 * j:2 * j + 2, :], banks[1 + j][:, :].rearrange("p (c s) -> p c s", c=2)).then_inc(s_qTs, 1)
                    yield

                def keep(m):
                    dve.wait_ge(s_e, m + 1)
                    yield from link(nc.vector.tensor_reduce(s8[:, m % 2, :], d8[:, m % 2, :, :], AX.X, ALU.add))
                    yield from link(nc.vector.reciprocal(s8[:, m % 2, :], s8[:, m % 2, :]))
                    if m >= 2:
                        dve.wait_ge(s_tr, m - 1)
                    nc.vector.scalar_tensor_tensor(em[:, m % 2, :], rep[:, m % 2, :], BIG, sh[:, m % 2, :],
                                                   ALU.is_equal, ALU.mult).then_inc(s_em, 1)
                    yield

                for n in range(NS + 1):
                    if n < NS:
                        dve.wait_ge(s_sc, n + 1)
                        if n >= 2:
                            dve.wait_ge(s_en, n - 1)
                            dve.wait_ge(s_em, n - 1)
                        bank = banks[n % 2]
                        for k in range(8):
                            ins = nc.vector.max(mx[:, n % 2, k, :], bank[:, k * NK:(k + 1) * NK])
                        yield from link(ins)
                        for k in range(8):
                            ins = nc.vector.match_replace(rep[:, n % 2, k * NK:(k + 1) * NK], mx[:, n % 2, k, :],
                                                          bank[:, k * NK:(k + 1) * NK], BIG)
                        nc.vector.tensor_tensor(d8[:, n % 2, :, :], mx[:, n % 2, :, :],
                                                mx[:, n % 2, :, 0:1].broadcast_to([P, 8, 8]), ALU.subtract)
                        yield from link(nc.vector.tensor_tensor(sh[:, n % 2, :].rearrange("p (h k) -> p h k", h=8), bank[:, :].rearrange("p (h k) -> p h k", h=8),
                                                mx[:, n % 2, :, 0:1].broadcast_to([P, 8, NK]), ALU.subtract))
                        nc.vector.engine_nop().then_inc(s_sh, 1)
                        yield
                    if n >= 1:
                        yield from keep(n - 1)
                for n in range(len(kq) + 1):
                    if n < len(kq):
                        dve.wait_ge(s_kq, n + 1)
                        nc.vector.tensor_scalar(ex[:, n % 2, :], banks[n % 2][:, :], 0.0, None, ALU.min).then_inc(s_mn, 1)
                        yield
                    if n >= 1:
                        m = n - 1
                        dst, i, _ = kq[m]
                        dve.wait_ge(s_ex, m + 1)
                        nc.vector.scalar_tensor_tensor(dst[:, 2 * i:2 * i + 2, :].rearrange("p r s -> p (r s)"), banks[m % 2][:, :], 0.0,
                                                       ex[:, m % 2, :], ALU.max, ALU.add).then_inc(s_hh, 1)
                        yield
                        dve.wait_ge(s_hh, m + 1)
                for n in range(len(groups) + 1):
                    if n < len(groups):
                        dve.wait_ge(s_a, n + 1)
                        if n >= 2:
                            dve.wait_ge(s_lo, n - 1)
                        for k in range(2):
                            ins = nc.vector.tensor_tensor(at[:, n % 2, k, :, :], banks[k][:, 0:2 * P].rearrange("p (j s) -> p j s", j=2),
                                                          causal[:, :].unsqueeze(1).broadcast_to([P, 2, P]), ALU.mult)
                        ins.then_inc(s_at, 1)
                        yield
                    if n >= 1:
                        m = n - 1
                        t, g = groups[m]
                        dve.wait_ge(s_lo, m + 1)
                        bank = banks[2 + m % 2][:, 0:4 * (DH + 1)].rearrange("p (k e) -> p k e", k=4)
                        dn = den[:, m % 2, :].unsqueeze(2)
                        yield from link(nc.vector.tensor_scalar(dn, bank[:, :, DH:DH + 1], EPS, None, ALU.add))
                        yield from link(nc.vector.reciprocal(den[:, m % 2, :], den[:, m % 2, :]))
                        yield from link(nc.vector.tensor_scalar(den[:, m % 2, :], den[:, m % 2, :], DH ** -0.5, None, ALU.mult))
                        nc.vector.tensor_tensor(lo[:, t, 4 * g * DH:4 * (g + 1) * DH].rearrange("p (k e) -> p k e", k=4),
                                                bank[:, :, 0:DH], dn.broadcast_to([P, 4, DH]), ALU.mult).then_inc(s_los, 1)
                        yield
                dve.wait_ge(s_y, 1)
                for t in range(NT):
                    yield from link(nc.vector.tensor_tensor(y[:, t, :], x[:, t, :], banks[2][:, t * D:(t + 1) * D], ALU.add))
                    yield from layer_norm(nc, dve, link, y[:, t, :], y[:, t, :], L, t)
                    yield from link(nc.vector.tensor_tensor(y[:, t, :], y[:, t, :], g_out[:, :], ALU.mult))
                    yield from link(nc.vector.tensor_tensor(y[:, t, :], y[:, t, :], b_out[:, :], ALU.add))
                for t in range(NT):
                    yield from link(nc.vector.tensor_tensor(x[:, t, :], x[:, t, :], y[:, t, :], ALU.add))
                    yield from layer_norm(nc, dve, link, x[:, t, :], y[:, t, :], L, NT + t)
                nc.vector.engine_nop().then_inc(s_ln, 1)
                yield

            return dict(sync=sync, gpsimd=gpsimd, tensor=tensor, scalar=scalar, vector=vector)

        run_streams(nc, sc, [stream(u) for u in range(STREAMS)])


def attend(nc, W, pe=None, dve=None, act=None):
    N = W.heads
    if pe is not None:
        for n in range(N + 2):
            if n < N:
                if n >= 1:
                    pe.wait_ge(W.s_exp, n)
                for t in range(NT):
                    ins = nc.tensor.matmul(W.scores[:, t * S:(t + 1) * S], W.qT[:, n // 4, t * P:(t + 1) * P],
                                           W.kM[:, n, :], start=True, stop=True)
                ins.then_inc(W.s_scores, 1)
                yield
            if 1 <= n <= N:
                m = n - 1
                pe.wait_ge(W.s_exp, m + 1)
                if m >= 1:
                    pe.wait_ge(W.s_wT, m)
                for jt in range(NT):
                    for t in range(NT):
                        ins = nc.tensor.transpose(W.turned[:, jt * S + t * P:jt * S + (t + 1) * P],
                                                  W.E[:, m % 3, t, jt * P:(jt + 1) * P], W.ident[:, :])
                ins.then_inc(W.s_turned, 1)
                yield
            if n >= 2:
                m = n - 2
                pe.wait_ge(W.s_wT, m + 1)
                for t in range(NT):
                    for jt in range(NT):
                        ins = nc.tensor.matmul(W.out[:, t * (N * W.dv) + m * W.dv:t * (N * W.dv) + (m + 1) * W.dv],
                                               W.wT[:, m % 3, jt, t * P:(t + 1) * P],
                                               W.V(jt, m), start=(jt == 0), stop=(jt == NT - 1))
                ins.then_inc(W.s_av, 1)
                yield
    if dve is not None:
        for n in range(N + 1):
            if n < N:
                dve.wait_ge(W.s_scores, n + 1)
                nc.vector.tensor_reduce(W.negmax[:, n, :], W.scores[:, :].rearrange("p (t k) -> p t k", t=NT),
                                        AX.X, ALU.max, negate=True).then_inc(W.s_max, 1)
                yield
            if n >= 1:
                m = n - 1
                dve.wait_ge(W.s_turned, m + 1)
                if m >= 3:
                    dve.wait_ge(W.s_av, m - 2)
                nc.vector.tensor_copy(W.wT[:, m % 3, :, :], W.turned[:, :].rearrange("p (j k) -> p j k", j=NT))\
                    .then_inc(W.s_wT, 1)
                yield
    if act is not None:
        for n in range(N):
            act.wait_ge(W.s_max, n + 1)
            if n >= 3:
                act.wait_ge(W.s_turned, n - 2)
            for t in range(NT):
                ins = nc.scalar.activation(W.E[:, n % 3, t, :], W.scores[:, t * S:(t + 1) * S], ACT.Exp,
                                           bias=W.negmax[:, n, t:t + 1], scale=1.0,
                                           accum_out=W.sums[:, n, t:t + 1])
            ins.then_inc(W.s_exp, 1)
            yield


def place_keys(eng, copy, kM, bank, blk0, first, signal):
    for k in range(2):
        for a in (first, first + 1):
            copy(kM[32 * a:32 * a + 32, 4 * (blk0 + k) + a, :], bank[32 * a:32 * a + 32, k * S:(k + 1) * S]).then_inc(signal, 1)
            yield


class AttentionTiles:

    def __init__(self, sc, ident, heads, dk, dv, scores, turned, out, kM):
        self.heads, self.dk, self.dv, self.ident = heads, dk, dv, ident
        self.scores, self.turned, self.out = scores, turned, out
        self.qT = sc.sb("qT", [P, heads // 4, S])
        self.kM = kM
        self.E = sc.sb("E", [P, 3, NT, S])
        self.wT = sc.sb("wT", [P, 3, NT, S])
        self.negmax = sc.sb("negmax", [P, heads, NT])
        self.sums = sc.sb("sums", [P, heads, NT])
        self.s_scores, self.s_max, self.s_exp = sc.sem("scores"), sc.sem("max"), sc.sem("exp")
        self.s_turned, self.s_wT, self.s_av = sc.sem("turned"), sc.sem("wT"), sc.sem("av")


def layer_norm(nc, dve, link, z, out, L, t):
    yield from link(nc.vector.bn_stats(L.stats[:, t, :], z))
    yield from link(nc.vector.bn_aggr(L.mv[:, t, :], L.stats[:, t, :]))
    nc.vector.tensor_scalar(L.ve[:, t:t + 1], L.mv[:, t, 1:2], EPS, None, ALU.add).then_inc(L.s_ve, 1)
    yield
    L.asked += 1
    dve.wait_ge(L.s_rstd, L.asked)
    yield from link(nc.vector.tensor_scalar(out, z, L.mv[:, t, 0:1], L.rstd[:, t:t + 1], ALU.subtract, ALU.mult))


class NormTiles:
    def __init__(self, sc, n=NT):
        self.stats, self.mv = sc.sb("ln_stats", [P, n, 6]), sc.sb("ln_mv", [P, n, 2])
        self.ve, self.rstd = sc.sb("ln_ve", [P, n]), sc.sb("ln_rstd", [P, n])
        self.power = sc.sb("ln_power", [P, 1])
        self.s_ve, self.s_rstd, self.s_power = sc.sem("ln_ve"), sc.sem("ln_rstd"), sc.sem("ln_power")
        self.asked = 0


def norm_powers(nc, pool, L, order):
    nc.gpsimd.memset(L.power[:, :], -0.5).then_inc(L.s_power, 1)
    yield
    pool.wait_ge(L.s_power, 1)
    for n, t in enumerate(order):
        pool.wait_ge(L.s_ve, n + 1)
        nc.gpsimd.tensor_tensor(L.rstd[:, t:t + 1], L.ve[:, t:t + 1], L.power[:, :], ALU.pow).then_inc(L.s_rstd, 1)
        yield


def cross_attention(nc, x_in, x_out, ctx_in, Wo):
    dk = D // H
    with stage(nc, "xa0") as sc:
        ident = sc.sb("ident", [P, P])
        make_identity(nc, sc, ident)
        wo_raw, woT = sc.sb("wo_raw", [P, DC, D]), sc.sb("woT", [P, DC, D])
        kMs = [sc.sb(f"kM{u}", [P, H, S]) for u in range(STREAMS)]
        xps = [sc.sb(f"x_padded{u}", [P, NT, H, 32]) for u in range(STREAMS)]
        cps = [sc.sb(f"ctx_padded{u}", [P, NT, H, 32]) for u in range(STREAMS)]
        load_weights(nc, sc, ident, [t[:, :, :, :] for t in xps + cps] + [t[:, :, :] for t in kMs],
                     [(wo_raw[:, :, :], Wo.rearrange("(c p) k -> p c k", p=P))],
                     [(wo_raw[:, o, c * P:(c + 1) * P], woT[:, c, o * P:(o + 1) * P]) for o in range(DC) for c in range(DC)])
        def stream(u):
            sc.part(u)
            x = sc.sb("x", [P, NT, D])
            cx = sc.sb("ctx", [P, NT, D])
            y = sc.sb("y", [P, NT, D])
            o_sb, oT = sc.sb("o", [P, NT, D]), sc.sb("oT", [P, DC, S])
            rs = sc.sb("rsums", [P, H, NT])
            banks = sc.part(u)
            xp, cp = xps[u], cps[u]
            A = AttentionTiles(sc, ident, H, dk, dk, banks[0], banks[1], banks[2], kMs[u])
            A.V = lambda jt, h: cx[:, jt, h * dk:(h + 1) * dk]
            L = NormTiles(sc)
            s_x, s_pad, s_qk, s_qkT, s_kA, s_kV = (sc.sem(n) for n in ("x", "pad", "qk", "qkT", "kA", "kV"))
            s_o, s_oT, s_oTs, s_y, s_dve, s_ln, s_st = (sc.sem(n) for n in ("o", "oT", "oTs", "y", "dve", "ln", "stored"))

            def sync(sp, b):
                sp.dma_start(x[:, :, :], rows(x_in, b)).then_inc(s_x, 16)
                yield
                sp.dma_start(cx[:, :, :], rows(ctx_in, b)).then_inc(s_x, 16)
                yield
                sp.wait_ge(s_ln, 1)
                sp.dma_start(rows(x_out, b), y[:, :, :]).then_inc(s_st, 16)
                yield
                sp.wait_ge(s_st, 16)

            def gpsimd(pool, b):
                yield from norm_powers(nc, pool, L, range(NT))

            def tensor(pe, b):
                pe.wait_ge(s_pad, 2)
                n = 0
                for src in (xp, cp):
                    for half in range(2):
                        if n == 2:
                            pe.wait_ge(s_qkT, 1)
                        if n == 3:
                            pe.wait_ge(s_qkT, 2)
                        for k in range(2):
                            for t in range(NT):
                                blk = 2 * half + k
                                ins = nc.tensor.transpose(banks[n % 2][:, k * S + t * P:k * S + (t + 1) * P],
                                                          src[:, t, 4 * blk:4 * blk + 4, :].rearrange("p h d -> p (h d)"),
                                                          ident[:, :])
                        ins.then_inc(s_qk, 1)
                        yield
                        n += 1
                pe.wait_ge(s_qkT, 2)
                pe.wait_ge(s_kA, 8)
                pe.wait_ge(s_kV, 8)
                yield from attend(nc, A, pe=pe)
                pe.wait_ge(s_o, 1)
                for c in range(DC):
                    for t in range(NT):
                        ins = nc.tensor.transpose(banks[0][:, c * S + t * P:c * S + (t + 1) * P],
                                                  o_sb[:, t, c * P:(c + 1) * P], ident[:, :])
                ins.then_inc(s_oT, 1)
                yield
                pe.wait_ge(s_oTs, 1)
                for t in range(NT):
                    for c in range(DC):
                        ins = nc.tensor.matmul(banks[1][:, t * D:(t + 1) * D], oT[:, c, t * P:(t + 1) * P],
                                               woT[:, c, :], start=(c == 0), stop=(c == DC - 1))
                ins.then_inc(s_y, 1)
                yield

            def scalar(act, b):
                for n in range(2):
                    act.wait_ge(s_qk, 3 + n)
                    yield from place_keys(act, nc.scalar.copy, A.kM, banks[n], 2 * n, 0, s_kA)
                yield from attend(nc, A, act=act)

            def vector(dve, b):
                link = Chain(dve, s_dve)
                L.asked = 0
                dve.wait_ge(s_x, 32)
                for dst, src in ((xp, x), (cp, cx)):
                    for t in range(NT):
                        ins = nc.vector.tensor_copy(dst[:, t, :, 0:dk], src[:, t, :].rearrange("p (h d) -> p h d", h=H))
                    ins.then_inc(s_pad, 1)
                    yield
                for n in range(4):
                    dve.wait_ge(s_qk, n + 1)
                    if n >= 2:
                        yield from place_keys(dve, nc.vector.tensor_copy, A.kM, banks[n % 2], 2 * (n % 2), 2, s_kV)
                        continue
                    dst = A.qT[:, 2 * n:2 * n + 2, :]
                    src = banks[n % 2][:, :].rearrange("p (k s) -> p k s", k=2)
                    nc.vector.tensor_scalar(dst, src, dk ** -0.5, None, ALU.mult).then_inc(s_qkT, 1)
                    yield
                yield from attend(nc, A, dve=dve)
                dve.wait_ge(A.s_exp, H)
                yield from link(nc.vector.reciprocal(rs[:, :, :], A.sums[:, :, :]))
                dve.wait_ge(A.s_av, H)
                for t in range(NT):
                    ins = nc.vector.tensor_tensor(o_sb[:, t, :].rearrange("p (h d) -> p h d", h=H),
                                                  banks[2][:, t * D:(t + 1) * D].rearrange("p (h d) -> p h d", h=H),
                                                  rs[:, :, t:t + 1].broadcast_to([P, H, dk]), ALU.mult)
                ins.then_inc(s_o, 1)
                yield
                dve.wait_ge(s_oT, 1)
                nc.vector.tensor_copy(oT[:, :, :], banks[0][:, :].rearrange("p (c s) -> p c s", c=DC)).then_inc(s_oTs, 1)
                yield
                dve.wait_ge(s_y, 1)
                for t in range(NT):
                    yield from link(nc.vector.tensor_tensor(x[:, t, :], x[:, t, :], banks[1][:, t * D:(t + 1) * D], ALU.add))
                    yield from layer_norm(nc, dve, link, x[:, t, :], y[:, t, :], L, t)
                nc.vector.engine_nop().then_inc(s_ln, 1)
                yield

            return dict(sync=sync, gpsimd=gpsimd, tensor=tensor, scalar=scalar, vector=vector)

        run_streams(nc, sc, [stream(u) for u in range(STREAMS)])


def top2(nc, dve, link, lg, mx, ix, ixf, iota, onehot, t, times):
    yield from link(nc.vector.max(mx[:, t, :], lg[:, t, :]))
    yield from link(nc.vector.max_index(ix[:, t, :], mx[:, t, :], lg[:, t, :]))
    yield from link(nc.vector.tensor_copy(ixf[:, t, :], ix[:, t, 0:2]))
    for k in range(2):
        ins = nc.vector.tensor_scalar(onehot[:, t, k, :], iota[:, :], ixf[:, t, k:k + 1], times, ALU.is_equal, ALU.mult)
    yield from link(ins)


def ffn_0(nc, x_in, x_out, W):
    E, R, F = 8, 16, 1024
    FC, ER, SCALE = F // P, E * R, 2.0
    WD = D + ER
    with stage(nc, "ff0") as sc:
        ident = sc.sb("ident", [P, P])
        make_identity(nc, sc, ident)
        wgT, wuT = sc.sb("wgT", [P, DC, F]), sc.sb("wuT", [P, DC, F])
        wdT = sc.sb("wdT_A2T", [P, FC, WD])
        a13T = sc.sb("A13T", [P, DC, 2 * ER])
        b1T, b3T, b2T = sc.sb("B1T", [P, F]), sc.sb("B3T", [P, F]), sc.sb("B2T", [P, D])
        gateT = sc.sb("gateT", [P, DC, E])
        with ExitStack() as raw_ctx:
            raw = lambda name, shape: raw_ctx.enter_context(nc.sbuf_tensor(f"ff0_raw_{name}", shape, F32))
            wg_r, wu_r = raw("wg", [P, FC, D]), raw("wu", [P, FC, D])
            wd_r, a2_r = raw("wd", [P, DC, F]), raw("A2", [P, F])
            a1_r, a3_r = raw("A1", [P, D]), raw("A3", [P, D])
            b1_r, b3_r, b2_r = raw("B1", [P, FC, ER]), raw("B3", [P, FC, ER]), raw("B2", [P, DC, ER])
            g_r = raw("gate", [E, D])
            loads = [(wg_r[:, :, :], W["L0_ffn_w_gate"].rearrange("(c p) d -> p c d", p=P)),
                     (wu_r[:, :, :], W["L0_ffn_w_up"].rearrange("(c p) d -> p c d", p=P)),
                     (wd_r[:, :, :], W["L0_ffn_w_down"].rearrange("(c p) f -> p c f", p=P)),
                     (a2_r[:, :], W["L0_ffn_A2"].rearrange("e r f -> (e r) f")),
                     (a1_r[:, :], W["L0_ffn_A1"].rearrange("e r d -> (e r) d")),
                     (a3_r[:, :], W["L0_ffn_A3"].rearrange("e r d -> (e r) d")),
                     (g_r[:, :], W["L0_ffn_gate_w"])]
            for dst, src, n in ((b1_r, "L0_ffn_B1", FC), (b3_r, "L0_ffn_B3", FC), (b2_r, "L0_ffn_B2", DC)):
                for c in range(n):
                    loads.append((dst[:, c, :].rearrange("p (e r) -> p e r", e=E),
                                  W[src][:, c * P:(c + 1) * P, :].rearrange("e p r -> p e r")))
            turned = []
            for f in range(FC):
                for c in range(DC):
                    turned += [(wg_r[:, f, c * P:(c + 1) * P], wgT[:, c, f * P:(f + 1) * P]),
                               (wu_r[:, f, c * P:(c + 1) * P], wuT[:, c, f * P:(f + 1) * P]),
                               (wd_r[:, c, f * P:(f + 1) * P], wdT[:, f, c * P:(c + 1) * P])]
                turned += [(a2_r[:, f * P:(f + 1) * P], wdT[:, f, D:WD]),
                           (b1_r[:, f, :], b1T[:, f * P:(f + 1) * P]), (b3_r[:, f, :], b3T[:, f * P:(f + 1) * P])]
            for c in range(DC):
                turned += [(a1_r[:, c * P:(c + 1) * P], a13T[:, c, 0:ER]), (a3_r[:, c * P:(c + 1) * P], a13T[:, c, ER:2 * ER]),
                           (b2_r[:, c, :], b2T[:, c * P:(c + 1) * P]), (g_r[:, c * P:(c + 1) * P], gateT[:, c, :])]
            load_weights(nc, sc, ident, [], loads, turned)
        iota = sc.sb("iota", [P, E])
        s_iota = sc.sem("iota")
        with nc.Block() as block:
            @block.gpsimd
            def _(pool):
                for e in range(E):
                    nc.gpsimd.memset(iota[:, e:e + 1], float(e)).then_inc(s_iota, 1)
                pool.wait_ge(s_iota, E)
        def stream(u):
            sc.part(u)
            x, y, xT = sc.sb("x", [P, NT, D]), sc.sb("y", [P, NT, D]), sc.sb("xT", [P, DC, S])
            lg, mx = sc.sb("logits", [P, NT, E]), sc.sb("top", [P, NT, 8])
            ix, ixf = sc.sb("index", [P, NT, 8], U32), sc.sb("indexf", [P, NT, 2])
            oh = sc.sb("onehot", [P, NT, 2, E])
            diff, wt = sc.sb("diff", [P, NT, 2]), sc.sb("weight", [P, NT, 2])
            coef = sc.sb("coef", [P, NT, 2, E])
            hm, hT = sc.sb("h", [P, 2, 2, NT, ER]), sc.sb("hT", [P, 2, 2, S])
            sg, a = sc.sb("silu", [P, 3, S]), sc.sb("act", [P, FC, 2, S])
            z, zz, zT = sc.sb("z", [P, NT, ER]), sc.sb("zz", [P, NT, ER]), sc.sb("zT", [P, S])
            banks = sc.part(u)
            L = NormTiles(sc)
            (s_x, s_xT, s_xTs, s_proj, s_hm, s_hT, s_hTs, s_gu, s_silu, s_act, s_down, s_z, s_zT, s_zTs, s_added, s_lo, s_dve, s_diff, s_wt,
             s_ln, s_st) = (sc.sem(n) for n in ("x xT xTs proj hm hT hTs gu silu act down z zT zTs added lo dve diff wt ln st").split())

            def sync(sp, b):
                sp.dma_start(x[:, :, :], rows(x_in, b)).then_inc(s_x, 16)
                yield
                sp.wait_ge(s_ln, 1)
                sp.dma_start(rows(x_out, b), y[:, :, :]).then_inc(s_st, 16)
                yield
                sp.wait_ge(s_st, 16)

            def gpsimd(pool, b):
                yield from norm_powers(nc, pool, L, range(NT))

            def tensor(pe, b):
                pe.wait_ge(s_x, 16)
                for c in range(DC):
                    for t in range(NT):
                        ins = nc.tensor.transpose(banks[0][:, c * S + t * P:c * S + (t + 1) * P],
                                                  x[:, t, c * P:(c + 1) * P], ident[:, :])
                ins.then_inc(s_xT, 1)
                yield
                pe.wait_ge(s_xTs, 1)
                for t in range(NT):
                    for bank, w, n in ((banks[1], gateT, E), (banks[2], a13T, 2 * ER)):
                        for c in range(DC):
                            ins = nc.tensor.matmul(bank[:, t * n:(t + 1) * n], xT[:, c, t * P:(t + 1) * P], w[:, c, :],
                                                   start=(c == 0), stop=(c == DC - 1))
                ins.then_inc(s_proj, 1)
                yield
                pe.wait_ge(s_hm, 1)
                for k in range(2):
                    for m in range(2):
                        for t in range(NT):
                            ins = nc.tensor.transpose(banks[3 - 3 * k][:, m * S + t * P:m * S + (t + 1) * P],
                                                      hm[:, k, m, t, :], ident[:, :])
                    ins.then_inc(s_hT, 1)
                    yield
                pe.wait_ge(s_hTs, 2)
                for n in range(2 * FC):
                    f, k = n // 2, n % 2
                    if n >= 2:
                        pe.wait_ge(s_act, n - 1)
                    for m, (w, bT) in enumerate(((wgT, b1T), (wuT, b3T))):
                        o = banks[1 + n % 2][:, m * S:(m + 1) * S]
                        for c in range(DC):
                            nc.tensor.matmul(o, w[:, c, f * P:(f + 1) * P], xT[:, c, :], start=(c == 0), stop=False)
                        ins = nc.tensor.matmul(o, bT[:, f * P:(f + 1) * P], hT[:, k, m, :], start=False, stop=True)
                    ins.then_inc(s_gu, 1)
                    yield
                pe.wait_ge(s_act, 2 * FC)
                for k in range(2):
                    for t in range(NT):
                        for f in range(FC):
                            ins = nc.tensor.matmul(banks[2 * k + t][:, 0:WD], a[:, f, k, t * P:(t + 1) * P], wdT[:, f, :],
                                                   start=(f == 0), stop=(f == FC - 1))
                        ins.then_inc(s_down, 1)
                        yield
                pe.wait_ge(s_z, 1)
                for t in range(NT):
                    ins = nc.tensor.transpose(banks[t][:, WD:WD + P], z[:, t, :], ident[:, :])
                ins.then_inc(s_zT, 1)
                yield
                pe.wait_ge(s_zTs, 1)
                pe.wait_ge(s_added, 1)
                for t in range(NT):
                    ins = nc.tensor.matmul(banks[2 + t][:, 0:D], zT[:, t * P:(t + 1) * P], b2T[:, :],
                                           start=True, stop=True)
                ins.then_inc(s_lo, 1)
                yield

            def scalar(act, b):
                act.wait_ge(s_diff, 1)
                nc.scalar.activation(wt[:, :, :], diff[:, :, :], ACT.Sigmoid).then_inc(s_wt, 1)
                yield
                for n in range(2 * FC):
                    act.wait_ge(s_gu, n + 1)
                    if n >= 3:
                        act.wait_ge(s_act, n - 2)
                    nc.scalar.activation(sg[:, n % 3, :], banks[1 + n % 2][:, 0:S], ACT.Silu).then_inc(s_silu, 1)
                    yield

            def vector(dve, b):
                link = Chain(dve, s_dve)
                L.asked = 0
                dve.wait_ge(s_xT, 1)
                nc.vector.tensor_copy(xT[:, :, :], banks[0][:, :].rearrange("p (c s) -> p c s", c=DC)).then_inc(s_xTs, 1)
                yield
                dve.wait_ge(s_proj, 1)
                yield from link(nc.vector.tensor_copy(lg[:, :, :], banks[1][:, 0:NT * E].rearrange("p (t e) -> p t e", t=NT)))
                for t in range(NT):
                    yield from top2(nc, dve, link, lg, mx, ix, ixf, iota, oh, t, SCALE)
                nc.vector.tensor_tensor(diff[:, :, 0:1], mx[:, :, 0:1], mx[:, :, 1:2], ALU.subtract)
                nc.vector.tensor_tensor(diff[:, :, 1:2], mx[:, :, 1:2], mx[:, :, 0:1], ALU.subtract).then_inc(s_diff, 1)
                yield
                for t in range(NT):
                    for k in range(2):
                        for m in range(2):
                            ins = nc.vector.tensor_tensor(
                                hm[:, k, m, t, :].rearrange("p (e r) -> p e r", e=E),
                                banks[2][:, t * 2 * ER + m * ER:t * 2 * ER + (m + 1) * ER].rearrange("p (e r) -> p e r", e=E),
                                oh[:, t, k, :].unsqueeze(2).broadcast_to([P, E, R]), ALU.mult)
                ins.then_inc(s_hm, 1)
                yield
                dve.wait_ge(s_wt, 1)
                for t in range(NT):
                    for k in range(2):
                        ins = nc.vector.tensor_scalar(coef[:, t, k, :], oh[:, t, k, :], wt[:, t, k:k + 1], None, ALU.mult)
                yield from link(ins)
                for k in range(2):
                    dve.wait_ge(s_hT, k + 1)
                    nc.vector.tensor_copy(hT[:, k, :, :], banks[3 - 3 * k][:, :].rearrange("p (m s) -> p m s", m=2)).then_inc(s_hTs, 1)
                    yield
                for n in range(2 * FC):
                    dve.wait_ge(s_silu, n + 1)
                    nc.vector.tensor_tensor(a[:, n // 2, n % 2, :], sg[:, n % 3, :], banks[1 + n % 2][:, S:2 * S],
                                            ALU.mult).then_inc(s_act, 1)
                    yield
                dve.wait_ge(s_down, 4)
                for t in range(NT):
                    for k in range(2):
                        yield from link(nc.vector.tensor_tensor(
                            (z, zz)[k][:, t, :].rearrange("p (e r) -> p e r", e=E),
                            banks[2 * k + t][:, D:WD].rearrange("p (e r) -> p e r", e=E),
                            coef[:, t, k, :].unsqueeze(2).broadcast_to([P, E, R]), ALU.mult))
                nc.vector.tensor_tensor(z[:, :, :], z[:, :, :], zz[:, :, :], ALU.add).then_inc(s_z, 1)
                yield
                dve.wait_ge(s_zT, 1)
                for t in range(NT):
                    ins = nc.vector.tensor_copy(zT[:, t * P:(t + 1) * P], banks[t][:, WD:WD + P])
                ins.then_inc(s_zTs, 1)
                yield
                for k in range(2):
                    for t in range(NT):
                        ins = nc.vector.scalar_tensor_tensor(x[:, t, :], banks[2 * k + t][:, 0:D], wt[:, t, k:k + 1],
                                                             x[:, t, :], ALU.mult, ALU.add)
                        if (k, t) != (1, NT - 1):
                            yield from link(ins)
                ins.then_inc(s_added, 1)
                yield
                dve.wait_ge(s_added, 1)
                dve.wait_ge(s_lo, 1)
                for t in range(NT):
                    yield from link(nc.vector.tensor_tensor(x[:, t, :], x[:, t, :], banks[2 + t][:, 0:D], ALU.add))
                    yield from layer_norm(nc, dve, link, x[:, t, :], y[:, t, :], L, t)
                nc.vector.engine_nop().then_inc(s_ln, 1)
                yield

            return dict(sync=sync, gpsimd=gpsimd, tensor=tensor, scalar=scalar, vector=vector)

        run_streams(nc, sc, [stream(u) for u in range(STREAMS)])


RPE = 63
HALF = RPE // 2
GR = 32
NG = S // GR
BW = 128
WIN = GR + 2 * HALF


def window(g):
    lo, hi = GR * g - HALF, GR * g - HALF + WIN
    return max(lo, 0), min(hi, S), max(lo, 0) - lo


def edge_rows(t):
    rows = []
    for side in range(2):
        for edge in range(2):
            same = {}
            for g in (range(4 * t, 4 * t + 4) if side == 0 else range(NG)):
                lo, hi = GR * g - HALF, GR * g - HALF + WIN
                r = (0, max(lo, 0)) if edge == 0 else (min(hi, S), S)
                if side == 1:
                    r = (max(r[0], t * P), min(r[1], (t + 1) * P))
                if r[0] < r[1]:
                    same.setdefault(r if side else (g, r), []).append(g)
            for key, gs in same.items():
                rows.append((side, edge, gs, key if side else key[1]))
    assert len(rows) <= 16
    return rows


def shape_constants():
    qmask, qadd = np.zeros((P, NT, P), np.float32), np.zeros((P, NT, P), np.float32)
    kmask, kadd = np.zeros((P, NT, S), np.float32), np.zeros((P, NT, S), np.float32)
    for a in range(4):
        for t in range(NT):
            qmask[32 * a:32 * a + 16, t] = kmask[32 * a:32 * a + 16, t] = 1.0
            for n, (side, edge, gs, (lo, hi)) in enumerate(edge_rows(t)):
                r = 32 * a + 16 + n
                for g in gs:
                    if side == 0:
                        qmask[r, t, GR * g - t * P:GR * (g + 1) - t * P] = 1.0
                        kadd[r, t, lo:hi] = 1.0
                    else:
                        kmask[r, t, GR * g:GR * (g + 1)] = 1.0
                        qadd[r, t, lo - t * P:hi - t * P] = 1.0
    slots = np.zeros((P, P), np.float32)
    edges = np.zeros((P, NT, NT, 8), np.float32)
    own = np.zeros((P, NT, 8), np.float32)
    for p in range(P):
        slots[p, p] = p % 32 < 16
        for t in range(NT):
            i = t * P + p
            own[p, t, p // GR] = own[p, t, 4 + p // GR] = 1.0
            for g in range(NG):
                edges[p, t, g // 4, g % 4] = i < GR * g - HALF
                edges[p, t, g // 4, 4 + g % 4] = i >= GR * g - HALF + WIN
    return {"qmask": qmask, "qadd": qadd, "kmask": kmask, "kadd": kadd, "slots": slots, "edges": edges, "own": own}


def skewed(scratch, g, h0, nh, transposed_t=None):
    lo, hi, cut = window(g)
    base = scratch[h0:h0 + nh, GR * g:GR * (g + 1), 0:hi - lo].rearrange("h p n -> p h n")
    return bass.AP(tensor=base.tensor, offset=base.offset + HALF + cut,
                   ap=[[BW - 1, GR], [S * BW, nh], [1, hi - lo]])


def self_attention_1(nc, x_in, x_out, W):
    DK = D // H
    BLK = H // 4
    with stage(nc, "sa1") as sc:
        ident = sc.sb("ident", [P, P])
        make_identity(nc, sc, ident)
        eqs = [nc.dram_tensor(f"rpe_q_rows{u}", (H, S, BW), F32, kind="Internal").ap() for u in range(STREAMS)]
        eks = [nc.dram_tensor(f"rpe_k_rows{u}", (H, S, BW), F32, kind="Internal").ap() for u in range(STREAMS)]
        ess = [nc.dram_tensor(f"rpe_sums{u}", (H, S, BW), F32, kind="Internal").ap() for u in range(STREAMS)]
        qwT, kwT = sc.sb("qwT", [P, DC, H * 32]), sc.sb("kwT", [P, DC, H * 32])
        vwT, pwT, pb = sc.sb("vwT", [P, DC, D]), sc.sb("pwT", [P, DC, D]), sc.sb("pb", [1, D])
        qmask, qadd = sc.sb("qmask", [P, NT, P]), sc.sb("qadd", [P, NT, P])
        kmask, kadd = sc.sb("kmask", [P, NT, S]), sc.sb("kadd", [P, NT, S])
        own, slots, edges = sc.sb("own", [P, NT, 8]), sc.sb("slots", [P, P]), sc.sb("edges", [P, NT, NT, 8])
        tq, tk = sc.sb("tq", [P, BLK, RPE]), sc.sb("tk", [P, BLK, RPE])
        tqx, tkx = sc.sb("tqx", [P, BLK, BW]), sc.sb("tkx", [P, BLK, BW])
        extq, extk = sc.sb("extq", [P, NT, BLK, P]), sc.sb("extk", [P, NT, BLK, P])
        VC = DK + 8
        rvx, rve = sc.sb("rvx", [P, H, VC]), sc.sb("rve", [P, 2, H, DK])
        zero = sc.sb("zero", [P, 2 * BW])
        WH = 4
        bqs, bks = ([sc.sb(f"{n}{u}", [P, NT, WH, S]) for u in range(STREAMS)] for n in ("bq", "bk"))
        with ExitStack() as raw_ctx:
            raw = lambda name, shape: raw_ctx.enter_context(nc.sbuf_tensor(f"sa1_raw_{name}", shape, F32))
            qw_r, kw_r = raw("qw", [P, BLK, D]), raw("kw", [P, BLK, D])
            vw_r, pw_r = raw("vw", [P, DC, D]), raw("pw", [P, DC, D])
            loads = []
            for blk in range(BLK):
                for a in range(4):
                    h = 4 * blk + a
                    for part, r in enumerate((qw_r, kw_r)):
                        loads.append((r[32 * a:32 * a + DK, blk, :], W["L1_attn_w_qkv"][part * D + h * DK:part * D + (h + 1) * DK, :]))
                    loads += [(tq[32 * a:32 * a + DK, blk, :], W["L1_attn_rpe_k_table"][h, :, :]),
                              (tk[32 * a:32 * a + DK, blk, :], W["L1_attn_rpe_q_table"][h, :, :])]
            loads += [(vw_r[:, :, :], W["L1_attn_w_qkv"][2 * D:3 * D, :].rearrange("(c p) d -> p c d", p=P)),
                      (pw_r[:, :, :], W["L1_attn_w_proj"].rearrange("(c p) d -> p c d", p=P)),
                      (pb[:, :], W["L1_attn_b_proj"].rearrange("(a n) -> a n", a=1))]
            for n, dst in (("qmask", qmask), ("qadd", qadd), ("kmask", kmask), ("kadd", kadd), ("own", own)):
                loads.append((dst[:, :, :], W["const_" + n]))
            loads.append((edges[:, :, :, :], W["const_edges"]))
            loads.append((slots[:, :], W["const_slots"]))
            rv = W["L1_attn_rpe_v_table"].rearrange("h m d -> m h d")
            loads += [(rvx[0:GR, :, 0:DK], rv[0:1, :, :].broadcast_to([GR, H, DK])),
                      (rvx[GR:GR + RPE - 2, :, 0:DK], rv[1:RPE - 1, :, :]),
                      (rvx[GR + RPE - 2:P, :, 0:DK], rv[RPE - 1:RPE, :, :].broadcast_to([P - GR - RPE + 2, H, DK])),
                      (rve[:, 0, :, :], rv[0:1, :, :].broadcast_to([P, H, DK])),
                      (rve[:, 1, :, :], rv[RPE - 1:RPE, :, :].broadcast_to([P, H, DK]))]
            for h in range(H):
                loads += [(es[h, :, :].rearrange("(p r) n -> p (r n)", p=P), zero[:, :]) for es in ess]
            turned = []
            for c in range(DC):
                for blk in range(BLK):
                    turned += [(qw_r[:, blk, c * P:(c + 1) * P], qwT[:, c, blk * P:(blk + 1) * P]),
                               (kw_r[:, blk, c * P:(c + 1) * P], kwT[:, c, blk * P:(blk + 1) * P])]
                for o in range(DC):
                    turned += [(vw_r[:, o, c * P:(c + 1) * P], vwT[:, c, o * P:(o + 1) * P]),
                               (pw_r[:, o, c * P:(c + 1) * P], pwT[:, c, o * P:(o + 1) * P])]
            load_weights(nc, sc, ident, [qw_r[:, :, :], kw_r[:, :, :], tq[:, :, :], tk[:, :, :], zero[:, :],
                                         rvx[:, :, :], extq[:, :, :, :], extk[:, :, :, :]]
                         + [t[:, :, :, :] for t in bqs + bks], loads, turned)
        ones, vxs = sc.sb("ones", [1, P]), [sc.sb(f"vx{u}", [P, NT, NT, H, VC]) for u in range(STREAMS)]
        s_t, s_o1 = sc.sem("tables"), sc.sem("ones")
        with nc.Block() as block:
            @block.gpsimd
            def _(pool):
                nc.gpsimd.memset(ones[:, :], 1.0).then_inc(s_o1, 1)
                pool.wait_ge(s_o1, 1)

            @block.vector
            def _(dve):
                link = Chain(dve, s_t)
                drain(link(nc.vector.tensor_scalar(tk[:, :, :], tk[:, :, :], DK ** -0.5, None, ALU.mult)))
                for t, x in ((tq, tqx), (tk, tkx)):
                    drain(link(nc.vector.tensor_copy(x[:, :, 0:GR], t[:, :, 0:1].broadcast_to([P, BLK, GR]))))
                    drain(link(nc.vector.tensor_copy(x[:, :, GR:GR + RPE - 2], t[:, :, 1:RPE - 1])))
                    drain(link(nc.vector.tensor_copy(x[:, :, GR + RPE - 2:BW], t[:, :, RPE - 1:RPE].broadcast_to([P, BLK, BW - GR - RPE + 2]))))
                for t in range(NT):
                    for blk in range(BLK):
                        drain(link(nc.vector.tensor_copy(extq[:, t, blk, :], slots[:, :])))
                        drain(link(nc.vector.tensor_copy(extk[:, t, blk, :], slots[:, :])))
                        for n, (side, edge, _, _) in enumerate(edge_rows(t)):
                            src, dst = ((tq, extq), (tk, extk))[side]
                            m = edge * (RPE - 1)
                            for a in range(4):
                                drain(link(nc.vector.tensor_copy(dst[32 * a:32 * a + DK, t, blk, 32 * a + 16 + n:32 * a + 17 + n],
                                                           src[32 * a:32 * a + DK, blk, m:m + 1])))
                for vx in vxs:
                    for jt in range(NT):
                        for t in range(NT):
                            drain(link(nc.vector.tensor_copy(vx[:, jt, t, :, DK:VC], edges[:, jt, t, :].unsqueeze(1).broadcast_to([P, H, 8]))))
        def stream(u):
            sc.part(u)
            x, y, xT = sc.sb("x", [P, NT, D]), sc.sb("y", [P, NT, D]), sc.sb("xT", [P, DC, S])
            qT, kT = sc.sb("qT", [P, BLK, S]), sc.sb("kT", [P, BLK, S])
            qE, kE = sc.sb("qE", [P, BLK, NT, P]), sc.sb("kE", [P, BLK, NT, S])
            tmp = sc.sb("tmp", [P, 2, 2 * S])
            er = sc.sb("er", [P, 4, NT, BW])
            E = sc.sb("E", [P, 4, NT, S])
            WR = 6
            wT = sc.sb("wT", [P, WR, NT, S])
            top, sums, rs = sc.sb("max", [P, H, NT]), sc.sb("sums", [P, H, NT]), sc.sb("rs", [P, H, NT])
            sr = er
            srT, o_sb, oT = qT[:, 0:2, :], qT[:, 2:4, :], kT[:, 0:2, :]
            outside, pair = kT[:, 2:4, :].rearrange("p t (h d) -> p t h d", h=H), sc.sb("pair", [P, NT, H, 2])
            AH = H // 2
            av = tmp[:, :, :].rearrange("p a b -> p (a b)")[:, 0:NT * H * VC].rearrange("p (t h k) -> p t h k", t=NT, h=H)
            banks = sc.part(u)
            bq, bk, vx, eq, ek, es = bqs[u], bks[u], vxs[u], eqs[u], eks[u], ess[u]
            L = NormTiles(sc)
            (s_x, s_xT, s_xTs, s_pr, s_prs, s_ext, s_tmp, s_exts, s_row, s_rows, s_sc, s_max, s_exp, s_tr, s_wT, s_av, 
              s_st1, s_srT, s_half, s_o, s_oT, s_oTs, s_y, s_dve, s_ln, s_st) = (sc.sem(n) for n in (
                 "x xT xTs pr prs ext tmp exts row rows sc max exp tr wT av st1 srT half o oT oTs y dve ln st").split())
            s_sw, s_sr = ([sc.sem(f"{n}{i}") for i in range(2)] for n in ("sw", "sr"))
            s_win = [sc.sem(f"win{i}") for i in range(H // WH)]
            s_bw = [sc.sem(f"bw{i}") for i in range(4)]
            LAG = 5
            proj = [(dst, w, i) for dst, w in ((qT, qwT), (kT, kwT)) for i in range(BLK // 2)]
            exts = [("q", 0, 0), ("q", 0, 1)] + [("k", t, i) for t in range(NT) for i in range(BLK // 2)]

            def sync(sp, b):
                sp.dma_start(x[:, :, :], rows(x_in, b)).then_inc(s_x, 16)
                yield
                for n in range(2 * H):
                    h, dst = n // 2, (eq, ek)[n % 2]
                    sp.wait_ge(s_rows, n + 1)
                    sp.dma_start(dst[h, :, :].rearrange("(t p) n -> p t n", p=P), er[:, n % 4, :, :]).then_inc(s_bw[n % 4], 16)
                    yield
                for slot in range(4):
                    sp.wait_ge(s_bw[slot], 16 * H * 2 // 4)

                def load_windows(part):
                    for src, dst in ((eq, bq), (ek, bk)):
                        for g in range(NG):
                            lo, hi, _ = window(g)
                            p0 = GR * (g % 4)
                            sp.dma_start(dst[p0:p0 + GR, g // 4, :, lo:hi], skewed(src, g, WH * part, WH))\
                              .then_inc(s_win[part], 16)
                            yield

                yield from load_windows(0)
                for p in range(H // 2):
                    if 2 * (p + 1) % WH == 0 and 2 * (p + 1) < H:
                        sp.wait_ge(s_max, 2 * (p + 1))
                        yield from load_windows((2 * p + 2) // WH)
                    sp.wait_ge(s_exp, 2 * p + 2)
                    e0 = 2 * p % 4
                    for g in range(NG):
                        lo, hi, _ = window(g)
                        p0 = GR * (g % 4)
                        sp.dma_start(skewed(es, g, 2 * p, 2), E[p0:p0 + GR, e0:e0 + 2, g // 4, lo:hi]).then_inc(s_sw[p % 2], 16)
                        yield
                    sp.wait_ge(s_sw[p % 2], 16 * NG * (p // 2 + 1))
                    if p >= 2:
                        sp.wait_ge(s_st1, 2 * (p - 1))
                    sp.dma_start(sr[:, e0:e0 + 2, :, :], es[2 * p:2 * p + 2, :, :].rearrange("h (t p) n -> p h t n", p=P))\
                      .then_inc(s_sr[p % 2], 16)
                    yield
                sp.wait_ge(s_ln, 1)
                sp.dma_start(rows(x_out, b), y[:, :, :]).then_inc(s_st, 16)
                yield
                sp.wait_ge(s_st, 16)

            def gpsimd(pool, b):
                yield from norm_powers(nc, pool, L, range(NT))

            def tensor(pe, b):
                pe.wait_ge(s_x, 16)
                for c in range(DC):
                    for t in range(NT):
                        ins = nc.tensor.transpose(banks[0][:, c * S + t * P:c * S + (t + 1) * P],
                                                  x[:, t, c * P:(c + 1) * P], ident[:, :])
                ins.then_inc(s_xT, 1)
                yield
                pe.wait_ge(s_xTs, 1)
                for t in range(NT):
                    for c in range(DC):
                        ins = nc.tensor.matmul(banks[2][:, t * D:(t + 1) * D], xT[:, c, t * P:(t + 1) * P], vwT[:, c, :],
                                               start=(c == 0), stop=(c == DC - 1))
                ins.then_inc(s_pr, 1)
                yield
                for n, (dst, w, i) in enumerate(proj):
                    if n >= 2:
                        pe.wait_ge(s_prs, n)
                    for k in range(2):
                        blk = 2 * i + k
                        for c in range(DC):
                            ins = nc.tensor.matmul(banks[3 - 2 * (n % 2)][:, k * S:(k + 1) * S], w[:, c, blk * P:(blk + 1) * P],
                                                   xT[:, c, :], start=(c == 0), stop=(c == DC - 1))
                    ins.then_inc(s_pr, 1)
                    yield
                pe.wait_ge(s_prs, 1 + len(proj))
                for n in range(2 * H):
                    h, src, table = n // 2, (qT, kT)[n % 2], (tqx, tkx)[n % 2]
                    a, blk = h % 4, h // 4
                    if n >= 2:
                        pe.wait_ge(s_rows, n - 1)
                    for t in range(NT):
                        ins = nc.tensor.matmul(banks[2 + n % 2][:, t * BW:(t + 1) * BW], src[32 * a:32 * a + DK, blk, t * P:(t + 1) * P],
                                               table[32 * a:32 * a + DK, blk, :], start=True, stop=True)
                    ins.then_inc(s_row, 1)
                    yield
                for n, (side, t, i) in enumerate(exts):
                    if n >= 2:
                        pe.wait_ge(s_tmp, n - 1)
                    for k in range(2):
                        blk = 2 * i + k
                        if side == "q":
                            for tt in range(NT):
                                ins = nc.tensor.matmul(banks[n % 2][:, k * S + tt * P:k * S + (tt + 1) * P], extq[:, tt, blk, :],
                                                       qT[:, blk, tt * P:(tt + 1) * P], start=True, stop=True)
                        else:
                            ins = nc.tensor.matmul(banks[n % 2][:, k * S:(k + 1) * S], extk[:, t, blk, :], kT[:, blk, :],
                                                   start=True, stop=True)
                    ins.then_inc(s_ext, 1)
                    yield
                pe.wait_ge(s_exts, len(exts))
                pe.wait_ge(s_rows, 2 * H)
                for n in range(H + LAG):
                    if n < H:
                        pe.wait_ge(s_win[n // WH], 16 * 2 * NG)
                        if n >= 1:
                            pe.wait_ge(s_max, n)
                        a, blk = n % 4, n // 4
                        for t in range(NT):
                            o = banks[0][:, t * S:(t + 1) * S]
                            nc.tensor.matmul(o, qE[32 * a:32 * a + 32, blk, t, :], kE[32 * a:32 * a + 32, blk, t, :],
                                             start=True, stop=False)
                            for jt in range(NT):
                                ins = nc.tensor.matmul(o[:, jt * P:(jt + 1) * P], bk[:, jt, n % WH, t * P:(t + 1) * P], ident[:, :],
                                                       start=False, stop=(jt == NT - 1))
                        ins.then_inc(s_sc, 1)
                        yield
                    if 1 <= n <= H:
                        m = n - 1
                        pe.wait_ge(s_exp, m + 1)
                        if m >= 1:
                            pe.wait_ge(s_wT, m)
                        for jt in range(NT):
                            for t in range(NT):
                                ins = nc.tensor.transpose(banks[1][:, jt * S + t * P:jt * S + (t + 1) * P],
                                                          E[:, m % 4, t, jt * P:(jt + 1) * P], ident[:, :])
                        ins.then_inc(s_tr, 1)
                        yield
                    if n >= LAG - 1 and n - LAG + 1 < H:
                        m = n - LAG + 1
                        pe.wait_ge(s_sr[(m // 2) % 2], 16 * (m // 4 + 1))
                        if m >= 1:
                            pe.wait_ge(s_srT, m)
                        for t in range(NT):
                            ins = nc.tensor.transpose(banks[3][:, t * P:(t + 1) * P], sr[:, m % 4, t, :], ident[:, :])
                        ins.then_inc(s_st1, 1)
                        yield
                    if n >= LAG:
                        m = n - LAG
                        pe.wait_ge(s_wT, m + 1)
                        pe.wait_ge(s_srT, m + 1)
                        if m == AH:
                            pe.wait_ge(s_half, 1)
                        for t in range(NT):
                            o = banks[2][:, (t * AH + m % AH) * VC:(t * AH + m % AH + 1) * VC]
                            for jt in range(NT):
                                nc.tensor.matmul(o, wT[:, m % WR, jt, t * P:(t + 1) * P], vx[:, jt, t, m, :], start=(jt == 0), stop=False)
                            ins = nc.tensor.matmul(o, srT[:, m % 2, t * P:(t + 1) * P], rvx[:, m, :], start=False, stop=True)
                        ins.then_inc(s_av, 1)
                        yield
                pe.wait_ge(s_o, 1)
                for c in range(DC):
                    for t in range(NT):
                        ins = nc.tensor.transpose(banks[0][:, c * S + t * P:c * S + (t + 1) * P],
                                                  o_sb[:, t, c * P:(c + 1) * P], ident[:, :])
                ins.then_inc(s_oT, 1)
                yield
                pe.wait_ge(s_oTs, 1)
                for t in range(NT):
                    o = banks[1][:, t * D:(t + 1) * D]
                    for c in range(DC):
                        nc.tensor.matmul(o, oT[:, c, t * P:(t + 1) * P], pwT[:, c, :], start=(c == 0), stop=False)
                    ins = nc.tensor.matmul(o, ones[0:1, :], pb[0:1, :], start=False, stop=True)
                ins.then_inc(s_y, 1)
                yield

            def scalar(act, b):
                for n in range(2 * H):
                    act.wait_ge(s_row, n + 1)
                    if n >= 4:
                        act.wait_ge(s_bw[n % 4], 16 * (n // 4))
                    nc.scalar.copy(er[:, n % 4, :, :], banks[2 + n % 2][:, 0:NT * BW].rearrange("p (t n) -> p t n", t=NT))\
                        .then_inc(s_rows, 1)
                    yield
                for n in range(H):
                    act.wait_ge(s_max, n + 1)
                    for t in range(NT):
                        ins = nc.scalar.activation(E[:, n % 4, t, :], E[:, n % 4, t, :], ACT.Exp, bias=top[:, n, t:t + 1],
                                                   scale=1.0, accum_out=sums[:, n, t:t + 1])
                    ins.then_inc(s_exp, 1)
                    yield

            def vector(dve, b):
                link = Chain(dve, s_dve)
                L.asked = 0
                dve.wait_ge(s_xT, 1)
                nc.vector.tensor_copy(xT[:, :, :], banks[0][:, :].rearrange("p (c s) -> p c s", c=DC)).then_inc(s_xTs, 1)
                yield
                dve.wait_ge(s_pr, 1)
                for jt in range(NT):
                    for t in range(NT):
                        ins = nc.vector.tensor_copy(vx[:, jt, t, :, 0:DK], banks[2][:, jt * D:(jt + 1) * D].rearrange("p (h d) -> p h d", h=H))
                ins.then_inc(s_prs, 1)
                yield
                for n, (dst, w, i) in enumerate(proj):
                    dve.wait_ge(s_pr, n + 2)
                    out, bank = dst[:, 2 * i:2 * i + 2, :], banks[3 - 2 * (n % 2)][:, :].rearrange("p (k s) -> p k s", k=2)
                    if dst is qT:
                        nc.vector.tensor_scalar(out, bank, DK ** -0.5, None, ALU.mult).then_inc(s_prs, 1)
                        yield
                    else:
                        nc.vector.tensor_copy(out, bank).then_inc(s_prs, 1)
                        yield
                for n, (side, t, i) in enumerate(exts):
                    dve.wait_ge(s_ext, n + 1)
                    half = tmp[:, n % 2, :].rearrange("p (k s) -> p k s", k=2)
                    if side == "q":
                        mask, add = (m[:, :, :].rearrange("p t s -> p (t s)") for m in (qmask, qadd))
                        dst = qE[:, 2 * i:2 * i + 2, :, :].rearrange("p k t s -> p k (t s)")
                    else:
                        mask, add = kmask[:, t, :], kadd[:, t, :]
                        dst = kE[:, 2 * i:2 * i + 2, t, :]
                    nc.vector.tensor_tensor(half, banks[n % 2][:, :].rearrange("p (k s) -> p k s", k=2),
                                            mask.unsqueeze(1).broadcast_to([P, 2, S]), ALU.mult).then_inc(s_tmp, 1)
                    yield
                    dve.wait_ge(s_tmp, n + 1)
                    nc.vector.tensor_tensor(dst, half, add.unsqueeze(1).broadcast_to([P, 2, S]), ALU.add).then_inc(s_exts, 1)
                    yield

                def sum_rows(m):
                    dve.wait_ge(s_st1, m + 1)
                    if m >= 2:
                        dve.wait_ge(s_av, m - 1)
                    nc.vector.tensor_copy(srT[:, m % 2, :], banks[3][:, 0:S]).then_inc(s_srT, 1)
                    yield

                def heads_out(g):
                    dve.wait_ge(s_av, AH * (g + 1))
                    nc.vector.tensor_copy(av[:, :, AH * g:AH * (g + 1), :],
                                          banks[2][:, 0:NT * AH * VC].rearrange("p (t h k) -> p t h k", t=NT, h=AH)).then_inc(s_half, 1)
                    yield

                for n in range(H + LAG):
                    if n == AH + LAG:
                        yield from heads_out(0)
                    if n < H:
                        dve.wait_ge(s_sc, n + 1)
                        dve.wait_ge(s_win[n // WH], 16 * 2 * NG)
                        if n >= 4:
                            dve.wait_ge(s_tr, n - 3)
                            p = (n - 4) // 2
                            dve.wait_ge(s_sw[p % 2], 16 * NG * (p // 2 + 1))
                        for t in range(NT):
                            ins = nc.vector.tensor_tensor_reduce(
                                out=E[:, n % 4, t, :], in0=banks[0][:, t * S:(t + 1) * S], in1=bq[:, t, n % WH, :],
                                scale=1.0, scalar=-3.0e38, op0=ALU.add, op1=ALU.max, accum_out=top[:, n, t:t + 1])
                        yield from link(ins)
                        nc.vector.tensor_scalar(top[:, n, :], top[:, n, :], -1.0, None, ALU.mult).then_inc(s_max, 1)
                        yield
                    if 1 <= n <= H:
                        m = n - 1
                        dve.wait_ge(s_tr, m + 1)
                        if m >= WR:
                            dve.wait_ge(s_av, m - WR + 1)
                        nc.vector.tensor_copy(wT[:, m % WR, :, :], banks[1][:, :].rearrange("p (j k) -> p j k", j=NT))\
                            .then_inc(s_wT, 1)
                        yield
                    if n >= LAG - 1 and n - LAG + 1 < H:
                        yield from sum_rows(n - LAG + 1)
                dve.wait_ge(s_exp, H)
                yield from link(nc.vector.reciprocal(rs[:, :, :], sums[:, :, :]))
                yield from heads_out(1)
                dve.wait_ge(s_half, 2)
                v3 = lambda ap: ap.rearrange("p (h d) -> p h d", h=H)
                for t in range(NT):
                    heads = av[:, t, :, :]
                    yield from link(nc.vector.tensor_tensor(outside[:, t, :, 0:8], heads[:, :, DK:VC],
                                                 own[:, t, :].unsqueeze(1).broadcast_to([P, H, 8]), ALU.mult))
                    yield from link(nc.vector.tensor_reduce(pair[:, t, :, :], outside[:, t, :, 0:8].rearrange("p h (e g) -> p h e g", e=2),
                                                 AX.X, ALU.add))
                    yield from link(nc.vector.tensor_copy(v3(o_sb[:, t, :]), heads[:, :, 0:DK]))
                    for e in range(2):
                        yield from link(nc.vector.tensor_tensor(outside[:, t, :, :], rve[:, e, :, :],
                                                     pair[:, t, :, e:e + 1].broadcast_to([P, H, DK]), ALU.mult))
                        yield from link(nc.vector.tensor_tensor(v3(o_sb[:, t, :]), v3(o_sb[:, t, :]), outside[:, t, :, :], ALU.add))
                    ins = nc.vector.tensor_tensor(v3(o_sb[:, t, :]), v3(o_sb[:, t, :]),
                                                  rs[:, :, t:t + 1].broadcast_to([P, H, DK]), ALU.mult)
                ins.then_inc(s_o, 1)
                yield
                dve.wait_ge(s_oT, 1)
                nc.vector.tensor_copy(oT[:, :, :], banks[0][:, :].rearrange("p (c s) -> p c s", c=DC)).then_inc(s_oTs, 1)
                yield
                dve.wait_ge(s_y, 1)
                for t in range(NT):
                    yield from link(nc.vector.tensor_tensor(x[:, t, :], x[:, t, :], banks[1][:, t * D:(t + 1) * D], ALU.add))
                    yield from layer_norm(nc, dve, link, x[:, t, :], y[:, t, :], L, t)
                nc.vector.engine_nop().then_inc(s_ln, 1)
                yield

            return dict(sync=sync, gpsimd=gpsimd, tensor=tensor, scalar=scalar, vector=vector)

        run_streams(nc, sc, [stream(u) for u in range(STREAMS)])


def cross_attention_1(nc, x_in, x_out, W):
    DH, LAMBDA_INIT = D // H, 0.8
    HQ = 2 * DH
    BLK = H // 4
    with stage(nc, "xa1") as sc:
        ident = sc.sb("ident", [P, P])
        make_identity(nc, sc, ident)
        qw, kw = sc.sb("qw", [P, DC, 2 * H * 32]), sc.sb("kw", [P, DC, 2 * H * 32])
        vw, ow = sc.sb("vw", [P, DC, D]), sc.sb("ow", [P, DC, D])
        lam_in = sc.sb("lambda_in", [P, 4, H, DH])
        rms_w = sc.sb("rms_scale", [P, DH])
        kMs = [sc.sb(f"kM{u}", [P, 2 * H, S]) for u in range(STREAMS)]
        loads = []
        for dst, src in ((qw, W["L1_xattn_W_q"]), (kw, W["L1_xattn_W_k"])):
            for part in range(2):
                loads += padded_heads(dst[:, :, part * H * 32:(part + 1) * H * 32], src, H, HQ, part * DH, DH, 32)
        loads += [(vw[:, :, :], W["L1_xattn_W_v"].rearrange("(c p) n -> p c n", p=P)),
                  (ow[:, :, :], W["L1_xattn_W_o"].rearrange("(c p) n -> p c n", p=P)),
                  (rms_w[:, :], W["L1_xattn_rms_scale"].rearrange("(a d) -> a d", a=1).broadcast_to([P, DH]))]
        for i, name in enumerate(("lambda_q1", "lambda_k1", "lambda_q2", "lambda_k2")):
            loads.append((lam_in[:, i, :, :].rearrange("p h d -> p (h d)"),
                          W["L1_xattn_" + name].rearrange("(a h) d -> a (h d)", a=1).broadcast_to([P, H * DH])))
        load_weights(nc, sc, ident, [qw[:, :, :], kw[:, :, :]] + [t[:, :, :] for t in kMs], loads, [])
        prod, dots = sc.sb("lambda_prod", [P, 2, H, DH]), sc.sb("lambda_dot", [P, 2, H])
        neglam = sc.sb("neg_lambda", [P, H])
        s_dots, s_elam, s_lam = sc.sem("dots"), sc.sem("elam"), sc.sem("lam")
        with nc.Block() as block:
            @block.scalar
            def _(act):
                act.wait_ge(s_dots, 1)
                nc.scalar.activation(dots[:, :, :], dots[:, :, :], ACT.Exp).then_inc(s_elam, 1)

            @block.vector
            def _(dve):
                link = Chain(dve, s_lam)
                for i in range(2):
                    ins = nc.vector.tensor_tensor(prod[:, i, :, :], lam_in[:, 2 * i, :, :], lam_in[:, 2 * i + 1, :, :], ALU.mult)
                drain(link(ins))
                nc.vector.tensor_reduce(dots[:, :, :], prod[:, :, :, :], AX.X, ALU.add).then_inc(s_dots, 1)
                dve.wait_ge(s_elam, 1)
                drain(link(nc.vector.tensor_tensor(neglam[:, :], dots[:, 1, :], dots[:, 0, :], ALU.subtract)))
                drain(link(nc.vector.tensor_scalar(neglam[:, :], neglam[:, :], -LAMBDA_INIT, None, ALU.add)))
                drain(link(nc.vector.tensor_scalar(rms_w[:, :], rms_w[:, :], 1.0 - LAMBDA_INIT, None, ALU.mult)))
        def stream(u):
            sc.part(u)
            x, cx, y = sc.sb("x", [P, NT, D]), sc.sb("ctx", [P, NT, D]), sc.sb("y", [P, NT, D])
            xT, cT, v = sc.sb("xT", [P, DC, S]), sc.sb("ctxT", [P, DC, S]), sc.sb("v", [P, NT, D])
            qT, kM = sc.sb("qT", [P, 2 * BLK, S]), kMs[u]
            MR = 3
            mask = sc.sb("mask", [P, MR, NT, S])
            E = sc.sb("E", [P, 2, 2, NT, S])
            wd, wT = sc.sb("w", [P, 2, NT, S]), sc.sb("wT", [P, 2, NT, S])
            top, sums = sc.sb("max", [P, H, 2, NT]), sc.sb("sums", [P, H, 2, NT])
            ratio = sc.sb("ratio", [P, H, NT])
            r1 = sc.sb("r1", [P, H, NT])
            o_sb, sq, oT = sc.sb("o", [P, NT, D]), sc.sb("sq", [P, NT, D]), sc.sb("oT", [P, DC, S])
            ms, rr, pw = sc.sb("ms", [P, NT, H]), sc.sb("rr", [P, NT, H]), sc.sb("pw", [P, NT, H])
            banks = sc.part(u)
            L = NormTiles(sc)
            (s_x, s_mask0, s_mask1, s_mask2, s_xT, s_xTs, s_pr, s_prs, s_kA, s_kV, s_sc, s_max, s_exp, s_w, s_tr, s_wT, s_av, s_ms, s_rr, s_pw, s_o, s_oT, s_oTs,
             s_y, s_dve, s_ln, s_st) = (sc.sem(n) for n in (
                 "x mask0 mask1 mask2 xT xTs pr prs kA kV sc max exp w tr wT av ms rr pw o oT oTs y dve ln st").split())
            s_mask = (s_mask0, s_mask1, s_mask2)
            steps = [(dst, w, src, i) for dst, w, src in ((qT, qw, xT), (kM, kw, cT)) for i in range(BLK)]

            def sync(sp, b):
                sp.dma_start(x[:, :, :], rows(x_in, b)).then_inc(s_x, 16)
                yield
                sp.dma_start(cx[:, :, :], rows(W["ctx_1024"], b)).then_inc(s_x, 16)
                yield
                for h in range(H):
                    if h >= MR:
                        sp.wait_ge(s_max, h - MR + 1)
                    sp.dma_start(mask[:, h % MR, :, :],
                                 W["mask_Bx16xSxS2_ff0"][b, h, :, :].rearrange("(t p) k -> p t k", p=P))\
                      .then_inc(s_mask[h % MR], 16)
                    yield
                sp.wait_ge(s_ln, 1)
                sp.dma_start(rows(x_out, b), y[:, :, :]).then_inc(s_st, 16)
                yield
                sp.wait_ge(s_st, 16)

            def gpsimd(pool, b):
                nc.gpsimd.memset(pw[:, :, :], -0.5).then_inc(s_pw, 1)
                yield
                pool.wait_ge(s_pw, 1)
                pool.wait_ge(s_ms, 1)
                nc.gpsimd.tensor_tensor(rr[:, :, :], ms[:, :, :], pw[:, :, :], ALU.pow).then_inc(s_rr, 1)
                yield
                yield from norm_powers(nc, pool, L, range(NT))

            def tensor(pe, b):
                pe.wait_ge(s_x, 32)
                for n, src in enumerate((x, cx)):
                    for c in range(DC):
                        for t in range(NT):
                            ins = nc.tensor.transpose(banks[n][:, c * S + t * P:c * S + (t + 1) * P],
                                                      src[:, t, c * P:(c + 1) * P], ident[:, :])
                    ins.then_inc(s_xT, 1)
                    yield
                pe.wait_ge(s_xTs, 2)
                for t in range(NT):
                    for c in range(DC):
                        ins = nc.tensor.matmul(banks[2][:, t * D:(t + 1) * D], cT[:, c, t * P:(t + 1) * P], vw[:, c, :],
                                               start=(c == 0), stop=(c == DC - 1))
                ins.then_inc(s_pr, 1)
                yield
                for n, (dst, w, src, i) in enumerate(steps):
                    if n >= 2:
                        pe.wait_ge(s_prs, min(n, 1 + BLK))
                    if n - 2 >= BLK:
                        pe.wait_ge(s_kA, 4 * (n - 1 - BLK))
                        pe.wait_ge(s_kV, 4 * (n - 1 - BLK))
                    for k in range(2):
                        blk = 2 * i + k
                        for c in range(DC):
                            ins = nc.tensor.matmul(banks[3 - 3 * (n % 2)][:, k * S:(k + 1) * S], w[:, c, blk * P:(blk + 1) * P],
                                                   src[:, c, :], start=(c == 0), stop=(c == DC - 1))
                    ins.then_inc(s_pr, 1)
                    yield
                pe.wait_ge(s_prs, 1 + BLK)
                pe.wait_ge(s_kA, 4 * BLK)
                pe.wait_ge(s_kV, 4 * BLK)
                for n in range(H + 2):
                    if n < H:
                        if n >= 1:
                            pe.wait_ge(s_max, n)
                        for j in range(2):
                            blk = j * BLK + n // 4
                            for t in range(NT):
                                ins = nc.tensor.matmul(banks[j][:, t * S:(t + 1) * S],
                                                       qT[:, blk, t * P:(t + 1) * P], kM[:, 4 * blk + n % 4, :],
                                                       start=True, stop=True)
                        ins.then_inc(s_sc, 1)
                        yield
                    if 1 <= n <= H:
                        m = n - 1
                        pe.wait_ge(s_w, m + 1)
                        if m >= 1:
                            pe.wait_ge(s_wT, m)
                        for jt in range(NT):
                            for t in range(NT):
                                ins = nc.tensor.transpose(banks[2][:, jt * S + t * P:jt * S + (t + 1) * P],
                                                          wd[:, m % 2, t, jt * P:(jt + 1) * P], ident[:, :])
                        ins.then_inc(s_tr, 1)
                        yield
                    if n >= 2:
                        m = n - 2
                        pe.wait_ge(s_wT, m + 1)
                        for t in range(NT):
                            for jt in range(NT):
                                ins = nc.tensor.matmul(banks[3][:, t * D + m * DH:t * D + (m + 1) * DH],
                                                       wT[:, m % 2, jt, t * P:(t + 1) * P], v[:, jt, m * DH:(m + 1) * DH],
                                                       start=(jt == 0), stop=(jt == NT - 1))
                        ins.then_inc(s_av, 1)
                        yield
                pe.wait_ge(s_o, 1)
                for c in range(DC):
                    for t in range(NT):
                        ins = nc.tensor.transpose(banks[0][:, c * S + t * P:c * S + (t + 1) * P],
                                                  o_sb[:, t, c * P:(c + 1) * P], ident[:, :])
                ins.then_inc(s_oT, 1)
                yield
                pe.wait_ge(s_oTs, 1)
                for t in range(NT):
                    for c in range(DC):
                        ins = nc.tensor.matmul(banks[1][:, t * D:(t + 1) * D], oT[:, c, t * P:(t + 1) * P],
                                               ow[:, c, :], start=(c == 0), stop=(c == DC - 1))
                ins.then_inc(s_y, 1)
                yield

            def scalar(act, b):
                for i in range(BLK):
                    act.wait_ge(s_pr, BLK + i + 2)
                    yield from place_keys(act, nc.scalar.copy, kM, banks[3 - 3 * ((BLK + i) % 2)], 2 * i, 0, s_kA)
                for n in range(H + 1):
                    if n < H:
                        act.wait_ge(s_max, n + 1)
                        for j in range(2):
                            for t in range(NT):
                                ins = nc.scalar.activation(E[:, n % 2, j, t, :], E[:, n % 2, j, t, :], ACT.Exp,
                                                           bias=top[:, n, j, t:t + 1], scale=1.0,
                                                           accum_out=sums[:, n, j, t:t + 1])
                        ins.then_inc(s_exp, 1)
                        yield
                    if n >= 1:
                        m = n - 1
                        act.wait_ge(s_tr, m + 1)
                        if m >= 2:
                            act.wait_ge(s_av, m - 1)
                        nc.scalar.copy(wT[:, m % 2, :, :], banks[2][:, :].rearrange("p (j k) -> p j k", j=NT))\
                            .then_inc(s_wT, 1)
                        yield

            def vector(dve, b):
                link = Chain(dve, s_dve)
                L.asked = 0
                for n, dst in enumerate((xT, cT)):
                    dve.wait_ge(s_xT, n + 1)
                    nc.vector.tensor_copy(dst[:, :, :], banks[n][:, :].rearrange("p (c s) -> p c s", c=DC)).then_inc(s_xTs, 1)
                    yield
                dve.wait_ge(s_pr, 1)
                nc.vector.tensor_copy(v[:, :, :], banks[2][:, :].rearrange("p (t n) -> p t n", t=NT)).then_inc(s_prs, 1)
                yield
                for n, (dst, w, src, i) in enumerate(steps):
                    dve.wait_ge(s_pr, n + 2)
                    bank = banks[3 - 3 * (n % 2)]
                    if dst is kM:
                        yield from place_keys(dve, nc.vector.tensor_copy, kM, bank, 2 * i, 2, s_kV)
                        continue
                    nc.vector.tensor_scalar(qT[:, 2 * i:2 * i + 2, :], bank[:, :].rearrange("p (k s) -> p k s", k=2), DH ** -0.5,
                                            None, ALU.mult).then_inc(s_prs, 1)
                    yield

                def combine(m):
                    dve.wait_ge(s_exp, m + 1)
                    yield from link(nc.vector.reciprocal(ratio[:, m, :], sums[:, m, 1, :]))
                    yield from link(nc.vector.scalar_tensor_tensor(ratio[:, m, :], ratio[:, m, :], neglam[:, m:m + 1],
                                                        sums[:, m, 0, :], ALU.mult, ALU.mult))
                    if m >= 2:
                        dve.wait_ge(s_tr, m - 1)
                    for t in range(NT):
                        ins = nc.vector.scalar_tensor_tensor(wd[:, m % 2, t, :], E[:, m % 2, 1, t, :], ratio[:, m, t:t + 1],
                                                             E[:, m % 2, 0, t, :], ALU.mult, ALU.add)
                    ins.then_inc(s_w, 1)
                    yield

                for n in range(H + 1):
                    if n < H:
                        dve.wait_ge(s_sc, n + 1)
                        dve.wait_ge(s_mask[n % MR], 16 * (n // MR + 1))
                        if n >= 2:
                            dve.wait_ge(s_w, n - 1)
                        for j in range(2):
                            for t in range(NT):
                                ins = nc.vector.tensor_tensor_reduce(
                                    out=E[:, n % 2, j, t, :], in0=banks[j][:, t * S:(t + 1) * S],
                                    in1=mask[:, n % MR, t, :], scale=1.0, scalar=-3.0e38, op0=ALU.add, op1=ALU.max,
                                    accum_out=top[:, n, j, t:t + 1])
                        yield from link(ins)
                        nc.vector.tensor_scalar(top[:, n, :, :], top[:, n, :, :], -1.0, None, ALU.mult).then_inc(s_max, 1)
                        yield
                    if n >= 1:
                        yield from combine(n - 1)
                yield from link(nc.vector.reciprocal(r1[:, :, :], sums[:, :, 0, :]))
                dve.wait_ge(s_av, H)
                v4 = lambda ap: ap.rearrange("p (h d) -> p h d", h=H)
                for t in range(NT):
                    yield from link(nc.vector.tensor_tensor(v4(o_sb[:, t, :]), v4(banks[3][:, t * D:(t + 1) * D]),
                                                 r1[:, :, t:t + 1].broadcast_to([P, H, DH]), ALU.mult))
                yield from link(nc.vector.tensor_tensor(sq[:, :, :], o_sb[:, :, :], o_sb[:, :, :], ALU.mult))
                for t in range(NT):
                    ins = nc.vector.tensor_reduce(ms[:, t, :], v4(sq[:, t, :]), AX.X, ALU.add)
                yield from link(ins)
                nc.vector.tensor_scalar(ms[:, :, :], ms[:, :, :], 1.0 / DH, EPS, ALU.mult, ALU.add).then_inc(s_ms, 1)
                yield
                for t in range(NT):
                    ins = nc.vector.tensor_tensor(v4(o_sb[:, t, :]), v4(o_sb[:, t, :]),
                                                  rms_w[:, :].unsqueeze(1).broadcast_to([P, H, DH]), ALU.mult)
                yield from link(ins)
                dve.wait_ge(s_rr, 1)
                for t in range(NT):
                    ins = nc.vector.tensor_tensor(v4(o_sb[:, t, :]), v4(o_sb[:, t, :]),
                                                  rr[:, t, :].unsqueeze(2).broadcast_to([P, H, DH]), ALU.mult)
                ins.then_inc(s_o, 1)
                yield
                dve.wait_ge(s_oT, 1)
                nc.vector.tensor_copy(oT[:, :, :], banks[0][:, :].rearrange("p (c s) -> p c s", c=DC)).then_inc(s_oTs, 1)
                yield
                dve.wait_ge(s_y, 1)
                for t in range(NT):
                    yield from link(nc.vector.tensor_tensor(x[:, t, :], x[:, t, :], banks[1][:, t * D:(t + 1) * D], ALU.add))
                    yield from layer_norm(nc, dve, link, x[:, t, :], y[:, t, :], L, t)
                nc.vector.engine_nop().then_inc(s_ln, 1)
                yield

            return dict(sync=sync, gpsimd=gpsimd, tensor=tensor, scalar=scalar, vector=vector)

        run_streams(nc, sc, [stream(u) for u in range(STREAMS)])


def ffn_1(nc, x_in, x_out, W):
    E, LAT, F = 8, D // 2, 2 * D
    KPH, HD, FC = LAT // H, D // H, F // P
    with stage(nc, "ff1") as sc:
        ident = sc.sb("ident", [P, P])
        make_identity(nc, sc, ident)
        qw, kw = sc.sb("qw", [P, DC, H * 32]), sc.sb("kw", [P, DC, H * 32])
        qb, kb = sc.sb("qb", [1, H * 32]), sc.sb("kb", [1, H * 32])
        vw, vb = sc.sb("vw", [P, DC, LAT]), sc.sb("vb", [1, LAT])
        ow, ob = sc.sb("ow", [P, D]), sc.sb("ob", [1, D])
        rw, rb = sc.sb("rw", [P, DC, E]), sc.sb("rb", [1, E])
        w1, w2 = sc.sb("w1", [P, E, DC, F]), sc.sb("w2", [P, E, FC, D])
        b1r, b1T, b2 = sc.sb("b1r", [E * FC, P]), sc.sb("b1T", [P, E * FC]), sc.sb("b2", [E, D])
        kMs = [sc.sb(f"kM{u}", [P, H, S]) for u in range(STREAMS)]
        loads = padded_heads(qw, W["L1_ffn_q_w"], H, HD, 0, KPH, 32) + padded_heads(kw, W["L1_ffn_k_w"], H, KPH, 0, KPH, 32)
        loads += [(qb[:, :].rearrange("p (h k) -> p h k", k=32)[:, :, 0:KPH], W["L1_ffn_q_b"].rearrange("(a h w) -> a h w", a=1, w=HD)[:, :, 0:KPH]),
                  (kb[:, :].rearrange("p (h k) -> p h k", k=32)[:, :, 0:KPH], W["L1_ffn_k_b"].rearrange("(a h w) -> a h w", a=1, w=KPH)),
                  (vw[:, :, :], W["L1_ffn_v_w"].rearrange("(c p) n -> p c n", p=P)),
                  (vb[:, :], W["L1_ffn_v_b"].rearrange("(a n) -> a n", a=1)),
                  (ow[:, :], W["L1_ffn_o_w"][0:LAT, :]), (ob[:, :], W["L1_ffn_o_b"].rearrange("(a n) -> a n", a=1)),
                  (rw[:, :, :], W["L1_ffn_router_w"].rearrange("(c p) n -> p c n", p=P)),
                  (rb[:, :], W["L1_ffn_router_b"].rearrange("(a n) -> a n", a=1)),
                  (b1r[:, :], W["L1_ffn_b1"].rearrange("e (c p) -> (e c) p", p=P)), (b2[:, :], W["L1_ffn_b2"])]
        for e in range(E):
            loads += [(w1[:, e, :, :], W["L1_ffn_w1"][e, :, :].rearrange("(c p) f -> p c f", p=P)),
                      (w2[:, e, :, :], W["L1_ffn_w2"][e, :, :].rearrange("(c p) d -> p c d", p=P))]
        load_weights(nc, sc, ident, [qw[:, :, :], kw[:, :, :], qb[:, :], kb[:, :]] + [t[:, :, :] for t in kMs], loads, [(b1r[:, :], b1T[:, :])])
        iota, ones = sc.sb("iota", [P, E]), sc.sb("ones", [1, S])
        s_iota = sc.sem("iota")
        with nc.Block() as block:
            @block.gpsimd
            def _(pool):
                for e in range(E):
                    nc.gpsimd.memset(iota[:, e:e + 1], float(e)).then_inc(s_iota, 1)
                nc.gpsimd.memset(ones[:, :], 1.0).then_inc(s_iota, 1)
                pool.wait_ge(s_iota, E + 1)
        def stream(u):
            sc.part(u)
            x, y, xT = sc.sb("x", [P, NT, D]), sc.sb("y", [P, NT, D]), sc.sb("xT", [P, DC, S])
            v = sc.sb("v", [P, NT, LAT])
            o_sb, oT, rs = sc.sb("o", [P, NT, LAT]), sc.sb("oT", [P, S]), sc.sb("rsums", [P, H, NT])
            mT = sc.sb("mlaT", [P, DC, S])
            pr, mx = sc.sb("probs", [P, NT, E]), sc.sb("top", [P, NT, 8])
            negl, suml = sc.sb("neg_logit", [P, NT]), sc.sb("sum_logit", [P, NT])
            ix, ixf = sc.sb("index", [P, NT, 8], U32), sc.sb("indexf", [P, NT, 2])
            oh, den = sc.sb("onehot", [P, NT, 2, E]), sc.sb("den", [P, NT])
            comb, cT = sc.sb("combine", [P, NT, E]), sc.sb("combineT", [E, S])
            h1, acc = sc.sb("h1", [P, 2, FC, S]), sc.sb("acc", [P, NT, D])
            banks = sc.part(u)
            A = AttentionTiles(sc, ident, H, KPH, KPH, banks[0], banks[1], banks[2], kMs[u])
            A.V = lambda jt, h: v[:, jt, h * KPH:(h + 1) * KPH]
            L = NormTiles(sc)
            (s_x, s_xT, s_xTs, s_qk, s_qkT, s_kA, s_kV, s_v, s_vs, s_o, s_oT, s_oTs, s_m, s_mT, s_lg, s_neg, s_pexp, s_comb, s_cT, s_cTs, s_b2,
             s_h1, s_g, s_h2, s_acc, s_dve, s_ln, s_st) = (sc.sem(n) for n in (
                 "x xT xTs qk qkT kA kV v vs o oT oTs m mT lg neg pexp comb cT cTs b2 h1 g h2 acc dve ln st").split())

            def sync(sp, b):
                sp.dma_start(x[:, :, :], rows(x_in, b)).then_inc(s_x, 16)
                yield
                sp.wait_ge(s_ln, 1)
                sp.dma_start(rows(x_out, b), y[:, :, :]).then_inc(s_st, 16)
                yield
                sp.wait_ge(s_st, 16)

            def gpsimd(pool, b):
                yield from norm_powers(nc, pool, L, range(NT))

            def tensor(pe, b):
                pe.wait_ge(s_x, 16)
                for c in range(DC):
                    for t in range(NT):
                        ins = nc.tensor.transpose(banks[0][:, c * S + t * P:c * S + (t + 1) * P],
                                                  x[:, t, c * P:(c + 1) * P], ident[:, :])
                ins.then_inc(s_xT, 1)
                yield
                pe.wait_ge(s_xTs, 1)
                for t in range(NT):
                    o = banks[1][:, t * LAT:(t + 1) * LAT]
                    for c in range(DC):
                        nc.tensor.matmul(o, xT[:, c, t * P:(t + 1) * P], vw[:, c, :], start=(c == 0), stop=False)
                    ins = nc.tensor.matmul(o, ones[0:1, 0:P], vb[0:1, :], start=False, stop=True)
                ins.then_inc(s_v, 1)
                yield
                n = 0
                for w, bias in ((qw, qb), (kw, kb)):
                    for half in range(2):
                        if n == 2:
                            pe.wait_ge(s_qkT, 1)
                        if n == 3:
                            pe.wait_ge(s_qkT, 2)
                        for k in range(2):
                            blk = 2 * half + k
                            o = banks[2 + n % 2][:, k * S:(k + 1) * S]
                            for c in range(DC):
                                nc.tensor.matmul(o, w[:, c, blk * P:(blk + 1) * P], xT[:, c, :], start=(c == 0), stop=False)
                            ins = nc.tensor.matmul(o, bias[0:1, blk * P:(blk + 1) * P], ones[0:1, :], start=False, stop=True)
                        ins.then_inc(s_qk, 1)
                        yield
                        n += 1
                pe.wait_ge(s_qkT, 2)
                pe.wait_ge(s_kA, 8)
                pe.wait_ge(s_kV, 8)
                pe.wait_ge(s_vs, 1)
                yield from attend(nc, A, pe=pe)
                pe.wait_ge(s_o, 1)
                for t in range(NT):
                    ins = nc.tensor.transpose(banks[3][:, t * P:(t + 1) * P], o_sb[:, t, :], ident[:, :])
                ins.then_inc(s_oT, 1)
                yield
                pe.wait_ge(s_oTs, 1)
                for c in range(DC):
                    o = banks[0][:, c * S:(c + 1) * S]
                    nc.tensor.matmul(o, ow[:, c * P:(c + 1) * P], oT[:, :], start=True, stop=False)
                    ins = nc.tensor.matmul(o, ob[0:1, c * P:(c + 1) * P], ones[0:1, :], start=False, stop=True)
                ins.then_inc(s_m, 1)
                yield
                pe.wait_ge(s_mT, 1)
                for t in range(NT):
                    o = banks[1][:, t * E:(t + 1) * E]
                    for c in range(DC):
                        nc.tensor.matmul(o, mT[:, c, t * P:(t + 1) * P], rw[:, c, :], start=(c == 0), stop=False)
                    ins = nc.tensor.matmul(o, ones[0:1, 0:P], rb[0:1, :], start=False, stop=True)
                ins.then_inc(s_lg, 1)
                yield
                for e in range(E + 1):
                    if e < E:
                        for half in range(2):
                            n = 2 * e + half
                            if n == 1:
                                pe.wait_ge(s_pexp, 1)
                            if n >= 2:
                                pe.wait_ge(s_g, 2 * (n - 1))
                            for k in range(2):
                                f = 2 * half + k
                                for c in range(DC):
                                    ins = nc.tensor.matmul(banks[n % 2][:, k * S:(k + 1) * S], w1[:, e, c, f * P:(f + 1) * P],
                                                           mT[:, c, :], start=(c == 0), stop=(c == DC - 1))
                            ins.then_inc(s_h1, 1)
                            yield
                    if e == 2:
                        pe.wait_ge(s_comb, 1)
                        for t in range(NT):
                            ins = nc.tensor.transpose(banks[3][0:E, t * P:(t + 1) * P], comb[:, t, :], ident[:, :])
                        ins.then_inc(s_cT, 1)
                        yield
                        pe.wait_ge(s_cTs, 1)
                        for t in range(NT):
                            ins = nc.tensor.matmul(banks[3][:, t * D:(t + 1) * D], cT[:, t * P:(t + 1) * P], b2[:, :],
                                                   start=True, stop=True)
                        ins.then_inc(s_b2, 1)
                        yield
                    if e >= 1:
                        m = e - 1
                        pe.wait_ge(s_g, 4 * (m + 1))
                        if m >= 1:
                            pe.wait_ge(s_acc, m)
                        for t in range(NT):
                            for f in range(FC):
                                ins = nc.tensor.matmul(banks[2][:, t * D:(t + 1) * D], h1[:, m % 2, f, t * P:(t + 1) * P],
                                                       w2[:, m, f, :], start=(f == 0), stop=(f == FC - 1))
                        ins.then_inc(s_h2, 1)
                        yield

            def scalar(act, b):
                for n in range(2):
                    act.wait_ge(s_qk, 3 + n)
                    yield from place_keys(act, nc.scalar.copy, A.kM, banks[2 + n], 2 * n, 0, s_kA)
                yield from attend(nc, A, act=act)
                act.wait_ge(s_neg, 1)
                for t in range(NT):
                    ins = nc.scalar.activation(pr[:, t, :], banks[1][:, t * E:(t + 1) * E], ACT.Exp, bias=negl[:, t:t + 1],
                                               scale=1.0, accum_out=suml[:, t:t + 1])
                ins.then_inc(s_pexp, 1)
                yield
                for e in range(E):
                    if e >= 2:
                        act.wait_ge(s_h2, e - 1)
                    for f in range(FC):
                        act.wait_ge(s_h1, 2 * e + f // 2 + 1)
                        nc.scalar.activation(h1[:, e % 2, f, :], banks[(2 * e + f // 2) % 2][:, (f % 2) * S:(f % 2 + 1) * S],
                                             ACT.Gelu, bias=b1T[:, e * FC + f:e * FC + f + 1], scale=1.0).then_inc(s_g, 1)
                        yield

            def vector(dve, b):
                link = Chain(dve, s_dve)
                L.asked = 0
                dve.wait_ge(s_xT, 1)
                nc.vector.tensor_copy(xT[:, :, :], banks[0][:, :].rearrange("p (c s) -> p c s", c=DC)).then_inc(s_xTs, 1)
                yield
                dve.wait_ge(s_v, 1)
                nc.vector.tensor_copy(v[:, :, :], banks[1][:, 0:NT * LAT].rearrange("p (t n) -> p t n", t=NT)).then_inc(s_vs, 1)
                yield
                for n in range(4):
                    dve.wait_ge(s_qk, n + 1)
                    if n >= 2:
                        yield from place_keys(dve, nc.vector.tensor_copy, A.kM, banks[2 + n % 2], 2 * (n % 2), 2, s_kV)
                        continue
                    dst = A.qT[:, 2 * n:2 * n + 2, :]
                    src = banks[2 + n % 2][:, :].rearrange("p (k s) -> p k s", k=2)
                    nc.vector.tensor_scalar(dst, src, KPH ** -0.5, None, ALU.mult).then_inc(s_qkT, 1)
                    yield
                yield from attend(nc, A, dve=dve)
                dve.wait_ge(A.s_exp, H)
                yield from link(nc.vector.reciprocal(rs[:, :, :], A.sums[:, :, :]))
                dve.wait_ge(A.s_av, H)
                for t in range(NT):
                    ins = nc.vector.tensor_tensor(o_sb[:, t, :].rearrange("p (h d) -> p h d", h=H),
                                                  banks[2][:, t * LAT:(t + 1) * LAT].rearrange("p (h d) -> p h d", h=H),
                                                  rs[:, :, t:t + 1].broadcast_to([P, H, KPH]), ALU.mult)
                ins.then_inc(s_o, 1)
                yield
                dve.wait_ge(s_oT, 1)
                nc.vector.tensor_copy(oT[:, :], banks[3][:, 0:S]).then_inc(s_oTs, 1)
                yield
                dve.wait_ge(s_m, 1)
                nc.vector.tensor_copy(mT[:, :, :], banks[0][:, :].rearrange("p (c s) -> p c s", c=DC)).then_inc(s_mT, 1)
                yield
                dve.wait_ge(s_lg, 1)
                nc.vector.tensor_reduce(negl[:, :], banks[1][:, 0:NT * E].rearrange("p (t e) -> p t e", t=NT),
                                        AX.X, ALU.max, negate=True).then_inc(s_neg, 1)
                yield
                dve.wait_ge(s_pexp, 1)
                yield from link(nc.vector.reciprocal(suml[:, :], suml[:, :]))
                for t in range(NT):
                    yield from link(nc.vector.tensor_scalar(pr[:, t, :], pr[:, t, :], suml[:, t:t + 1], None, ALU.mult))
                    yield from top2(nc, dve, link, pr, mx, ix, ixf, iota, oh, t, 1.0)
                    yield from link(nc.vector.tensor_scalar(den[:, t:t + 1], mx[:, t, 0:1], mx[:, t, 1:2], 1e-8, ALU.add, ALU.add))
                    yield from link(nc.vector.reciprocal(den[:, t:t + 1], den[:, t:t + 1]))
                    for k in range(2):
                        ins = nc.vector.tensor_scalar(oh[:, t, k, :], oh[:, t, k, :], mx[:, t, k:k + 1], den[:, t:t + 1],
                                                      ALU.mult, ALU.mult)
                    yield from link(ins)
                nc.vector.tensor_tensor(comb[:, :, :], oh[:, :, 0, :], oh[:, :, 1, :], ALU.add).then_inc(s_comb, 1)
                yield
                dve.wait_ge(s_comb, 1)
                dve.wait_ge(s_cT, 1)
                nc.vector.tensor_copy(cT[:, :], banks[3][0:E, 0:S]).then_inc(s_cTs, 1)
                yield
                dve.wait_ge(s_b2, 1)
                yield from link(nc.vector.tensor_copy(acc[:, :, :], banks[3][:, :].rearrange("p (t d) -> p t d", t=NT)))
                for e in range(E):
                    dve.wait_ge(s_h2, e + 1)
                    for t in range(NT):
                        ins = nc.vector.scalar_tensor_tensor(acc[:, t, :], banks[2][:, t * D:(t + 1) * D],
                                                             comb[:, t, e:e + 1], acc[:, t, :], ALU.mult, ALU.add)
                    ins.then_inc(s_acc, 1)
                    yield
                    dve.wait_ge(s_acc, e + 1)
                for t in range(NT):
                    yield from link(nc.vector.tensor_tensor(x[:, t, :], x[:, t, :], x[:, t, :], ALU.add))
                    yield from link(nc.vector.scalar_tensor_tensor(x[:, t, :], acc[:, t, :], 0.3, x[:, t, :], ALU.mult, ALU.add))
                    yield from layer_norm(nc, dve, link, x[:, t, :], y[:, t, :], L, t)
                nc.vector.engine_nop().then_inc(s_ln, 1)
                yield

            return dict(sync=sync, gpsimd=gpsimd, tensor=tensor, scalar=scalar, vector=vector)

        run_streams(nc, sc, [stream(u) for u in range(STREAMS)])


def decoder(nc, args, out):
    x1 = nc.dram_tensor("act1", (NB, S, D), F32, kind="Internal").ap()
    self_attention_0(nc, args["x"], x1, args)
    x2 = nc.dram_tensor("act2", (NB, S, D), F32, kind="Internal").ap()
    cross_attention(nc, x1, x2, args["ctx_1024"], args["L0_xattn_Wo"])
    x3 = nc.dram_tensor("act3", (NB, S, D), F32, kind="Internal").ap()
    ffn_0(nc, x2, x3, args)
    x4 = nc.dram_tensor("act4", (NB, S, D), F32, kind="Internal").ap()
    self_attention_1(nc, x3, x4, args)
    x5 = nc.dram_tensor("act5", (NB, S, D), F32, kind="Internal").ap()
    cross_attention_1(nc, x4, x5, args)
    ffn_1(nc, x5, out, args)


def constants():
    return {**memory_constants(), **shape_constants()}


_INS = ['x',
        'ctx_1024',
        'mask_Bx16xSxS2_ff0',
        'L0_attn_Wq',
        'L0_attn_bq',
        'L0_attn_gq',
        'L0_attn_bq_ln',
        'L0_attn_keys',
        'L0_attn_values',
        'L0_attn_Wres',
        'L0_attn_bres',
        'L0_attn_Wmem',
        'L0_attn_bmem',
        'L0_attn_Wo',
        'L0_attn_g_out',
        'L0_attn_b_out',
        'L0_xattn_Wo',
        'L0_ffn_gate_w',
        'L0_ffn_w_gate',
        'L0_ffn_w_up',
        'L0_ffn_w_down',
        'L0_ffn_A1',
        'L0_ffn_B1',
        'L0_ffn_A3',
        'L0_ffn_B3',
        'L0_ffn_A2',
        'L0_ffn_B2',
        'L1_attn_w_qkv',
        'L1_attn_w_proj',
        'L1_attn_b_proj',
        'L1_attn_rpe_q_table',
        'L1_attn_rpe_k_table',
        'L1_attn_rpe_v_table',
        'L1_xattn_W_q',
        'L1_xattn_W_k',
        'L1_xattn_W_v',
        'L1_xattn_W_o',
        'L1_xattn_lambda_q1',
        'L1_xattn_lambda_k1',
        'L1_xattn_lambda_q2',
        'L1_xattn_lambda_k2',
        'L1_xattn_rms_scale',
        'L1_ffn_q_w',
        'L1_ffn_q_b',
        'L1_ffn_k_w',
        'L1_ffn_k_b',
        'L1_ffn_v_w',
        'L1_ffn_v_b',
        'L1_ffn_o_w',
        'L1_ffn_o_b',
        'L1_ffn_router_w',
        'L1_ffn_router_b',
        'L1_ffn_w1',
        'L1_ffn_b1',
        'L1_ffn_w2',
        'L1_ffn_b2']


def kernel(**inputs):
    import numpy as _np
    import concourse.bacc as _bacc
    from concourse import mybir as _mybir
    from concourse.bass_utils import run_bass_kernel_spmd as _run

    nc = _bacc.Bacc("TRN2", target_bir_lowering=False, num_devices=1)
    arrays, args = {}, {}
    for name in _INS:
        a = _np.ascontiguousarray(inputs[name])
        arrays[f"in_{name}_dram"] = a
        args[name] = nc.dram_tensor(f"in_{name}_dram", a.shape, _mybir.dt.from_np(a.dtype), kind="ExternalInput").ap()
    for name, a in constants().items():
        arrays[f"const_{name}_dram"] = a
        args[f"const_{name}"] = nc.dram_tensor(f"const_{name}_dram", a.shape, _mybir.dt.float32, kind="ExternalInput").ap()
    out = nc.dram_tensor("out_dram", (16, 256, 256), _mybir.dt.float32, kind="ExternalOutput").ap()
    decoder(nc, args, out)
    r = _run(nc, [arrays], core_ids=[0])
    return r.results[0]["out_dram"]
```
